# Optimizing a Trainium2 kernel written in Bass

```python
import numpy as np
import jax
import jax.numpy as jnp

def _softmax(x, axis=-1):
    return jax.nn.softmax(x, axis=axis)

def _gelu(x):
    return jax.nn.gelu(x, approximate=True)

def _silu(x):
    return jax.nn.silu(x)

def _sigmoid(x):
    return jax.nn.sigmoid(x)

def _layernorm(x, axis=-1, eps=1e-05):
    m = jnp.mean(x, axis=axis, keepdims=True)
    v = jnp.var(x, axis=axis, keepdims=True)
    return (x - m) / jnp.sqrt(v + eps)

def _scatter_add(tgt, idx, src, axis=0):
    return tgt.at[idx].add(src)

def _segment_sum(src, seg, n):
    return jax.ops.segment_sum(src, seg, n)
kernel_name = 'mk_adaln_d1_jaxref_r8_339c1e'

def setup_inputs(seed: int=0):
    np.random.seed(seed)
    _w = jnp.asarray

    def _L0_attn_setup():
        import jax, jax.numpy as jnp
        import numpy as np
        B, N, D, H = (4, 512, 128, 16)
        HD = D // H
        EPS_NORM = 1e-12
        EPS_LN = 1e-05

        def _silu(x):
            return x * jax.nn.sigmoid(x)

        def _simple_gla(q, k, v, f):
            qT = jnp.moveaxis(q, 1, 0)
            kT = jnp.moveaxis(k, 1, 0)
            vT = jnp.moveaxis(v, 1, 0)
            fT = jnp.moveaxis(f, 1, 0)

            def step(S, inp):
                qt, kt, vt, ft = inp
                S = jnp.exp(ft)[..., None, None] * S + kt[..., :, None] * vt[..., None, :]
                o = jnp.einsum('bhk,bhkv->bhv', qt, S)
                return (S, o)
            S0 = jnp.zeros((q.shape[0], q.shape[2], q.shape[3], v.shape[3]), q.dtype)
            _, o = jax.lax.scan(step, S0, (qT, kT, vT, fT))
            return jnp.moveaxis(o, 0, 1)
        key = jax.random.key(seed)
        ks = jax.random.split(key, 9)
        s = 0.02
        return {'x': jax.random.normal(ks[0], (B, N, D), jnp.float32), 'Wq': jax.random.normal(ks[1], (D, D), jnp.float32) * s, 'Wk': jax.random.normal(ks[2], (D, D), jnp.float32) * s, 'Wv': jax.random.normal(ks[3], (D, D), jnp.float32) * s, 'Wf': jax.random.normal(ks[4], (H, D), jnp.float32) * s, 'Wg1': jax.random.normal(ks[5], (HD, D), jnp.float32) * s, 'Wg2': jax.random.normal(ks[6], (D, HD), jnp.float32) * s, 'ln_w': jnp.ones((D,), jnp.float32), 'Wo': jax.random.normal(ks[7], (D, D), jnp.float32) * s}
    _L0_attn_in = _L0_attn_setup()

    def _L0_ffn_setup():
        import jax, jax.numpy as jnp
        import numpy as np
        B, S, D = (2, 256, 128)
        E, K, DFF = (8, 2, 4 * 128)
        EPS_GATE = 1e-08
        EPS_LN = 1e-05
        key = jax.random.key(seed)
        ks = jax.random.split(key, 4)
        scaled = lambda k, shape, fan: jax.random.normal(k, shape, jnp.float32) / np.sqrt(fan).astype(np.float32)
        return {'x': jax.random.normal(ks[0], (B, S, D), jnp.float32), 'Wg': scaled(ks[1], (D, E), D), 'bg': jnp.zeros((E,), jnp.float32), 'W1': scaled(ks[2], (E, D, DFF), D), 'b1': jnp.zeros((E, DFF), jnp.float32), 'W2': scaled(ks[3], (E, DFF, D), DFF), 'b2': jnp.zeros((E, D), jnp.float32), 'gamma': jnp.ones((D,), jnp.float32), 'beta': jnp.zeros((D,), jnp.float32)}
    _L0_ffn_in = _L0_ffn_setup()
    _L0_c = _w((lambda *s: np.random.randn(*s).astype(np.float32) * 0.05)(4, 128))
    _L0_wmod = _w((lambda *s: np.random.randn(*s).astype(np.float32) * 0.05)(128, 6 * 128) * 128 ** (-0.5))
    _d = {'L0_attn_x': _L0_attn_in['x'], 'L0_attn_Wq': _L0_attn_in['Wq'], 'L0_attn_Wk': _L0_attn_in['Wk'], 'L0_attn_Wv': _L0_attn_in['Wv'], 'L0_attn_Wf': _L0_attn_in['Wf'], 'L0_attn_Wg1': _L0_attn_in['Wg1'], 'L0_attn_Wg2': _L0_attn_in['Wg2'], 'L0_attn_ln_w': _L0_attn_in['ln_w'], 'L0_attn_Wo': _L0_attn_in['Wo'], 'L0_ffn_Wg': _L0_ffn_in['Wg'], 'L0_ffn_bg': _L0_ffn_in['bg'], 'L0_ffn_W1': _L0_ffn_in['W1'], 'L0_ffn_b1': _L0_ffn_in['b1'], 'L0_ffn_W2': _L0_ffn_in['W2'], 'L0_ffn_b2': _L0_ffn_in['b2'], 'L0_ffn_gamma': _L0_ffn_in['gamma'], 'L0_ffn_beta': _L0_ffn_in['beta'], 'L0_c': _L0_c, 'L0_wmod': _L0_wmod}
    _x0 = _d['L0_attn_x']
    _d['L0_attn_x'] = jax.random.normal(jax.random.fold_in(jax.random.key(seed), 1), (4, 1024, 128), dtype=_x0.dtype)
    del _x0
    return _d

def reference(L0_attn_x, L0_attn_Wq, L0_attn_Wk, L0_attn_Wv, L0_attn_Wf, L0_attn_Wg1, L0_attn_Wg2, L0_attn_ln_w, L0_attn_Wo, L0_ffn_Wg, L0_ffn_bg, L0_ffn_W1, L0_ffn_b1, L0_ffn_W2, L0_ffn_b2, L0_ffn_gamma, L0_ffn_beta, L0_c, L0_wmod):

    def _L0_attn_ref(x, Wq, Wk, Wv, Wf, Wg1, Wg2, ln_w, Wo):
        import jax, jax.numpy as jnp
        import numpy as np
        B, N, D, H = (4, 512, 128, 16)
        HD = D // H
        EPS_NORM = 1e-12
        EPS_LN = 1e-05

        def _silu(x):
            return x * jax.nn.sigmoid(x)

        def _simple_gla(q, k, v, f):
            qT = jnp.moveaxis(q, 1, 0)
            kT = jnp.moveaxis(k, 1, 0)
            vT = jnp.moveaxis(v, 1, 0)
            fT = jnp.moveaxis(f, 1, 0)

            def step(S, inp):
                qt, kt, vt, ft = inp
                S = jnp.exp(ft)[..., None, None] * S + kt[..., :, None] * vt[..., None, :]
                o = jnp.einsum('bhk,bhkv->bhv', qt, S)
                return (S, o)
            S0 = jnp.zeros((q.shape[0], q.shape[2], q.shape[3], v.shape[3]), q.dtype)
            _, o = jax.lax.scan(step, S0, (qT, kT, vT, fT))
            return jnp.moveaxis(o, 0, 1)
        b, n, d = x.shape
        q = _silu(x @ Wq.T).reshape(b, n, H, HD)
        k = _silu(x @ Wk.T).reshape(b, n, H, HD)
        v = _silu(x @ Wv.T).reshape(b, n, H, HD)
        f = jax.nn.log_sigmoid(x @ Wf.T)
        k = k / jnp.maximum(jnp.linalg.norm(k, axis=-1, keepdims=True), EPS_NORM)
        o = _simple_gla(q, k, v, f).reshape(b, n, d)
        gate = jax.nn.sigmoid(x @ Wg1.T @ Wg2.T)
        o = o * gate
        mu = jnp.mean(o, axis=-1, keepdims=True)
        xc = o - mu
        var = jnp.mean(xc * xc, axis=-1, keepdims=True)
        o = xc / jnp.sqrt(var + EPS_LN) * ln_w
        return o @ Wo.T

    def _L0_ffn_ref(x, Wg, bg, W1, b1, W2, b2, gamma, beta):
        import jax, jax.numpy as jnp
        import numpy as np
        B, S, D = (2, 256, 128)
        E, K, DFF = (8, 2, 4 * 128)
        EPS_GATE = 1e-08
        EPS_LN = 1e-05
        b, s, d = x.shape
        xf = x.reshape(-1, d)
        T = xf.shape[0]
        num_experts = Wg.shape[1]
        logits = xf @ Wg + bg
        w = jax.nn.softmax(logits, axis=-1)
        top_w, top_idx = jax.lax.top_k(w, K)
        top_w = top_w / (top_w.sum(axis=-1, keepdims=True) + EPS_GATE)
        cw = jnp.zeros((T, num_experts), xf.dtype).at[jnp.arange(T)[:, None], top_idx].add(top_w)
        out = jnp.zeros_like(xf)
        for e in range(num_experts):
            h = jax.nn.gelu(xf @ W1[e] + b1[e], approximate=False)
            y = h @ W2[e] + b2[e]
            out = out + cw[:, e:e + 1] * y
        mu = out.mean(axis=-1, keepdims=True)
        var = out.var(axis=-1, keepdims=True)
        out = (out - mu) / jnp.sqrt(var + EPS_LN) * gamma + beta
        return out.reshape(b, s, d)
    x = L0_attn_x
    mod = (_silu(L0_c) @ L0_wmod).reshape(L0_c.shape[0], 6, 1, -1)
    sa, ca, ga, sb, cb, gb = (mod[:, 0], mod[:, 1], mod[:, 2], mod[:, 3], mod[:, 4], mod[:, 5])
    ga = (2 * (ga >= 0) - 1) * jnp.maximum(jnp.abs(ga), 0.25)
    gb = (2 * (gb >= 0) - 1) * jnp.maximum(jnp.abs(gb), 0.25)
    h = _layernorm(x, axis=-1) * (1 + ca) + sa
    x = x + ga * _L0_attn_ref(h, L0_attn_Wq, L0_attn_Wk, L0_attn_Wv, L0_attn_Wf, L0_attn_Wg1, L0_attn_Wg2, L0_attn_ln_w, L0_attn_Wo)
    h = _layernorm(x, axis=-1) * (1 + cb) + sb
    x = x + gb * _L0_ffn_ref(h, L0_ffn_Wg, L0_ffn_bg, L0_ffn_W1, L0_ffn_b1, L0_ffn_W2, L0_ffn_b2, L0_ffn_gamma, L0_ffn_beta)
    return x

_drawn_inputs = setup_inputs


def setup_inputs(seed=0):
    import zlib

    import numpy as np

    out = dict(_drawn_inputs(seed))
    spreads = {'L0_attn_ln_w': (1.0, 0.6),
     'L0_ffn_bg': (0.0, 0.1),
     'L0_ffn_b1': (0.0, 0.313),
     'L0_ffn_b2': (0.0, 0.1),
     'L0_ffn_gamma': (1.0, 0.2),
     'L0_ffn_beta': (0.0, 0.312)}
    factors = {'L0_attn_Wf': 6.002, 'L0_attn_Wg1': 8.0, 'L0_attn_Wg2': 8.0}
    for name, (base, spread) in spreads.items():
        noise = np.random.default_rng([zlib.crc32(name.encode()), seed]).standard_normal(out[name].shape)
        drawn = base * np.exp(spread * noise) if base else spread * noise
        out[name] = jnp.asarray(drawn.astype(out[name].dtype))
    for name, factor in factors.items():
        out[name] = (out[name] * factor).astype(out[name].dtype)
    return out
```

```python
from contextlib import ExitStack

import concourse.bass as bass
from concourse import mybir

F32 = mybir.dt.float32
BF16 = mybir.dt.bfloat16
I32 = mybir.dt.int32
ALU = mybir.AluOpType
ACT = mybir.ActivationFunctionType
AX = mybir.AxisListType.X

P = 128
B, N, D = 4, 1024, 128
H, HD = 16, 8
E, F = 8, 512
NT = N // P
U = NT * B
W = B * P
C = 32
NC = P // C
G = 4
HG = H // G
FC = F // P
TOK = 3 * P + H
NB = 2 * B * N // P + E
EPS_LN, EPS_GATE, EPS_NORM = 1e-5, 1e-8, 1e-12
PAD = 1 << 20
ROWS = B * N

CONST_WIDTHS = [("ident", P), ("later", P), ("upto", P), ("before", P), ("ones", P), ("headsel", P),
                ("slot_iota", P), ("block_iota", NB), ("causal", C), ("blockmask", C), ("start_iota", 32),
                ("dest_hi", 2 * U), ("chunk_of", NC), ("head_of", HG), ("rank8", E), ("dest_lo", 1)]
CONST_AT, _at = {}, 0
for _name, _w in CONST_WIDTHS:
    CONST_AT[_name] = (_at, _w)
    _at += _w
CONST_N = _at


def wait(eng, sem, value):
    if not (isinstance(value, int) and value <= 0):
        eng.wait_ge(sem, value)


def build(nc, x, wq_t, wk_t, wkv_t, wf_t, wg1, wg2_t, lnw, wo_t, wg, bg, w1, b1_t, w2, b2, gamma, beta, c_t, wmod,
          consts, out):
    ctx = ExitStack()
    with ctx:
        def sb(name, shape, dt=F32):
            return ctx.enter_context(nc.sbuf_tensor(name, shape, dt))

        def psum(name, shape, dt=F32):
            return ctx.enter_context(nc.psum_tensor(name, shape, dt))

        def sem(name):
            return ctx.enter_context(nc.semaphore(name))

        h2_rows = nc.dram_tensor("h2_rows", (ROWS, D), F32, kind="Internal").ap()
        y_rows = nc.dram_tensor("y_rows", (2 * ROWS, D), F32, kind="Internal").ap()

        xs = sb("xs", [P, NT, W])
        ct = sb("ct", [P, CONST_N])
        qT = sb("qT", [P, NT, W])
        kT = sb("kT", [P, NT, W])
        kv = sb("kv", [P, NT, B, 2 * P])
        gz = sb("gz", [P, NT, B, P + H])
        wqs = sb("wqs", [P, P])
        wks = sb("wks", [P, P])
        wtok = sb("wtok", [P, TOK])
        wos = sb("wos", [P, P])
        wog = sb("wog", [P, B, P])
        lnws = sb("lnws", [P, 1])
        wgs = sb("wgs", [P, E])
        bgs = sb("bgs", [P, E])
        wg1s = sb("wg1s", [HD, D])
        wg2s = sb("wg2s", [HD, D])
        cs = sb("cs", [P, B])
        csil = sb("csil", [P, B])
        modT = sb("modT", [P, 2, B])
        mod = sb("mod", [P, 4, B, P])
        gam = sb("gam", [P, 2, P])
        epst = sb("epst", [P, 2])
        onebf = sb("onebf", [P, C], BF16)

        st = sb("st", [P, U, 6])
        ln = sb("ln", [P, 8, U])
        mean = sb("mean", [P, U])
        rstd = sb("rstd", [P, U])
        zf = sb("zf", [P, U * H])
        rk = sb("rk", [P, U * H])
        eg = sb("eg", [P, U * H])
        ef = sb("ef", [P, U * H])
        tc = sb("tc", [H, U * NC])
        td = sb("td", [P, U * NC])

        WORK = 38 * W
        work = sb("work", [P, WORK])

        def ws(at, n):
            return work[:, at:at + n]

        xn = [ws(m * W, W) for m in range(2)]
        hT = [ws((2 + m) * W, W) for m in range(2)]
        ksq = [ws((4 + m) * W, W) for m in range(2)]

        wmods = ws(8 * W, 6 * D)
        cbc = ws(10 * W, B * P).rearrange("p (b w) -> p b w", b=B)

        cur = [0]

        def take(n):
            cur[0] += n
            return ws(cur[0] - n, n)

        Qx = take(HG * W)
        kTs, qTs, kd = ([take(W), take(W)] for _ in range(3))
        vx = [take(B * W), take(B * W)]
        vp = take(W)
        R, EM, PR = ([take(W), take(W)] for _ in range(3))
        Um = take(W)
        Sb = [take(W), take(W)]
        stmp = take(B * C)
        om, osum, ot = (take(W) for _ in range(3))
        o1, o2, onT, xn2, h2 = (take(W) for _ in range(5))
        o3, on, h2t, h2T = o2, o2, xn2, onT
        za = o1
        lg = ws(WORK - U * E, U * E)
        stb = [take(B * 6) for _ in range(2)]
        lnb = [take(8 * B) for _ in range(2)]
        assert cur[0] <= WORK - U * E, cur[0]

        UE = U * E
        base = 0

        def at(n):
            nonlocal base
            base += n
            return ws(base - n, n)

        lgx, wt, key, oh1, oh2, wt2, M, rank, pre, pos, t1r, t2r, ones_r = (at(UE) for _ in range(13))
        mx, zs, m1, m2, k1, tw1, tw2, tws, p1, p2 = (at(U) for _ in range(10))
        tot8, nbk, endb, startb, endv = (at(E) for _ in range(5))
        cmp32 = at(E * 32)
        posf = at(2 * U)
        posi, blki, sli = (at(2 * U) for _ in range(3))
        blkf, slf = at(2 * U), at(2 * U)
        ebc = at(NB * E)
        ebf = at(NB)
        ebi = at(NB)
        inv = at(2 * NB)
        invz = at(NB)
        dst_i = at(NB)
        src_i = at(NB)
        oneS = [at(P // 2) for _ in range(2)]
        oneB = [at(NB) for _ in range(2)]
        xg, ye = ([at(P) for _ in range(4)] for _ in range(2))
        xTe = [at(P), at(P)]
        h1, ge, w1e = ([at(F), at(F)] for _ in range(3))
        idg = [at(1) for _ in range(4)]
        idy = [at(1) for _ in range(4)]
        b1s = at(E * FC)
        b2s = at(E * P)
        GB = [at(W) for _ in range(2)]
        assert base <= WORK - U * E, base
        w1s = kv[:, 0:NT // 2].rearrange("p n b w -> p (n b w)")
        w2s = kv[:, NT // 2:NT].rearrange("p n b w -> p (n b w)")
        Y1 = kT[:, :, :].rearrange("p n w -> p (n w)")
        Y2 = qT[:, :, :].rearrange("p n w -> p (n w)")
        lgr = lg

        def o1v(j):
            return (xn2, onT, h2)[j].rearrange("p (b w) -> p b w", b=B)

        def DBG(n):
            return xs[:, n].rearrange("p (b d) -> p b d", b=B)

        CA = {k: ct[:, a:a + n] for k, (a, n) in CONST_AT.items()}
        ident = CA["ident"]

        ps4x = psum("ps4x", [P, 4, 512])
        ps = [psum(f"ps{i}", [P, 512]) for i in range(4)] + [ps4x[:, i] for i in range(4)]

        names = """x_lo x_hi w_in w1_in c_in mod_bc mod_done mod_evac modt_done modt_evac csil_ready cbc_ready wgate_done wgate_evac
            eps_ready st_ready lnw1 lnw2 var_ready std_ready rstd_ready
            xn_ready xT_done hT_ready q_done q_evac k_done k_evac tok_done kv_evac gz_evac ksq_ready kss_ready
            gate_ready kss_cl ksqrt rk_ready za_ready ez_ready lz_ready f_ready g_done f_done eg_ready ef_ready tc_done tc_evac
            te_done td_ready modfix S_zero
            U_done PV_done D_done A_done inter_done T1_done Wo_done T2_done router_done
            Um_ready S_mul S_step P_ready o1_ready o2_ready on_ready x2_ready xn2_ready logits_ready stage_ready
            bnA sumA sqA varA lnA_ready rstdA bnB sumB sqB varB lnB_ready rstdB
            om_ready osum_ready ot_ready kd_ready vx_ready E_ready Qx_ready onT_ready h2T_ready R_ready EM_ready vp_ready vpp_ready o3_ready h2a_ready h2_ready h2_stored modfix2 modfix3
            w2_in y_stored0 y_stored1 y_stored2 y_stored3 y1_in y2_in x3_ready out_stored
            r1 r2 r3 lx_ready le_ready M_ready rank_done pos_ready onehot_ready inv_done inv_evac eb_ready idg_ready
            gath0 gath1 gath2 gath3 w1e_ready Tx_done xT_ready mm1_done h1_ready gelu_ready TG_done gT_ready mm2_done y_ready
            gb_ready c1 c2 c3 bnC sumC sqC varC stdC rstdC c4 c5 c6 wog_ready dbg_out""".split()
        s = {n: sem(n) for n in names}

        def S(n):
            return s[n]

        block = ctx.enter_context(nc.Block())

        def cols(t, start, n):
            return t[:, start:start + n] if isinstance(start, int) else t[:, bass.ds(start, n)]

        def kv_step(n, lo):
            if isinstance(n, int):
                return kv[:, n, :, lo:lo + P]
            return kv[:, bass.ds(n, 1), :, lo:lo + P].rearrange("p a b w -> p (a b) w")

        def gate_step(n):
            if isinstance(n, int):
                return gz[:, n, :, 0:P]
            return gz[:, bass.ds(n, 1), :, 0:P].rearrange("p a b w -> p (a b) w")

        rowbank = ps4x

        x_v = x.rearrange("b (n p) d -> n p b d", p=P)

        def step_view(t, n):
            return t[:, bass.ds(n, 1)].rearrange("p a w -> p (a w)") if not isinstance(n, int) else t[:, n]

        @block.sync
        def _(sp):
            for n in range(NT):
                sp.dma_start(xs[:, n].rearrange("p (b d) -> p b d", b=B), x_v[n]).then_inc(S("x_lo" if n < NT // 2 else "x_hi"), 16)

            h2_v = h2_rows.rearrange("(b n p) d -> n p b d", b=B, p=P)

            def store_h2(q):
                sp.wait_ge(S("h2_ready"), q + 1)
                dst = h2_v[q] if isinstance(q, int) else h2_v[bass.ds(q, 1)].rearrange("a p b d -> (a p) b d")
                sp.dma_start(dst, h2.rearrange("p (b d) -> p b d", b=B)).then_inc(S("h2_stored"), 16)

            with sp.Fori(0, NT) as q:
                store_h2(q)

            sp.wait_ge(S("stage_ready"), NT)
            sp.wait_ge(S("vx_ready"), U)
            sp.dma_start(w1s.rearrange("p (e f) -> p e f", e=E), w1.rearrange("e d f -> d e f")).then_inc(S("w1_in"), 16)
            sp.wait_ge(S("Qx_ready"), NT)
            sp.dma_start(b1s.rearrange("p (e c) -> p e c", e=E), b1_t).then_inc(S("w2_in"), 16)
            sp.dma_start(w2s.rearrange("p (e c d) -> p e c d", e=E, c=FC), w2.rearrange("e (c p) d -> p e c d", p=P)).then_inc(S("w2_in"), 16)
            sp.dma_start(b2s.rearrange("p (e d) -> p e d", e=E), b2.partition_broadcast(P)).then_inc(S("w2_in"), 16)
            sp.dma_start(gam[:, 0], gamma.partition_broadcast(P)).then_inc(S("w2_in"), 16)
            sp.dma_start(gam[:, 1], beta.partition_broadcast(P)).then_inc(S("w2_in"), 16)

            for m in range(4):
                sp.wait_ge(S(f"y_stored{m}"), 16 * (NB // 4))
            y_v = y_rows.rearrange("(k b n p) d -> k p n b d", k=2, b=B, p=P)
            for k, (dst, name) in enumerate(((Y1, "y1_in"), (Y2, "y2_in"))):
                for n in range(NT):
                    sp.dma_start(dst[:, n * W:(n + 1) * W].rearrange("p (b d) -> p b d", b=B), y_v[k, :, n]).then_inc(S(name), 16)
            out_v = out.rearrange("b (n p) d -> n p b d", p=P)
            with sp.Fori(0, NT) as n:
                sp.wait_ge(S("x3_ready"), n + 1)
                sp.dma_start(out_v[bass.ds(n, 1)].rearrange("a p b d -> (a p) b d"), step_view(xs, n).rearrange("p (b d) -> p b d", b=B)).then_inc(S("out_stored"), 16)
            sp.wait_ge(S("out_stored"), 16 * NT)

        W_LOADS = 11

        @block.scalar
        def _(act):
            act.dma_start(cs[:, :], c_t).then_inc(S("c_in"), 16)
            act.dma_start(wmods[:, :], wmod).then_inc(S("c_in"), 16)
            for dst, src in ((ct[:, :], consts), (wqs[:, :], wq_t), (wks[:, :], wk_t), (wtok[:, 0:2 * P], wkv_t),
                             (wtok[:, 3 * P:TOK], wf_t), (wg1s[:, :], wg1), (wg2s[:, :], wg2_t), (wos[:, :], wo_t),
                             (lnws[:, :], lnw), (wgs[:, :], wg), (bgs[:, :], bg.partition_broadcast(P))):
                act.dma_start(dst, src).then_inc(S("w_in"), 16)
            act.wait_ge(S("c_in"), 32)
            nc.scalar.activation(csil[:, :], cs[:, :], ACT.Silu).then_inc(S("csil_ready"), 1)
            act.wait_ge(S("eps_ready"), 1)
            act.wait_ge(S("var_ready"), 1)
            nc.scalar.activation(ln[:, 5], ln[:, 4], ACT.Sqrt, bias=epst[:, 0:1], scale=1.0 / P).then_inc(S("std_ready"), 1)

            def a_step(n):
                act.wait_ge(S("q_done"), n + 1)
                nc.scalar.activation(step_view(qT, n), ps[2][:, :], ACT.Silu).then_inc(S("q_evac"), 1)
                act.wait_ge(S("k_done"), n + 1)
                nc.scalar.activation(step_view(kT, n), ps[3][:, :], ACT.Silu).then_inc(S("k_evac"), 1)
                for b in range(B):
                    act.wait_ge(S("tok_done"), n * B + b + 1)
                    dst = kv[:, bass.ds(n, 1), b].rearrange("p a w -> p (a w)") if not isinstance(n, int) else kv[:, n, b]
                    nc.scalar.activation(dst, ps[4 + b][:, 0:2 * P], ACT.Silu).then_inc(S("kv_evac"), 1)
            for n in range(2):
                a_step(n)
            with act.Fori(1, NT // 2) as i:
                for m in range(2):
                    a_step(i * 2 + m)

            act.wait_ge(S("gz_evac"), U)
            for j in range(4):
                v = gz[:, 2 * j:2 * j + 2, :, 0:P].rearrange("p a b w -> p (a b) w")
                last = nc.scalar.activation(v, v, ACT.Sigmoid)
            last.then_inc(S("gate_ready"), 1)
            act.wait_ge(S("kss_cl"), 1)
            nc.scalar.activation(rk[:, :], rk[:, :], ACT.Sqrt).then_inc(S("ksqrt"), 1)
            act.wait_ge(S("za_ready"), 1)
            nc.scalar.activation(za, za, ACT.Exp, scale=-1.0).then_inc(S("ez_ready"), 1)
            act.wait_ge(S("ez_ready"), 1)
            nc.scalar.activation(za, za, ACT.Ln, bias=1.0).then_inc(S("lz_ready"), 1)
            act.wait_ge(S("g_done"), 1)
            nc.scalar.activation(eg[:, :], ps[0][:, :], ACT.Exp).then_inc(S("eg_ready"), 1)
            act.wait_ge(S("f_done"), 1)
            for b in range(B):
                last = nc.scalar.activation(ef[:, :].rearrange("p (n g b s) -> p b n g s", n=NT, g=G, b=B)[:, b],
                                            ps[1][:, :].rearrange("p (n b g s) -> p b n g s", n=NT, g=G, b=B)[:, b], ACT.Exp)
            last.then_inc(S("ef_ready"), 1)
            act.wait_ge(S("te_done"), 1)
            nc.scalar.activation(td[:, :], ps[3][:, 0:U * NC], ACT.Exp).then_inc(S("td_ready"), 1)

            def decay(t, b):
                act.wait_ge(S("D_done"), t + 1)
                wait(act, S("P_ready"), t - 1)
                nc.scalar.activation(EM[b % 2], ps[b % 2][:, :], ACT.Exp).then_inc(S("E_ready"), 1)

            def spread_q(n):
                wait(act, S("A_done"), n * B)
                for h in range(HG):
                    last = nc.scalar.activation(Qx[:, h * W:(h + 1) * W], step_view(qT, n), ACT.Copy, scale=CA["head_of"][:, h:h + 1])
                last.then_inc(S("Qx_ready"), 1)

            def evacuate_on(q):
                act.wait_ge(S("T1_done"), q + 1)
                wait(act, S("router_done"), q - 1)
                nc.scalar.activation(onT, ps[2][:, :], ACT.Copy).then_inc(S("onT_ready"), 1)

            def evacuate_h2(q):
                act.wait_ge(S("T2_done"), q + 1)
                act.wait_ge(S("Wo_done"), min(q + 2, NT) if isinstance(q, int) else q + 2)
                if isinstance(q, int) and q == NT - 1:
                    act.wait_ge(S("router_done"), NT - 1)
                nc.scalar.activation(h2T, ps[2][:, :], ACT.Copy).then_inc(S("h2T_ready"), 1)

            def act_step(n, m, A=True, Bt=True, more=True):
                t = n * B
                decay(t + 1, 1)
                decay(t + 2, 2)
                decay(t + 3, 3)
                if A: evacuate_on(n - 1)
                if more:
                    decay(t + 4, 0)
                    spread_q(n + 1)
                if Bt: evacuate_h2(n - 2)

            act.wait_ge(S("w_in"), 16 * W_LOADS)
            act.wait_ge(S("q_evac"), NT)
            spread_q(0)
            decay(0, 0)
            act_step(0, 0, A=False, Bt=False)
            act_step(1, 1, Bt=False)
            act_step(2, 0)
            with act.Fori(1, NT // 2 - 1) as i:
                for m in range(2):
                    act_step(i * 2 + 1 + m, 1 - m)
            act_step(NT - 1, 1, more=False)
            evacuate_on(NT - 1)
            evacuate_h2(NT - 2)
            evacuate_h2(NT - 1)

            act.wait_ge(S("lx_ready"), 1)
            nc.scalar.activation(wt, lgx, ACT.Exp).then_inc(S("le_ready"), 1)

            act.wait_ge(S("eb_ready"), 1)
            act.wait_ge(S("w1_in"), 16)

            def expert(i):
                return act.value_load(ebi[0:1, i:i + 1].bitcast(I32) if isinstance(i, int) else ebi[0:1, bass.ds(i, 1)].bitcast(I32), min_val=0, max_val=E - 1)

            def take_w1(i, m):
                e = expert(i)
                wait(act, S("mm1_done"), i - 1)
                nc.scalar.activation(w1e[m], w1s[:, bass.ds(e * F, F)], ACT.Copy).then_inc(S("w1e_ready"), 1)

            def gelu(i, m):
                act.wait_ge(S("h1_ready"), i + 1)
                wait(act, S("mm2_done"), i - 1)
                nc.scalar.activation(ge[m], h1[m], ACT.Gelu).then_inc(S("gelu_ready"), 1)

            take_w1(0, 0)
            take_w1(1, 1)
            gelu(0, 0)
            for i in range(2, 4):
                take_w1(i, i % 2)
                gelu(i - 1, (i - 1) % 2)
            with act.Fori(1, NB // 4) as j:
                for m in range(4):
                    take_w1(j * 4 + m, m % 2)
                    gelu(j * 4 + m - 1, (m - 1) % 2)
            gelu(NB - 1, 1)

            act.wait_ge(S("varC"), 1)
            nc.scalar.activation(ln[:, 5], ln[:, 4], ACT.Sqrt, bias=epst[:, 0:1], scale=1.0 / P).then_inc(S("stdC"), 1)

        @block.tensor
        def _(pe):
            pe.wait_ge(S("c_in"), 32)
            pe.wait_ge(S("csil_ready"), 1)
            for i in range(2):
                last = nc.tensor.matmul(ps[0][:, 4 * i:4 * i + 4], wmods[:, i * D:(i + 1) * D], csil[:, :], start=True, stop=True)
            last.then_inc(S("modt_done"), 1)
            pe.wait_ge(S("w_in"), 16 * W_LOADS)
            nc.tensor.matmul(ps[1][:, 0:P], wg1s[:, :], wg2s[:, :], start=True, stop=True).then_inc(S("wgate_done"), 1)
            pe.wait_ge(S("cbc_ready"), 1)
            for b in range(B):
                last = nc.tensor.matmul(ps[4 + b][:, :], cbc[:, b], wmods[:, 2 * D:6 * D], start=True, stop=True)
            last.then_inc(S("mod_done"), 1)

            def transposes(n, m):
                wait(pe, S("xn_ready"), n * B + B)
                wait(pe, S("hT_ready"), (n - 1) * B)
                for b in range(B):
                    last = nc.tensor.transpose(ps[m][:, b * P:(b + 1) * P], xn[m][:, b * P:(b + 1) * P], ident)
                last.then_inc(S("xT_done"), 1)

            def projections(n, m):
                wait(pe, S("hT_ready"), (n + 1) * B)
                wait(pe, S("q_evac"), n)
                nc.tensor.matmul(ps[2][:, :], wqs[:, :], hT[m], start=True, stop=True).then_inc(S("q_done"), 1)
                wait(pe, S("k_evac"), n)
                nc.tensor.matmul(ps[3][:, :], wks[:, :], hT[m], start=True, stop=True).then_inc(S("k_done"), 1)
                for b in range(B):
                    wait(pe, S("kv_evac"), (n - 1) * B + b + 1)
                    wait(pe, S("gz_evac"), (n - 1) * B + b + 1)
                    nc.tensor.matmul(ps[4 + b][:, 0:TOK], hT[m][:, b * P:(b + 1) * P], wtok[:, :], start=True, stop=True).then_inc(S("tok_done"), 1)

            pe.wait_ge(S("modt_evac"), 1)
            pe.wait_ge(S("wgate_evac"), 1)
            transposes(0, 0)
            transposes(1, 1)
            pe.wait_ge(S("mod_evac"), 1)
            projections(0, 0)
            with pe.Fori(1, NT // 2) as i:
                for m in range(2):
                    n = i * 2 + m
                    transposes(n, m)
                    projections(n - 1, 1 - m)
            projections(NT - 1, 1)

            pe.wait_ge(S("f_ready"), 1)
            pe.wait_ge(S("gz_evac"), U)
            pe.wait_ge(S("k_evac"), NT)
            nc.tensor.matmul(ps[0][:, :], CA["later"], zf[:, :], start=True, stop=True).then_inc(S("g_done"), 1)
            nc.tensor.matmul(ps[1][:, :], CA["upto"], zf[:, :], start=True, stop=True).then_inc(S("f_done"), 1)
            for u in range(U):
                last = nc.tensor.matmul(ps[2][0:H, u * NC:(u + 1) * NC], zf[:, u * H:(u + 1) * H], CA["chunk_of"], start=True, stop=True)
            last.then_inc(S("tc_done"), 1)
            pe.wait_ge(S("tc_evac"), 1)
            nc.tensor.matmul(ps[3][:, 0:U * NC], CA["headsel"][0:H, :], tc[:, :], start=True, stop=True).then_inc(S("te_done"), 1)

            def open_group(dst):
                nc.tensor.matmul(dst, onebf[:, :], onebf[:, 0:1], start=True, stop=True)

            def state_updates(n, m):
                pe.wait_ge(S("kd_ready"), n + 1)
                pe.wait_ge(S("vx_ready"), (n + 1) * B)
                wait(pe, S("o1_ready"), n)
                for b in range(B):
                    for g in range(G):
                        at = b * P + g * C
                        last = nc.tensor.matmul(rowbank[g * C:(g + 1) * C, 0, b * P:(b + 1) * P], kd[m][:, at:at + C],
                                                vx[m][:, b * W + g * P:b * W + (g + 1) * P], start=True, stop=True)
                last.then_inc(S("U_done"), 1)

            def log_decay(t, b):
                pe.wait_ge(S("R_ready"), t + 1)
                wait(pe, S("E_ready"), t - 1)
                nc.tensor.matmul(ps[b % 2][:, :], CA["later"], R[b % 2], start=True, stop=True).then_inc(S("D_done"), 1)

            def scores(t, n, m, b):
                if b == 0:
                    pe.wait_ge(S("Um_ready"), n + 1)
                    pe.wait_ge(S("Qx_ready"), n + 1)
                    pe.wait_ge(S("stage_ready"), n + 1)
                else:
                    pe.wait_ge(S("P_ready"), t)
                open_group(rowbank[0:C, 0, 0:1])
                for c in range(NC):
                    at = b * P + c * C
                    for g in range(G):
                        rows = slice(g * C, (g + 1) * C)
                        q = Qx[rows, :].rearrange("p (s w) -> p s w", s=HG)[:, :, at:at + C]
                        last = nc.tensor.matmul(rowbank[c * C:(c + 1) * C, g, 0:P], kTs[m][rows, at:at + C], q, start=True, stop=True)
                last.then_inc(S("A_done"), 1)

            def weighted_values(t, n, m, b):
                pe.wait_ge(S("P_ready"), t + 1)
                wait(pe, S("om_ready"), t)
                for g in range(G):
                    last = nc.tensor.matmul(ps[3][:, g * P:(g + 1) * P], vx[m][:, b * W + g * P:b * W + (g + 1) * P], PR[b % 2][:, g * P:(g + 1) * P],
                                            start=True, stop=True)
                last.then_inc(S("PV_done"), 1)

            def state_terms(n, m):
                pe.wait_ge(S("P_ready"), (n + 1) * B)
                pe.wait_ge(S("S_step"), (n + 1) * NC)
                open_group(rowbank[0:C, 0, 0:1])
                for b in range(B):
                    for c in range(NC):
                        for g in range(G):
                            rows = slice(g * C, (g + 1) * C)
                            last = nc.tensor.matmul(rowbank[c * C:(c + 1) * C, g, b * C:(b + 1) * C], qTs[m][rows, b * P + c * C:b * P + (c + 1) * C],
                                                    Sb[m][rows, (c * B + b) * C:(c * B + b + 1) * C], start=True, stop=True)
                last.then_inc(S("inter_done"), 1)

            def turn_on(q):
                pe.wait_ge(S("on_ready"), q + 1)
                wait(pe, S("logits_ready"), q - 1)
                for b in range(B):
                    last = nc.tensor.transpose(ps[2][:, b * P:(b + 1) * P], on[:, b * P:(b + 1) * P], ident)
                last.then_inc(S("T1_done"), 1)

            def output_projection(q):
                pe.wait_ge(S("onT_ready"), q + 1)
                for b in range(B):
                    last = nc.tensor.matmul(ps[2][:, b * P:(b + 1) * P], onT[:, b * P:(b + 1) * P], wog[:, b], start=True, stop=True)
                last.then_inc(S("Wo_done"), 1)

            def turn_h2(q):
                pe.wait_ge(S("h2_ready"), q + 1)
                pe.wait_ge(S("x2_ready"), min(q + 2, NT) if isinstance(q, int) else q + 2)
                if isinstance(q, int) and q == NT - 1:
                    pe.wait_ge(S("logits_ready"), NT - 1)
                for b in range(B):
                    last = nc.tensor.transpose(ps[2][:, b * P:(b + 1) * P], h2[:, b * P:(b + 1) * P], ident)
                last.then_inc(S("T2_done"), 1)

            def router(q):
                pe.wait_ge(S("h2T_ready"), q + 1)
                for b in range(B):
                    last = nc.tensor.matmul(ps[2][:, b * E:(b + 1) * E], h2T[:, b * P:(b + 1) * P], wgs[:, :], start=True, stop=True)
                last.then_inc(S("router_done"), 1)

            def pe_step(n, m, A=True, Bt=True, more=True):
                t = n * B
                state_updates(n, m)
                if A: weighted_values(t - 1, n - 1, 1 - m, 3)
                scores(t, n, m, 0)
                log_decay(t + 2, 2)
                scores(t + 1, n, m, 1)
                weighted_values(t, n, m, 0)
                log_decay(t + 3, 3)
                scores(t + 2, n, m, 2)
                weighted_values(t + 1, n, m, 1)
                if A: turn_on(n - 1)
                if more: log_decay(t + 4, 0)
                scores(t + 3, n, m, 3)
                if A: output_projection(n - 1)
                weighted_values(t + 2, n, m, 2)
                if more: log_decay(t + 5, 1)
                state_terms(n, m)
                if Bt:
                    turn_h2(n - 2)
                    router(n - 2)

            pe.wait_ge(S("eg_ready"), 1)
            pe.wait_ge(S("ef_ready"), 1)
            log_decay(0, 0)
            log_decay(1, 1)
            pe.wait_ge(S("td_ready"), 1)
            pe.wait_ge(S("wog_ready"), B)
            pe.wait_ge(S("eps_ready"), 3)
            pe_step(0, 0, A=False, Bt=False)
            pe_step(1, 1, Bt=False)
            pe_step(2, 0)
            with pe.Fori(1, NT // 2 - 1) as i:
                for m in range(2):
                    pe_step(i * 2 + 1 + m, 1 - m)
            pe_step(NT - 1, 1, more=False)
            weighted_values(U - 1, NT - 1, 1, 3)
            turn_on(NT - 1)
            output_projection(NT - 1)
            turn_h2(NT - 2)
            router(NT - 2)
            turn_h2(NT - 1)
            router(NT - 1)

            pe.wait_ge(S("M_ready"), 1)
            nc.tensor.matmul(ps[0][:, 0:UE], CA["before"], M, start=True, stop=True).then_inc(S("rank_done"), 1)
            nc.tensor.matmul(ps[1][:, 0:UE], CA["ones"], M, start=True, stop=True).then_inc(S("rank_done"), 1)
            pe.wait_ge(S("logits_ready"), NT)
            def place(i, m, first, last):
                pe.wait_ge(S("onehot_ready"), i + 1)
                nc.tensor.matmul(ps[2][:, 0:2 * NB], oneS[m].bitcast(BF16)[:, 0:P], oneB[m].bitcast(BF16)[:, 0:2 * NB], start=first, stop=last).then_inc(S("inv_done"), 1)
            place(0, 0, True, False)
            place(1, 1, False, False)
            with pe.Fori(1, U - 1) as j:
                for m in range(2):
                    place(j * 2 + m, m, False, False)
            place(2 * U - 2, 0, False, False)
            place(2 * U - 1, 1, False, True)

            pe.wait_ge(S("eb_ready"), 1)
            pe.wait_ge(S("w1_in"), 16)
            pe.wait_ge(S("w2_in"), 16 * 5)
            pe.wait_ge(S("inv_evac"), 2)

            def expert(i):
                return pe.value_load(ebi[0:1, i:i + 1].bitcast(I32) if isinstance(i, int) else ebi[0:1, bass.ds(i, 1)].bitcast(I32), min_val=0, max_val=E - 1)

            def turn_rows(i, j, m4):
                m = m4 % 2
                pe.wait_ge(S(f"gath{m4}"), 16 * (j + 1))
                wait(pe, S("xT_ready"), i - 1)
                nc.tensor.transpose(ps[m][:, 0:P], xg[m4], ident).then_inc(S("Tx_done"), 1)

            def hidden(i, m):
                pe.wait_ge(S("w1e_ready"), i + 1)
                pe.wait_ge(S("xT_ready"), i + 1)
                wait(pe, S("h1_ready"), i - 1)
                for c in range(FC):
                    last = nc.tensor.matmul(ps[2 + m][:, c * P:(c + 1) * P], w1e[m][:, c * P:(c + 1) * P], xTe[m], start=True, stop=True)
                last.then_inc(S("mm1_done"), 1)

            def result(i, m, e):
                pe.wait_ge(S("gelu_ready"), i + 1)
                wait(pe, S("y_ready"), i - 1)
                for c in range(FC):
                    last = nc.tensor.matmul(ps[4 + m][:, 0:P], ge[m][:, c * P:(c + 1) * P], w2s[:, bass.ds(e * F + c * P, P)], start=(c == 0), stop=(c == FC - 1))
                last.then_inc(S("mm2_done"), 1)

            def pe_block(i, j, m):
                e = expert(i - 2)
                turn_rows(i, j, m)
                hidden(i - 1, (m - 1) % 2)
                result(i - 2, m % 2, e)

            turn_rows(0, 0, 0)
            turn_rows(1, 0, 1)
            hidden(0, 0)
            pe_block(2, 0, 2)
            pe_block(3, 0, 3)
            with pe.Fori(1, NB // 4) as j:
                for m in range(4):
                    pe_block(j * 4 + m, j, m)
            e = expert(NB - 2)
            hidden(NB - 1, 1)
            result(NB - 2, 0, e)
            result(NB - 1, 1, expert(NB - 1))

        @block.vector
        def _(dve):
            nc.vector.memset(epst[:, 0:1], EPS_LN).then_inc(S("eps_ready"), 1)
            nc.vector.memset(epst[:, 1:2], -0.5).then_inc(S("eps_ready"), 1)
            nc.vector.memset(onebf[:, :], 1.0).then_inc(S("eps_ready"), 1)

            for half, name in enumerate(("x_lo", "x_hi")):
                dve.wait_ge(S(name), 16 * NT // 2)
                with dve.Fori(half * U // 2 // 4, (half + 1) * U // 2 // 4) as n:
                    for b in range(B):
                        nc.vector.bn_stats(st[:, bass.ds(n * B + b, 1)].rearrange("p a w -> p (a w)"),
                                           xs[:, bass.ds(n, 1), b * P:(b + 1) * P].rearrange("p a w -> p (a w)")).then_inc(S("st_ready"), 1)
            dve.wait_ge(S("st_ready"), U)
            nc.vector.tensor_tensor(ln[:, 0], st[:, :, 1], st[:, :, 4], ALU.add).then_inc(S("lnw1"), 1)
            nc.vector.tensor_tensor(ln[:, 1], st[:, :, 1], st[:, :, 4], ALU.subtract).then_inc(S("lnw1"), 1)
            nc.vector.tensor_tensor(ln[:, 2], st[:, :, 2], st[:, :, 5], ALU.add).then_inc(S("lnw1"), 1)
            dve.wait_ge(S("lnw1"), 3)
            nc.vector.tensor_tensor(ln[:, 3], ln[:, 1], ln[:, 1], ALU.mult).then_inc(S("lnw2"), 1)
            nc.vector.tensor_scalar(mean[:, :], ln[:, 0], 0.5, None, ALU.mult).then_inc(S("lnw2"), 1)
            dve.wait_ge(S("lnw2"), 1)
            nc.vector.scalar_tensor_tensor(out=ln[:, 4], in0=ln[:, 3], scalar=P / 4.0, in1=ln[:, 2], op0=ALU.mult, op1=ALU.add).then_inc(S("var_ready"), 1)

            dve.wait_ge(S("csil_ready"), 1)
            nc.vector.tensor_copy(cbc[:, :, :], csil[:, :].unsqueeze(2).to_broadcast([P, B, P])).then_inc(S("cbc_ready"), 1)
            dve.wait_ge(S("modt_done"), 1)
            nc.vector.tensor_copy(modT[:, 0], ps[0][:, 0:B])
            nc.vector.tensor_scalar(modT[:, 1], ps[0][:, B:2 * B], 1.0, None, ALU.add).then_inc(S("modt_evac"), 1)
            dve.wait_ge(S("wgate_done"), 1)
            nc.vector.tensor_copy(wtok[:, 2 * P:3 * P], ps[1][:, 0:P]).then_inc(S("wgate_evac"), 1)
            dve.wait_ge(S("std_ready"), 1)
            nc.vector.reciprocal(rstd[:, :], ln[:, 5]).then_inc(S("rstd_ready"), 1)
            dve.wait_ge(S("mod_done"), 1)
            for b in range(B):
                last = nc.vector.tensor_copy(mod[:, :, b], ps[4 + b][:, :].rearrange("p (j d) -> p j d", j=4))
            last.then_inc(S("mod_evac"), 1)
            dve.wait_ge(S("rstd_ready"), 1)
            dve.wait_ge(S("lnw2"), 2)
            dve.wait_ge(S("modt_evac"), 1)

            def col(t, n, b):
                return t[:, n * B + b:n * B + b + 1] if isinstance(n, int) else t[:, bass.ds(n * B + b, 1)]

            def normalize(n, m):
                wait(dve, S("xT_done"), n - 1)
                src = step_view(xs, n)
                for b in range(B):
                    nc.vector.tensor_scalar(xn[m][:, b * P:(b + 1) * P], src[:, b * P:(b + 1) * P], col(mean, n, b), col(rstd, n, b),
                                            ALU.subtract, ALU.mult).then_inc(S("xn_ready"), 1)

            def modulate(n, m):
                dve.wait_ge(S("xT_done"), n + 1)
                wait(dve, S("tok_done"), (n - 1) * B)
                for b in range(B):
                    nc.vector.tensor_scalar(hT[m][:, b * P:(b + 1) * P], ps[m][:, b * P:(b + 1) * P], modT[:, 1, b:b + 1], modT[:, 0, b:b + 1],
                                            ALU.mult, ALU.add).then_inc(S("hT_ready"), 1)

            def keep_gate(n):
                for b in range(B):
                    dve.wait_ge(S("kv_evac"), n * B + b + 1)
                    dst = gz[:, bass.ds(n, 1), b].rearrange("p a w -> p (a w)") if not isinstance(n, int) else gz[:, n, b]
                    nc.vector.tensor_copy(dst, ps[4 + b][:, 2 * P:TOK]).then_inc(S("gz_evac"), 1)

            def key_sums(n, m):
                dve.wait_ge(S("ksq_ready"), n + 1)
                w = B * H
                dst = rk[:, n * w:(n + 1) * w] if isinstance(n, int) else rk[:, bass.ds(n * w, w)]
                nc.vector.tensor_reduce(dst, ksq[m].rearrange("p (g d) -> p g d", d=HD), AX, ALU.add).then_inc(S("kss_ready"), 1)

            normalize(0, 0)
            normalize(1, 1)
            modulate(0, 0)
            modulate(1, 1)
            keep_gate(0)
            with dve.Fori(1, NT // 2) as i:
                for m in range(2):
                    n = i * 2 + m
                    normalize(n, m)
                    modulate(n, m)
                    keep_gate(n - 1)
                    key_sums(n - 2, m)
            keep_gate(NT - 1)
            key_sums(NT - 2, 0)
            key_sums(NT - 1, 1)

            dve.wait_ge(S("kss_ready"), NT)
            nc.vector.tensor_scalar(rk[:, :], rk[:, :], EPS_NORM * EPS_NORM, None, ALU.max).then_inc(S("kss_cl"), 1)
            dve.wait_ge(S("gz_evac"), U)
            z = gz[:, :, :, P:P + H].rearrange("p n b h -> p (n b) h")
            za3 = za.rearrange("p (u h) -> p u h", h=H)
            nc.vector.scalar_tensor_tensor(out=za3, in0=z, scalar=-1.0, in1=z, op0=ALU.mult, op1=ALU.max).then_inc(S("za_ready"), 1)
            nc.vector.tensor_scalar(mod[:, 2], mod[:, 2], 1.0, None, ALU.add).then_inc(S("modfix3"), 1)
            for k, j in enumerate((0, 3)):
                nc.vector.scalar_tensor_tensor(out=o1v(0), in0=mod[:, j], scalar=-1.0, in1=mod[:, j], op0=ALU.mult, op1=ALU.max).then_inc(S("modfix"), 1)
                nc.vector.tensor_scalar(o1v(1), mod[:, j], 0.0, 2.0, ALU.is_ge, ALU.mult).then_inc(S("modfix"), 1)
                dve.wait_ge(S("modfix"), 2 * k + 2)
                nc.vector.tensor_scalar(o1v(2), o1v(0), 0.25, None, ALU.max).then_inc(S("modfix2"), 1)
                dve.wait_ge(S("modfix2"), k + 1)
                nc.vector.scalar_tensor_tensor(out=mod[:, j], in0=o1v(1), scalar=-1.0, in1=o1v(2), op0=ALU.add, op1=ALU.mult).then_inc(S("modfix3"), 1)
                dve.wait_ge(S("modfix3"), k + 2)
            for b in range(B):
                nc.vector.scalar_tensor_tensor(out=wog[:, b], in0=wos[:, :], scalar=lnws[:, 0:1], in1=mod[:, 0, b], op0=ALU.mult, op1=ALU.mult).then_inc(S("wog_ready"), 1)
            dve.wait_ge(S("lz_ready"), 1)
            nc.vector.scalar_tensor_tensor(out=zf[:, :].rearrange("p (u h) -> p u h", h=H), in0=z, scalar=0.0, in1=za3, op0=ALU.min,
                                           op1=ALU.subtract).then_inc(S("f_ready"), 1)
            dve.wait_ge(S("ksqrt"), 1)
            nc.vector.reciprocal(rk[:, :], rk[:, :]).then_inc(S("rk_ready"), 1)
            dve.wait_ge(S("tc_done"), 1)
            nc.vector.tensor_copy(tc[:, :], ps[2][0:H, 0:U * NC]).then_inc(S("tc_evac"), 1)

            def stage(n, m):
                wait(dve, S("A_done"), (n - 1) * B)
                nc.vector.tensor_copy(kTs[m], step_view(kT, n))
                wait(dve, S("inter_done"), n - 1)
                nc.vector.tensor_copy(qTs[m], step_view(qT, n)).then_inc(S("stage_ready"), 1)

            def take_updates(n):
                dve.wait_ge(S("U_done"), n + 1)
                wait(dve, S("S_step"), n * NC)
                nc.vector.tensor_tensor(Um.rearrange("p (c b w) -> p c b w", c=NC, b=B), rowbank[:, 0, :].rearrange("p (b c w) -> p c b w", b=B, c=NC),
                                        CA["blockmask"].unsqueeze(1).unsqueeze(1).to_broadcast([P, NC, B, C]), ALU.mult).then_inc(S("Um_ready"), 1)

            def state_chain(n, m):
                dve.wait_ge(S("Um_ready"), n + 1)
                wait(dve, S("inter_done"), n)
                for c in range(NC):
                    wait(dve, S("S_step"), n * NC + c)
                    before = Sb[m][:, c * B * C:(c + 1) * B * C].rearrange("p (b w) -> p b w", b=B)
                    tdc = cols(td, n * B * NC, B * NC).rearrange("p (b c) -> p b c", c=NC)[:, :, c:c + 1].to_broadcast([P, B, C])
                    nc.vector.tensor_tensor(stmp.rearrange("p (b w) -> p b w", b=B), before, tdc, ALU.mult).then_inc(S("S_mul"), 1)
                    dve.wait_ge(S("S_mul"), n * NC + c + 1)
                    dst = Sb[m][:, (c + 1) * B * C:(c + 2) * B * C] if c < NC - 1 else Sb[1 - m][:, 0:B * C]
                    nc.vector.tensor_tensor(dst, stmp, Um[:, c * B * C:(c + 1) * B * C], ALU.add).then_inc(S("S_step"), 1)

            def weigh(t, b):
                dve.wait_ge(S("A_done"), t + 1)
                dve.wait_ge(S("EM_ready"), t + 1)
                wait(dve, S("PV_done"), t - 1)
                nc.vector.tensor_tensor(PR[b % 2].rearrange("p (g w) -> p g w", g=G), EM[b % 2].rearrange("p (g w) -> p g w", g=G),
                                        rowbank[:, :, 0:P], ALU.mult).then_inc(S("P_ready"), 1)

            def take_state_terms(n):
                dve.wait_ge(S("inter_done"), n + 1)
                wait(dve, S("o2_ready"), n)
                nc.vector.tensor_tensor(o1.rearrange("p (g q d) -> p g q d", g=G, d=HD), rowbank[:, :, 0:B * C].rearrange("p g (q d) -> p g q d", d=HD),
                                        cols(ef, n * B * H, B * H).rearrange("p (g q) -> p g q", g=G).unsqueeze(3).to_broadcast([P, G, B * HG, HD]),
                                        ALU.mult).then_inc(S("o1_ready"), 1)

            def take_values(t, n, b):
                dve.wait_ge(S("PV_done"), t + 1)
                wait(dve, S("osum_ready"), t)
                nc.vector.tensor_tensor(om.rearrange("p (g s i) -> p g s i", g=G, s=HG), ps[3][:, :].rearrange("p (g s i) -> p g s i", g=G, s=HG),
                                        CA["head_of"].unsqueeze(1).unsqueeze(3).to_broadcast([P, G, HG, C]), ALU.mult).then_inc(S("om_ready"), 1)
                dve.wait_ge(S("om_ready"), t + 1)
                if b == 0: wait(dve, S("ot_ready"), n)
                nc.vector.tensor_reduce(osum[:, b * P:(b + 1) * P].rearrange("p (g i) -> p g i", g=G), om.rearrange("p (g s i) -> p g i s", g=G, s=HG),
                                        AX, ALU.add).then_inc(S("osum_ready"), 1)

            def add_values(q):
                dve.wait_ge(S("osum_ready"), (q + 1) * B)
                wait(dve, S("o2_ready"), q)
                nc.vector.transpose(ot, osum).then_inc(S("ot_ready"), 1)
                dve.wait_ge(S("ot_ready"), q + 1)
                dve.wait_ge(S("o1_ready"), q + 1)
                wait(dve, S("T1_done"), q)
                nc.vector.tensor_tensor(o2.rearrange("p (b g w) -> p b g w", b=B, g=G), o1.rearrange("p (g b w) -> p b g w", b=B, g=G),
                                        ot.rearrange("p (b g w) -> p b g w", b=B, g=G), ALU.add).then_inc(S("o2_ready"), 1)

            def before_statistics(q, tag, src_ready):
                dve.wait_ge(S(src_ready), q + 1)
                wait(dve, S("sum" + tag), 4 * q)

            def statistics(q, k, tag, src):
                for b in range(B):
                    last = nc.vector.bn_stats(stb[k][:, 6 * b:6 * b + 6], src[:, b * P:(b + 1) * P])
                last.then_inc(S("bn" + tag), 1)
                dve.wait_ge(S("bn" + tag), q + 1)
                wait(dve, S("sq" + tag), 2 * q)
                wait(dve, S("var" + tag), q)
                sv = stb[k].rearrange("p (b s) -> p b s", s=6)
                L = lambda j: lnb[k][:, j * B:(j + 1) * B]
                nc.vector.tensor_tensor(L(0), sv[:, :, 1], sv[:, :, 4], ALU.add).then_inc(S("sum" + tag), 1)
                nc.vector.tensor_tensor(L(1), sv[:, :, 1], sv[:, :, 4], ALU.subtract).then_inc(S("sum" + tag), 1)
                nc.vector.tensor_tensor(L(2), sv[:, :, 2], sv[:, :, 5], ALU.add).then_inc(S("sum" + tag), 1)
                dve.wait_ge(S("sum" + tag), 4 * q + 3)
                wait(dve, S("on_ready" if tag == "A" else "xn2_ready"), q)
                nc.vector.tensor_tensor(L(3), L(1), L(1), ALU.mult).then_inc(S("sq" + tag), 1)
                nc.vector.tensor_scalar(L(7), L(0), 0.5, None, ALU.mult).then_inc(S("sq" + tag), 1)
                dve.wait_ge(S("sq" + tag), 2 * q + 1)
                wait(dve, S("rstd" + tag), q)
                nc.vector.scalar_tensor_tensor(out=L(5), in0=L(3), scalar=P / 4.0, in1=L(2), op0=ALU.mult, op1=ALU.add).then_inc(S("sum" + tag), 1)
                dve.wait_ge(S("sum" + tag), 4 * q + 4)
                nc.vector.tensor_scalar(L(4), L(5), 1.0 / P, EPS_LN, ALU.mult, ALU.add).then_inc(S("var" + tag), 1)

            def scale_rows(q, k, tag, dst, src, done):
                dve.wait_ge(S("rstd" + tag), q + 1)
                dve.wait_ge(S("sq" + tag), 2 * q + 2)
                for b in range(B):
                    last = nc.vector.tensor_scalar(dst[:, b * P:(b + 1) * P], src[:, b * P:(b + 1) * P], lnb[k][:, 7 * B + b:7 * B + b + 1],
                                                   lnb[k][:, 6 * B + b:6 * B + b + 1], ALU.subtract, ALU.mult)
                last.then_inc(S(done), 1)

            def add_attention(q):
                dve.wait_ge(S("Wo_done"), q + 1)
                v = step_view(xs, q)
                nc.vector.tensor_tensor(v, v, ps[2][:, :], ALU.add).then_inc(S("x2_ready"), 1)

            def keep_logits(q):
                dve.wait_ge(S("router_done"), q + 1)
                nc.vector.tensor_tensor(cols(lg, q * B * E, B * E).rearrange("p (b e) -> p b e", b=B), ps[2][:, 0:B * E].rearrange("p (b e) -> p b e", b=B),
                                        bgs[:, :].unsqueeze(1).to_broadcast([P, B, E]), ALU.add).then_inc(S("logits_ready"), 1)

            def stats_A(q):
                before_statistics(q, "A", "o3_ready")
                statistics(q, 0, "A", o3)

            def stats_B(q):
                statistics(q, 1, "B", step_view(xs, q))

            def scale_A(q):
                scale_rows(q, 0, "A", on, o3, "on_ready")

            def scale_B(q):
                wait(dve, S("h2_ready"), q)
                scale_rows(q, 1, "B", xn2, step_view(xs, q), "xn2_ready")

            def dve_step(n, m, A=True, Bt=True, more=True):
                t = n * B
                take_updates(n)
                state_chain(n, m)
                if Bt: before_statistics(n - 2, "B", "x2_ready")
                weigh(t, 0)
                if Bt: stats_B(n - 2)
                if A:
                    take_values(t - 1, n - 1, 3)
                    add_values(n - 1)
                weigh(t + 1, 1)
                take_values(t, n, 0)
                if A: stats_A(n - 1)
                if Bt: scale_B(n - 2)
                if A: scale_A(n - 1)
                weigh(t + 2, 2)
                take_values(t + 1, n, 1)
                if more: stage(n + 1, 1 - m)
                weigh(t + 3, 3)
                take_values(t + 2, n, 2)
                if A: add_attention(n - 1)
                take_state_terms(n)
                if Bt: keep_logits(n - 2)

            nc.vector.memset(Sb[0][:, 0:B * C], 0.0).then_inc(S("S_zero"), 1)
            dve.wait_ge(S("S_zero"), 1)
            dve.wait_ge(S("k_evac"), NT)
            stage(0, 0)
            dve.wait_ge(S("td_ready"), 1)
            dve_step(0, 0, A=False, Bt=False)
            dve_step(1, 1, Bt=False)
            dve_step(2, 0)
            with dve.Fori(1, NT // 2 - 1) as i:
                for m in range(2):
                    dve_step(i * 2 + 1 + m, 1 - m)
            dve_step(NT - 1, 1, more=False)
            take_values(U - 1, NT - 1, 3)
            add_values(NT - 1)
            stats_A(NT - 1)
            before_statistics(NT - 2, "B", "x2_ready")
            stats_B(NT - 2)
            scale_A(NT - 1)
            scale_B(NT - 2)
            add_attention(NT - 1)
            keep_logits(NT - 2)
            before_statistics(NT - 1, "B", "x2_ready")
            stats_B(NT - 1)
            scale_B(NT - 1)
            keep_logits(NT - 1)

            def e3(t):
                return t.rearrange("p (u e) -> p u e", e=E)

            def eb(t):
                return t.unsqueeze(2).to_broadcast([P, U, E])

            steps = [0]

            def then(ins):
                steps[0] += 1
                ins.then_inc(S("r1"), 1)
                dve.wait_ge(S("r1"), steps[0])

            V = nc.vector
            dve.wait_ge(S("logits_ready"), NT)
            dve.wait_ge(S("h2_ready"), NT)
            dve.wait_ge(S("router_done"), NT)
            dve.wait_ge(S("h2_stored"), 16 * NT)
            then(V.tensor_reduce(mx, e3(lg), AX, ALU.max))
            V.tensor_tensor(e3(lgx), e3(lg), eb(mx), ALU.subtract).then_inc(S("lx_ready"), 1)
            dve.wait_ge(S("le_ready"), 1)
            then(V.tensor_reduce(zs, e3(wt), AX, ALU.add))
            then(V.reciprocal(m1, zs))
            then(V.tensor_tensor(e3(wt), e3(wt), eb(m1), ALU.mult))
            rank8 = CA["rank8"].unsqueeze(1).to_broadcast([P, U, E])

            def choose(src, top, onehot):
                then(V.tensor_reduce(top, e3(src), AX, ALU.max))
                then(V.tensor_tensor(e3(key), e3(src), eb(top), ALU.is_equal))
                then(V.tensor_tensor(e3(key), e3(key), rank8, ALU.mult))
                then(V.tensor_reduce(k1, e3(key), AX, ALU.max))
                then(V.tensor_tensor(e3(onehot), rank8, eb(k1), ALU.is_equal))

            choose(wt, tw1, oh1)
            then(V.scalar_tensor_tensor(out=wt2, in0=oh1, scalar=-2.0, in1=wt, op0=ALU.mult, op1=ALU.add))
            choose(wt2, tw2, oh2)
            V.tensor_tensor(M, oh1, oh2, ALU.add).then_inc(S("M_ready"), 1)
            then(V.tensor_tensor(tws, tw1, tw2, ALU.add))
            then(V.tensor_scalar(tws, tws, EPS_GATE, None, ALU.add))
            then(V.reciprocal(zs, tws))
            then(V.tensor_tensor(tw1, tw1, zs, ALU.mult))
            then(V.tensor_tensor(tw2, tw2, zs, ALU.mult))
            then(V.memset(ones_r, 1.0))
            dve.wait_ge(S("rank_done"), 2)
            then(V.tensor_copy(t1r, ps[1][:, 0:UE]))
            for e in range(E):
                then(V.tensor_tensor_scan(e3(pre)[:, :, e], ones_r[:, 0:U], e3(t1r)[:, :, e], 0.0, ALU.mult, ALU.add))
            then(V.tensor_tensor(e3(cmp32.rearrange("p (e k) -> p (e k)", e=E)) if False else cmp32.rearrange("p (e k) -> p e k", e=E),
                                 e3(pre)[:, U - 1, :].unsqueeze(2).to_broadcast([P, E, 32]),
                                 CA["start_iota"].unsqueeze(1).to_broadcast([P, E, 32]), ALU.is_gt))
            then(V.tensor_reduce(nbk, cmp32.rearrange("p (e k) -> p e k", e=E), AX, ALU.add))
            then(V.tensor_tensor_scan(endb, ones_r[:, 0:E], nbk, 0.0, ALU.mult, ALU.add))
            then(V.tensor_tensor(startb, endb, nbk, ALU.subtract))
            then(V.tensor_scalar(startb, startb, float(P), None, ALU.mult))
            then(V.tensor_tensor(pre, pre, t1r, ALU.subtract))
            then(V.tensor_tensor(pos, pre, ps[0][:, 0:UE], ALU.add))
            then(V.tensor_tensor(e3(pos), e3(pos), startb.unsqueeze(1).to_broadcast([P, U, E]), ALU.add))
            then(V.tensor_tensor(t1r, pos, oh1, ALU.mult))
            then(V.tensor_tensor(t2r, pos, oh2, ALU.mult))
            then(V.tensor_reduce(posf[:, 0:U], e3(t1r), AX, ALU.add))
            then(V.tensor_reduce(posf[:, U:2 * U], e3(t2r), AX, ALU.add))
            i32 = lambda t: t.bitcast(I32)
            then(V.tensor_copy(i32(posi), posf))
            then(V.tensor_scalar(i32(blki), i32(posi), 7, None, ALU.logical_shift_right))
            then(V.tensor_scalar(i32(sli), i32(posi), P - 1, None, ALU.bitwise_and))
            then(V.tensor_copy(blkf, i32(blki)))
            then(V.tensor_copy(slf, i32(sli)))
            ebc3 = ebc.rearrange("p (i e) -> p i e", e=E)
            then(V.tensor_tensor(ebc3, endb.unsqueeze(1).to_broadcast([P, NB, E]), CA["block_iota"].unsqueeze(2).to_broadcast([P, NB, E]), ALU.is_le))
            then(V.tensor_reduce(ebf, ebc3, AX, ALU.add))
            then(V.tensor_scalar(ebf, ebf, float(E - 1), None, ALU.min))
            V.tensor_copy(i32(ebi), ebf).then_inc(S("eb_ready"), 1)

            def one_hots(i, m):
                wait(dve, S("inv_done"), i - 1)
                sl, bk = cols(slf, i, 1), cols(blkf, i, 1)
                V.tensor_scalar(oneS[m].bitcast(BF16)[:, 0:P], CA["slot_iota"], sl, None, ALU.is_equal)
                V.tensor_scalar(oneB[m].bitcast(BF16)[:, 0:NB], CA["block_iota"], bk, cols(CA["dest_hi"], i, 1), ALU.is_equal, ALU.mult)
                V.tensor_scalar(oneB[m].bitcast(BF16)[:, NB:2 * NB], CA["block_iota"], bk, CA["dest_lo"], ALU.is_equal, ALU.mult).then_inc(S("onehot_ready"), 1)

            one_hots(0, 0)
            one_hots(1, 1)
            with dve.Fori(1, U) as j:
                for m in range(2):
                    one_hots(j * 2 + m, m)
            dve.wait_ge(S("inv_done"), 2 * U)
            then(V.tensor_copy(inv, ps[2][:, 0:2 * NB]))
            then(V.scalar_tensor_tensor(out=inv[:, 0:NB], in0=inv[:, 0:NB], scalar=float(P), in1=inv[:, NB:2 * NB], op0=ALU.mult, op1=ALU.add))
            then(V.tensor_scalar(invz, inv[:, 0:NB], 0.0, float(PAD), ALU.is_equal, ALU.mult))
            then(V.tensor_scalar(inv[:, 0:NB], inv[:, 0:NB], 1.0, None, ALU.subtract))
            then(V.tensor_tensor(inv[:, 0:NB], inv[:, 0:NB], invz, ALU.add))
            V.tensor_copy(i32(dst_i), inv[:, 0:NB]).then_inc(S("inv_evac"), 1)
            dve.wait_ge(S("inv_evac"), 1)
            V.tensor_scalar(i32(src_i), i32(dst_i), ROWS - 1, None, ALU.bitwise_and).then_inc(S("inv_evac"), 1)
            dve.wait_ge(S("inv_evac"), 2)
            dve.wait_ge(S("w2_in"), 16 * 5)

            def read_index(i, j, m):
                wait(dve, S(f"gath{m}"), 16 * j)
                V.tensor_copy(i32(idg[m]), cols(i32(src_i), i, 1)).then_inc(S("idg_ready"), 1)

            def write_index(i, j, m4):
                wait(dve, S(f"y_stored{m4}"), 16 * j)
                V.tensor_copy(i32(idy[m4]), cols(i32(dst_i), i, 1))

            def expert(i):
                return dve.value_load(ebi[0:1, i:i + 1].bitcast(I32) if isinstance(i, int) else ebi[0:1, bass.ds(i, 1)].bitcast(I32), min_val=0, max_val=E - 1)

            def take_rows(i, m):
                dve.wait_ge(S("Tx_done"), i + 1)
                wait(dve, S("mm1_done"), i - 1)
                V.tensor_copy(xTe[m], ps[m][:, 0:P]).then_inc(S("xT_ready"), 1)

            def bias1(i, m, e):
                dve.wait_ge(S("mm1_done"), i + 1)
                wait(dve, S("gelu_ready"), i - 1)
                V.tensor_tensor(h1[m].rearrange("p (c t) -> p c t", c=FC), ps[2 + m][:, :].rearrange("p (c t) -> p c t", c=FC),
                                b1s[:, bass.ds(e * FC, FC)].unsqueeze(2).to_broadcast([P, FC, P]), ALU.add).then_inc(S("h1_ready"), 1)

            def bias2(i, m4, e):
                dve.wait_ge(S("mm2_done"), i + 1)
                V.tensor_tensor(ye[m4], ps[4 + m4 % 2][:, 0:P], b2s[:, bass.ds(e * P, P)], ALU.add).then_inc(S("y_ready"), 1)

            def dve_block(i, j, m, more=True):
                e1, e2 = expert(i - 1), expert(i - 2)
                take_rows(i, m % 2)
                bias1(i - 1, (m - 1) % 2, e1)
                if more: read_index(i + 3, j + (m + 3) // 4, (m + 3) % 4)
                write_index(i - 2, j - (m < 2), (m - 2) % 4)
                bias2(i - 2, (m - 2) % 4, e2)

            for i in range(4):
                read_index(i, 0, i)
            take_rows(0, 0)
            take_rows(1, 1)
            bias1(0, 0, expert(0))
            read_index(4, 1, 0)
            for i in range(2, 4):
                dve_block(i, 0, i)
            with dve.Fori(1, NB // 4 - 1) as j:
                for m in range(4):
                    dve_block(j * 4 + m, j, m)
            for m in range(4):
                dve_block(NB - 4 + m, NB // 4 - 1, m, more=m == 0)
            bias1(NB - 1, 1, expert(NB - 1))
            for i in range(NB - 2, NB):
                write_index(i, NB // 4 - 1, i % 4)
                bias2(i, i % 4, expert(i))

            dve.wait_ge(S("y1_in"), 16 * NT)
            dve.wait_ge(S("y2_in"), 16 * NT)
            with dve.Fori(0, NT) as n:
                y1, y2 = cols(Y1, n * W, W), cols(Y2, n * W, W)
                for b in range(B):
                    V.tensor_scalar(y1[:, b * P:(b + 1) * P], y1[:, b * P:(b + 1) * P], cols(tw1, n * B + b, 1), None, ALU.mult).then_inc(S("c1"), 1)
                dve.wait_ge(S("c1"), (n + 1) * B)
                for b in range(B):
                    V.scalar_tensor_tensor(out=y1[:, b * P:(b + 1) * P], in0=y2[:, b * P:(b + 1) * P], scalar=cols(tw2, n * B + b, 1),
                                           in1=y1[:, b * P:(b + 1) * P], op0=ALU.mult, op1=ALU.add).then_inc(S("c2"), 1)
            dve.wait_ge(S("c2"), U)
            with dve.Fori(0, NT) as n:
                for b in range(B):
                    V.bn_stats(st[:, bass.ds(n * B + b, 1)].rearrange("p a w -> p (a w)"), cols(Y1, (n * B + b) * P, P)).then_inc(S("bnC"), 1)
            dve.wait_ge(S("bnC"), U)
            then(V.tensor_tensor(ln[:, 0], st[:, :, 1], st[:, :, 4], ALU.add))
            then(V.tensor_tensor(ln[:, 1], st[:, :, 1], st[:, :, 4], ALU.subtract))
            then(V.tensor_tensor(ln[:, 2], st[:, :, 2], st[:, :, 5], ALU.add))
            then(V.tensor_tensor(ln[:, 3], ln[:, 1], ln[:, 1], ALU.mult))
            then(V.tensor_scalar(mean[:, :], ln[:, 0], 0.5, None, ALU.mult))
            V.scalar_tensor_tensor(out=ln[:, 4], in0=ln[:, 3], scalar=P / 4.0, in1=ln[:, 2], op0=ALU.mult, op1=ALU.add).then_inc(S("varC"), 1)
            dve.wait_ge(S("stdC"), 1)
            V.reciprocal(rstd[:, :], ln[:, 5]).then_inc(S("rstdC"), 1)
            dve.wait_ge(S("rstdC"), 1)
            dve.wait_ge(S("gb_ready"), 2)
            with dve.Fori(0, NT) as n:
                y1, x3 = cols(Y1, n * W, W), step_view(xs, n)
                for b in range(B):
                    V.tensor_scalar(y1[:, b * P:(b + 1) * P], y1[:, b * P:(b + 1) * P], cols(mean, n * B + b, 1), cols(rstd, n * B + b, 1),
                                    ALU.subtract, ALU.mult).then_inc(S("c3"), 1)
                V.tensor_tensor(x3, x3, GB[1], ALU.add).then_inc(S("c4"), 1)
                dve.wait_ge(S("c3"), (n + 1) * B)
                V.tensor_tensor(y1, y1, GB[0], ALU.mult).then_inc(S("c5"), 1)
                dve.wait_ge(S("c5"), n + 1)
                dve.wait_ge(S("c4"), n + 1)
                V.tensor_tensor(x3, x3, y1, ALU.add).then_inc(S("x3_ready"), 1)

        @block.gpsimd
        def _(pool):
            def squares(n, m):
                pool.wait_ge(S("kv_evac"), (n + 1) * B)
                wait(pool, S("kss_ready"), n - 1)
                src = kv[:, n, :, 0:P] if isinstance(n, int) else kv[:, bass.ds(n, 1), :, 0:P].rearrange("p a b w -> p (a b) w")
                nc.gpsimd.tensor_tensor(ksq[m].rearrange("p (b w) -> p b w", b=B), src, src, ALU.mult).then_inc(S("ksq_ready"), 1)
            squares(0, 0)
            squares(1, 1)
            with pool.Fori(1, NT // 2) as i:
                for m in range(2):
                    squares(i * 2 + m, m)

            def decay_rows(t, n, b):
                wait(pool, S("D_done"), t - 1)
                fcol = cols(zf, (n * B + b) * H, H).unsqueeze(2).to_broadcast([P, H, C])
                nc.gpsimd.tensor_tensor(R[b % 2].rearrange("p (h i) -> p h i", h=H), fcol,
                                        CA["causal"].unsqueeze(1).to_broadcast([P, H, C]), ALU.mult).then_inc(S("R_ready"), 1)

            def mask_decay(t, b):
                pool.wait_ge(S("E_ready"), t + 1)
                v = EM[b % 2].rearrange("p (h i) -> p h i", h=H)
                nc.gpsimd.tensor_tensor(v, v, CA["causal"].unsqueeze(1).to_broadcast([P, H, C]), ALU.mult).then_inc(S("EM_ready"), 1)

            def values(r, m):
                def by_head(t):
                    return cols(t, r * B * H, B * H).rearrange("p (b h) -> p b h", b=B).unsqueeze(3).to_broadcast([P, B, H, HD])
                wait(pool, S("U_done"), r - 1)
                nc.gpsimd.tensor_tensor(kd[m].rearrange("p (b h d) -> p b h d", b=B, h=H), kv_step(r, 0).rearrange("p b (h d) -> p b h d", h=H),
                                        by_head(eg), ALU.mult).then_inc(S("kd_ready"), 1)
                wait(pool, S("vx_ready"), r * B)
                nc.gpsimd.tensor_tensor(vp.rearrange("p (b h d) -> p b h d", b=B, h=H), kv_step(r, P).rearrange("p b (h d) -> p b h d", h=H),
                                        by_head(rk), ALU.mult).then_inc(S("vp_ready"), 1)
                pool.wait_ge(S("vp_ready"), r + 1)
                wait(pool, S("PV_done"), (r - 1) * B)
                for b in range(B):
                    nc.gpsimd.tensor_tensor(vx[m][:, b * W:(b + 1) * W].rearrange("p (g c w) -> p g c w", g=G, c=NC),
                                            vp[:, b * P:(b + 1) * P].rearrange("p (g w) -> p g w", g=G).unsqueeze(2).to_broadcast([P, G, NC, C]),
                                            CA["chunk_of"].unsqueeze(1).unsqueeze(3).to_broadcast([P, G, NC, C]), ALU.mult).then_inc(S("vx_ready"), 1)

            def inverse_std(q, k, tag):
                pool.wait_ge(S("var" + tag), q + 1)
                wait(pool, S("on_ready" if tag == "A" else "xn2_ready"), q)
                nc.gpsimd.tensor_tensor(lnb[k][:, 6 * B:7 * B], lnb[k][:, 4 * B:5 * B], epst[:, 1:2].to_broadcast([P, B]), ALU.pow).then_inc(S("rstd" + tag), 1)

            def gate(q):
                pool.wait_ge(S("o2_ready"), q + 1)
                nc.gpsimd.tensor_tensor(o3.rearrange("p (b w) -> p b w", b=B), o2.rearrange("p (b w) -> p b w", b=B), gate_step(q),
                                        ALU.mult).then_inc(S("o3_ready"), 1)

            def modulate2(q):
                pool.wait_ge(S("xn2_ready"), q + 1)
                nc.gpsimd.tensor_tensor(h2t, xn2, mod[:, 2].rearrange("p b w -> p (b w)"), ALU.mult).then_inc(S("h2a_ready"), 1)
                pool.wait_ge(S("h2a_ready"), q + 1)
                wait(pool, S("T2_done"), q)
                wait(pool, S("h2_stored"), 16 * q)
                nc.gpsimd.tensor_tensor(h2, h2t, mod[:, 1].rearrange("p b w -> p (b w)"), ALU.add).then_inc(S("h2_ready"), 1)

            def pool_step(n, m, A=True, Bt=True, more=True):
                t = n * B
                mask_decay(t + 1, 1)
                decay_rows(t + 2, n, 2)
                if Bt: inverse_std(n - 2, 1, "B")
                if A: gate(n - 1)
                mask_decay(t + 2, 2)
                decay_rows(t + 3, n, 3)
                if A: inverse_std(n - 1, 0, "A")
                mask_decay(t + 3, 3)
                if Bt: modulate2(n - 2)
                if more:
                    decay_rows(t + 4, n + 1, 0)
                    values(n + 1, 1 - m)
                    mask_decay(t + 4, 0)
                    decay_rows(t + 5, n + 1, 1)

            pool.wait_ge(S("f_ready"), 1)
            decay_rows(0, 0, 0)
            decay_rows(1, 0, 1)
            pool.wait_ge(S("rk_ready"), 1)
            pool.wait_ge(S("eg_ready"), 1)
            values(0, 0)
            mask_decay(0, 0)
            pool.wait_ge(S("gate_ready"), 1)
            pool.wait_ge(S("modfix3"), 2)
            pool.wait_ge(S("eps_ready"), 3)
            pool_step(0, 0, A=False, Bt=False)
            pool_step(1, 1, Bt=False)
            pool_step(2, 0)
            with pool.Fori(1, NT // 2 - 1) as i:
                for m in range(2):
                    pool_step(i * 2 + 1 + m, 1 - m)
            pool_step(NT - 1, 1, more=False)
            gate(NT - 1)
            inverse_std(NT - 1, 0, "A")
            inverse_std(NT - 2, 1, "B")
            modulate2(NT - 2)
            inverse_std(NT - 1, 1, "B")
            modulate2(NT - 1)

            pool.wait_ge(S("w2_in"), 16 * 5)
            pool.wait_ge(S("logits_ready"), NT)
            for j in range(2):
                nc.gpsimd.tensor_tensor(GB[j].rearrange("p (b w) -> p b w", b=B), mod[:, 3], gam[:, j].unsqueeze(1).to_broadcast([P, B, P]),
                                        ALU.mult).then_inc(S("gb_ready"), 1)
            pool.wait_ge(S("h2_stored"), 16 * NT)

            bound = pool.alloc_register("bound")
            pool.reg_mov(bound, 2 * ROWS - 1)

            def gather(i, m):
                pool.wait_ge(S("idg_ready"), i + 1)
                wait(pool, S("Tx_done"), i - 3)
                pool.reg_alu(bound, bound, 1, op=ALU.bitwise_or)
                nc.gpsimd.indirect_dma_start(xg[m], None, h2_rows, bass.IndirectOffsetOnAxis(ap=idg[m].bitcast(I32), axis=0),
                                             bounds_check=bound, oob_is_err=False).then_inc(S(f"gath{m}"), 16)

            def scatter(i, m):
                pool.wait_ge(S("y_ready"), i + 1)
                pool.reg_alu(bound, bound, 1, op=ALU.bitwise_or)
                nc.gpsimd.indirect_dma_start(y_rows, bass.IndirectOffsetOnAxis(ap=idy[m].bitcast(I32), axis=0), ye[m], None,
                                             bounds_check=bound, oob_is_err=False).then_inc(S(f"y_stored{m}"), 16)

            def pool_block(i, m, more=True):
                if more: gather(i + 3, (m + 3) % 4)
                scatter(i - 2, (m - 2) % 4)

            for i in range(5):
                gather(i, i % 4)
            for i in range(2, 4):
                pool_block(i, i)
            with pool.Fori(1, NB // 4 - 1) as j:
                for m in range(4):
                    pool_block(j * 4 + m, m)
            for m in range(4):
                pool_block(NB - 4 + m, m, more=m == 0)
            for i in range(NB - 2, NB):
                scatter(i, i % 4)


def constants(np):
    p = np.arange(P)[:, None]
    q = np.arange(P)[None, :]
    t = {
        "ident": p == q,
        "later": (p // C == q // C) & (p > q),
        "upto": (p // C == q // C) & (p <= q),
        "before": p < q,
        "ones": np.ones((P, P)),
        "headsel": p == q // HD,
        "slot_iota": q + 0 * p,
        "block_iota": np.arange(NB)[None, :] + 0 * p,
        "causal": p % C <= np.arange(C)[None, :],
        "blockmask": (p % C) // HD == np.arange(C)[None, :] // HD,
        "start_iota": P * np.arange(32)[None, :] + 0 * p,
        "dest_hi": np.array([[k * U + (u % B) * NT + u // B for k in range(2) for u in range(U)]]) + 0 * p,
        "chunk_of": p // C == np.arange(NC)[None, :],
        "head_of": (p % C) // HD == np.arange(HG)[None, :],
        "rank8": E - np.arange(E)[None, :] + 0 * p,
        "dest_lo": p + 1,
    }
    return np.concatenate([np.asarray(t[n], np.float32) for n, _ in CONST_WIDTHS], axis=1)


def kernel(**inputs):
    import numpy as np
    import concourse.bacc as bacc
    from concourse import mybir as mb
    from concourse.bass_utils import run_bass_kernel_spmd

    a = {k: np.asarray(v) for k, v in inputs.items()}
    arrays = {
        "x": a["L0_attn_x"], "wq_t": a["L0_attn_Wq"].T, "wk_t": a["L0_attn_Wk"].T,
        "wkv_t": np.concatenate([a["L0_attn_Wk"].T, a["L0_attn_Wv"].T], axis=1), "wf_t": a["L0_attn_Wf"].T,
        "wg1": a["L0_attn_Wg1"], "wg2_t": a["L0_attn_Wg2"].T, "lnw": a["L0_attn_ln_w"].reshape(D, 1),
        "wo_t": a["L0_attn_Wo"].T, "wg": a["L0_ffn_Wg"], "bg": a["L0_ffn_bg"], "w1": a["L0_ffn_W1"],
        "b1_t": a["L0_ffn_b1"].reshape(E, FC, P).transpose(2, 0, 1), "w2": a["L0_ffn_W2"], "b2": a["L0_ffn_b2"], "gamma": a["L0_ffn_gamma"],
        "beta": a["L0_ffn_beta"], "c_t": a["L0_c"].T, "wmod": a["L0_wmod"], "consts": constants(np),
    }
    arrays = {f"in_{k}": np.ascontiguousarray(v) for k, v in arrays.items()}
    nc = bacc.Bacc("TRN2", target_bir_lowering=False, num_devices=1)
    args = [nc.dram_tensor(k, v.shape, mb.dt.from_np(v.dtype), kind="ExternalInput").ap() for k, v in arrays.items()]
    args.append(nc.dram_tensor("out_x", (B, N, D), F32, kind="ExternalOutput").ap())
    build(nc, *args)
    r = run_bass_kernel_spmd(nc, [arrays], core_ids=[0])
    return r.results[0]["out_x"]
```

```python
from contextlib import ExitStack

import concourse.bass as bass
from concourse import mybir

F32 = mybir.dt.float32
BF16 = mybir.dt.bfloat16
I32 = mybir.dt.int32
ALU = mybir.AluOpType
ACT = mybir.ActivationFunctionType
AX = mybir.AxisListType.X

P = 128
B, N, D = 4, 1024, 128
H, HD = 16, 8
E, F = 8, 512
NT = N // P
U = NT * B
W = B * P
C = 32
NC = P // C
G = 4
HG = H // G
FC = F // P
TOK = 3 * P + H
NB = 2 * B * N // P + E
LOG_ZERO = -30000.0
EPS_LN, EPS_GATE, EPS_NORM = 1e-5, 1e-8, 1e-12
PAD = 1 << 20
ROWS = B * N
EW = F + FC + D

CONST_WIDTHS = [("ident", P), ("later", P), ("upto", P), ("before", P), ("ones", P), ("headsel", P),
                ("slot_iota", P), ("block_iota", NB), ("causal", C), ("blockmask", C), ("start_iota", 32),
                ("dest", 2 * U), ("chunk_of", NC), ("head_of", HG), ("rank8", E)]
CONST_AT, _at = {}, 0
for _name, _w in CONST_WIDTHS:
    CONST_AT[_name] = (_at, _w)
    _at += _w
CONST_N = _at


def wait(eng, sem, value):
    if not (isinstance(value, int) and value <= 0):
        eng.wait_ge(sem, value)


def build(nc, x, wq_t, wk_t, wkv_t, wf_t, wg1, wg2_t, lnw, wo_t, wg, bg, w1, b1_t, w2, b2, gamma, beta, c_t, wmod,
          consts, out):
    ctx = ExitStack()
    with ctx:
        def sb(name, shape, dt=F32):
            return ctx.enter_context(nc.sbuf_tensor(name, shape, dt))

        def psum(name, shape, dt=F32):
            return ctx.enter_context(nc.psum_tensor(name, shape, dt))

        def sem(name):
            return ctx.enter_context(nc.semaphore(name))

        h2_rows = nc.dram_tensor("h2_rows", (ROWS, D), F32, kind="Internal").ap()
        y_rows = nc.dram_tensor("y_rows", (2 * ROWS, D), F32, kind="Internal").ap()

        xs = sb("xs", [P, NT, W])
        ct = sb("ct", [P, CONST_N])
        qT = sb("qT", [P, NT, W])
        kT = sb("kT", [P, NT, W])
        kv = sb("kv", [P, NT, B, 2 * P])
        gz = sb("gz", [P, NT, B, P + H])
        wqs = sb("wqs", [P, P])
        wks = sb("wks", [P, P])
        wtok = sb("wtok", [P, TOK])
        wos = sb("wos", [P, P])
        wog = sb("wog", [P, B, P])
        lnws = sb("lnws", [P, 1])
        wgs = sb("wgs", [P, E])
        bgs = sb("bgs", [P, E])
        wg1s = sb("wg1s", [HD, D])
        wg2s = sb("wg2s", [HD, D])
        cs = sb("cs", [P, B])
        csil = sb("csil", [P, B])
        modT = sb("modT", [P, 2, B])
        mod = sb("mod", [P, 4, B, P])
        gam = sb("gam", [P, 2, P])
        epst = sb("epst", [P, 2])
        onebf = sb("onebf", [P, C], BF16)
        far = sb("far", [C, P], BF16)
        acausal = sb("acausal", [C, W], BF16)

        st = sb("st", [P, U, 6])
        ln = sb("ln", [P, 8, U])
        mean = sb("mean", [P, U])
        rstd = sb("rstd", [P, U])
        zf = sb("zf", [P, U * H])
        rk = sb("rk", [P, U * H])
        eg = sb("eg", [P, U * H])
        ef = sb("ef", [P, U * H])
        tc = sb("tc", [H, U * NC])
        td = sb("td", [P, U * NC])

        WORK = 38 * W
        work = sb("work", [P, WORK])

        def ws(at, n):
            return work[:, at:at + n]

        xn = [ws(m * W, W) for m in range(2)]
        hT = [ws((2 + m) * W, W) for m in range(2)]
        ksq = [ws((4 + m) * W, W) for m in range(2)]

        wmods = ws(8 * W, 6 * D)
        cbc = ws(10 * W, B * P).rearrange("p (b w) -> p b w", b=B)

        cur = [0]

        def take(n):
            cur[0] += n
            return ws(cur[0] - n, n)

        Qx = take(HG * W)
        kTs, qTs, kd = ([take(W), take(W)] for _ in range(3))
        vx = [take(B * W), take(B * W)]
        vp = take(W)
        R, EM, PR = ([take(W), take(W)] for _ in range(3))
        Um = take(W)
        Sb = [take(W), take(W)]
        stmp = take(B * C)
        om, osum, ot = (take(W) for _ in range(3))
        o1, o2, onT, xn2, h2 = (take(W) for _ in range(5))
        o3, on, h2t, h2T = o2, o2, xn2, onT
        za = o1
        lg = ws(WORK - U * E, U * E)
        stb = [take(B * 6) for _ in range(2)]
        lnb = [take(8 * B) for _ in range(2)]
        assert cur[0] <= WORK - U * E, cur[0]

        UE = U * E
        base = 0

        def at(n):
            nonlocal base
            base += n
            return ws(base - n, n)

        lgx, wt, key, oh1, oh2, wt2, M, rank, pre, pos, t1r, t2r, ones_r = (at(UE) for _ in range(13))
        mx, zs, m1, m2, k1, tw1, tw2, tws, p1, p2 = (at(U) for _ in range(10))
        tot8, nbk, endb, startb, endv = (at(E) for _ in range(5))
        cmp32 = at(E * 32)
        posf = at(2 * U)
        posi, blki, sli = (at(2 * U) for _ in range(3))
        blkf, slf = at(2 * U), at(2 * U)
        ebc = at(NB * E)
        ebf = at(NB)
        ebi = at(NB)
        inv = at(NB)
        invz = at(NB)
        dst_i = at(NB)
        src_i = at(NB)
        oneS = [at(4 * P) for _ in range(2)]
        oneB = [at(4 * NB) for _ in range(2)]
        xg, ye = ([at(P) for _ in range(4)] for _ in range(2))
        xTe = [at(P), at(P)]
        h1, ge = ([at(F), at(F)] for _ in range(2))
        gz_flat = gz[:, :, :, :].rearrange("p n b w -> p (n b w)")
        w1e = [gz_flat[:, k * EW:(k + 1) * EW] for k in range(4)]
        slot_gap = [gz_flat[:, 4 * EW + k * 4 * P:4 * EW + (k + 1) * 4 * P] for k in range(2)]
        ysum = h1 + ge
        idg = [at(1) for _ in range(4)]
        idy = [at(1) for _ in range(4)]
        wtab = at(E * EW)
        stb.append(at(B * 6)), stb.append(at(B * 6))
        lnb.append(at(8 * B)), lnb.append(at(8 * B))
        GB = [at(W) for _ in range(2)]
        assert base <= WORK - U * E, base
        w2s = kv[:, NT // 2:NT].rearrange("p n b w -> p (n b w)")
        Y1 = kT[:, :, :].rearrange("p n w -> p (n w)")
        Y2 = qT[:, :, :].rearrange("p n w -> p (n w)")
        lgr = lg

        def o1v(j):
            return (xn2, onT, h2)[j].rearrange("p (b w) -> p b w", b=B)

        def DBG(n):
            return xs[:, n].rearrange("p (b d) -> p b d", b=B)

        CA = {k: ct[:, a:a + n] for k, (a, n) in CONST_AT.items()}
        ident = CA["ident"]

        ps4x = psum("ps4x", [P, 4, 512])
        ps = [psum(f"ps{i}", [P, 512]) for i in range(4)] + [ps4x[:, i] for i in range(4)]

        names = """x_lo x_hi w_in w1_in c_in mod_bc mod_done mod_evac modt_done modt_evac csil_ready cbc_ready wgate_done wgate_evac
            eps_ready st_ready lnw1 lnw2 var_ready std_ready rstd_ready
            xn_ready xT_done hT_ready q_done q_evac k_done k_evac tok_done kv_evac gz_evac ksq_ready kss_ready
            gate_ready kss_cl lnk_ready rk_ready za_ready ez_ready lz_ready f_ready g_done f_done eg_ready ef_ready tc_done tc_evac
            te_done td_ready modfix S_zero
            U_done PV_done D_done A_done inter_done T1_done Wo_done T2_done router_done
            Um_ready S_mul S_step P_ready o1_ready o2_ready on_ready x2_ready xn2_ready logits_ready stage_ready
            bnA sumA sqA varA lnA_ready rstdA bnB sumB sqB varB lnB_ready rstdB
            om_ready osum_ready ot_ready kd_ready vx_ready E_ready Qx_ready onT_ready h2T_ready R_ready far_ready vp_ready vpp_ready o3_ready h2a_ready h2_ready h2_stored modfix2 modfix3
            w2_in y_stored0 y_stored1 y_stored2 y_stored3 y_in0 y_in1 y_in2 y_in3 gam_in x3_ready out_stored
            r1 slots_ready lx_ready le_ready M_ready rank_done gap_ready gap2_ready oneS_ready oneB_ready inv_done inv_evac eb_ready idg_ready
            gath0 gath1 gath2 gath3 w1e_ready Tx_done xT_ready mm1_done h1_ready gelu_ready TG_done gT_ready mm2_done y_ready
            gb_ready c1 c2 c3 bnC sumC sqC varC stdC rstdC c4 c5 c6 wog_ready dbg_out""".split()
        s = {n: sem(n) for n in names}

        def S(n):
            return s[n]

        block = ctx.enter_context(nc.Block())

        def cols(t, start, n):
            return t[:, start:start + n] if isinstance(start, int) else t[:, bass.ds(start, n)]

        def kv_step(n, lo):
            if isinstance(n, int):
                return kv[:, n, :, lo:lo + P]
            return kv[:, bass.ds(n, 1), :, lo:lo + P].rearrange("p a b w -> p (a b) w")

        def gate_step(n):
            if isinstance(n, int):
                return gz[:, n, :, 0:P]
            return gz[:, bass.ds(n, 1), :, 0:P].rearrange("p a b w -> p (a b) w")

        scaled = {"A": "on_ready", "B": "xn2_ready", "C": "c3"}
        lag = {"A": 0, "B": 0, "C": 1}

        rowbank = ps4x

        x_v = x.rearrange("b (n p) d -> n p b d", p=P)

        def step_view(t, n):
            return t[:, bass.ds(n, 1)].rearrange("p a w -> p (a w)") if not isinstance(n, int) else t[:, n]

        @block.sync
        def _(sp):
            for n in range(NT):
                sp.dma_start(xs[:, n].rearrange("p (b d) -> p b d", b=B), x_v[n]).then_inc(S("x_lo" if n < NT // 2 else "x_hi"), 16)

            h2_v = h2_rows.rearrange("(b n p) d -> n p b d", b=B, p=P)

            def store_h2(q):
                sp.wait_ge(S("h2_ready"), q + 1)
                dst = h2_v[q] if isinstance(q, int) else h2_v[bass.ds(q, 1)].rearrange("a p b d -> (a p) b d")
                sp.dma_start(dst, h2.rearrange("p (b d) -> p b d", b=B)).then_inc(S("h2_stored"), 16)

            with sp.Fori(0, NT) as q:
                store_h2(q)

            sp.wait_ge(S("stage_ready"), NT)
            sp.wait_ge(S("vx_ready"), U)
            sp.dma_start(gam[:, 0], gamma.partition_broadcast(P)).then_inc(S("gam_in"), 16)
            sp.dma_start(gam[:, 1], beta.partition_broadcast(P)).then_inc(S("gam_in"), 16)
            sp.dma_start(w2s.rearrange("p (e c d) -> p e c d", e=E, c=FC), w2.rearrange("e (c p) d -> p e c d", p=P)).then_inc(S("w2_in"), 16)
            sp.wait_ge(S("logits_ready"), NT)
            sp.wait_ge(S("h2_stored"), 16 * NT)
            table = wtab.rearrange("p (e w) -> p e w", e=E)
            sp.dma_start(table[:, :, 0:F], w1.rearrange("e d f -> d e f")).then_inc(S("w1_in"), 16)
            sp.dma_start(table[:, :, F:F + FC], b1_t).then_inc(S("w1_in"), 16)
            sp.dma_start(table[:, :, F + FC:EW], b2.partition_broadcast(P)).then_inc(S("w1_in"), 16)

            for m in range(4):
                sp.wait_ge(S(f"y_stored{m}"), 16 * (NB // 4))
            y_v = y_rows.rearrange("(k b n p) d -> k p n b d", k=2, b=B, p=P)
            for n in range(NT):
                m = n % 4
                wait(sp, S(f"y_in{m}"), 32 * (n // 4))
                for k, dst in enumerate((Y1, Y2)):
                    sp.dma_start(dst[:, n * W:(n + 1) * W].rearrange("p (b d) -> p b d", b=B), y_v[k, :, n]).then_inc(S(f"y_in{m}"), 16)
            out_v = out.rearrange("b (n p) d -> n p b d", p=P)
            with sp.Fori(0, NT) as n:
                sp.wait_ge(S("x3_ready"), n + 1)
                sp.dma_start(out_v[bass.ds(n, 1)].rearrange("a p b d -> (a p) b d"), step_view(xs, n).rearrange("p (b d) -> p b d", b=B)).then_inc(S("out_stored"), 16)
            sp.wait_ge(S("out_stored"), 16 * NT)

        W_LOADS = 11

        @block.scalar
        def _(act):
            act.dma_start(cs[:, :], c_t).then_inc(S("c_in"), 16)
            act.dma_start(wmods[:, :], wmod).then_inc(S("c_in"), 16)
            for dst, src in ((ct[:, :], consts), (wqs[:, :], wq_t), (wks[:, :], wk_t), (wtok[:, 0:2 * P], wkv_t),
                             (wtok[:, 3 * P:TOK], wf_t), (wg1s[:, :], wg1), (wg2s[:, :], wg2_t), (wos[:, :], wo_t),
                             (lnws[:, :], lnw), (wgs[:, :], wg), (bgs[:, :], bg.partition_broadcast(P))):
                act.dma_start(dst, src).then_inc(S("w_in"), 16)
            act.wait_ge(S("c_in"), 32)
            nc.scalar.activation(csil[:, :], cs[:, :], ACT.Silu).then_inc(S("csil_ready"), 1)
            act.wait_ge(S("mod_done"), 1)
            for b in range(B):
                last = nc.scalar.activation(mod[:, :, b], ps[4 + b][:, :].rearrange("p (j d) -> p j d", j=4), ACT.Copy)
            last.then_inc(S("mod_evac"), 1)
            act.wait_ge(S("eps_ready"), 1)
            act.wait_ge(S("var_ready"), 1)
            nc.scalar.activation(ln[:, 5], ln[:, 4], ACT.Sqrt, bias=epst[:, 0:1], scale=1.0 / P).then_inc(S("std_ready"), 1)

            def a_step(n):
                act.wait_ge(S("q_done"), n + 1)
                nc.scalar.activation(step_view(qT, n), ps[2][:, :], ACT.Silu).then_inc(S("q_evac"), 1)
                act.wait_ge(S("k_done"), n + 1)
                nc.scalar.activation(step_view(kT, n), ps[3][:, :], ACT.Silu).then_inc(S("k_evac"), 1)
                for b in range(B):
                    act.wait_ge(S("tok_done"), n * B + b + 1)
                    dst = kv[:, bass.ds(n, 1), b].rearrange("p a w -> p (a w)") if not isinstance(n, int) else kv[:, n, b]
                    nc.scalar.activation(dst, ps[4 + b][:, 0:2 * P], ACT.Silu).then_inc(S("kv_evac"), 1)
            for n in range(2):
                a_step(n)
            with act.Fori(1, NT // 2) as i:
                for m in range(2):
                    a_step(i * 2 + m)

            act.wait_ge(S("za_ready"), 1)
            nc.scalar.activation(za, za, ACT.Exp, scale=-1.0).then_inc(S("ez_ready"), 1)
            act.wait_ge(S("ez_ready"), 1)
            nc.scalar.activation(za, za, ACT.Ln, bias=1.0).then_inc(S("lz_ready"), 1)
            act.wait_ge(S("kss_cl"), 1)
            nc.scalar.activation(rk[:, :], rk[:, :], ACT.Ln).then_inc(S("lnk_ready"), 1)
            act.wait_ge(S("lnk_ready"), 1)
            nc.scalar.activation(rk[:, :], rk[:, :], ACT.Exp, scale=-0.5).then_inc(S("rk_ready"), 1)
            act.wait_ge(S("g_done"), 1)
            nc.scalar.activation(eg[:, :], ps[0][:, :], ACT.Exp).then_inc(S("eg_ready"), 1)
            act.wait_ge(S("f_done"), 1)
            for b in range(B):
                last = nc.scalar.activation(ef[:, :].rearrange("p (n g b s) -> p b n g s", n=NT, g=G, b=B)[:, b],
                                            ps[1][:, :].rearrange("p (n b g s) -> p b n g s", n=NT, g=G, b=B)[:, b], ACT.Exp)
            last.then_inc(S("ef_ready"), 1)
            def decay(t, b):
                act.wait_ge(S("D_done"), t + 1)
                wait(act, S("P_ready"), t - 1)
                nc.scalar.activation(EM[b % 2], ps[b % 2][:, :], ACT.Exp).then_inc(S("E_ready"), 1)

            def spread_q(n):
                wait(act, S("A_done"), n * B)
                for h in range(HG):
                    last = nc.scalar.activation(Qx[:, h * W:(h + 1) * W], step_view(qT, n), ACT.Copy, scale=CA["head_of"][:, h:h + 1])
                last.then_inc(S("Qx_ready"), 1)

            def evacuate_on(q):
                act.wait_ge(S("T1_done"), q + 1)
                wait(act, S("router_done"), q - 1)
                nc.scalar.activation(onT, ps[2][:, :], ACT.Copy).then_inc(S("onT_ready"), 1)

            def evacuate_h2(q):
                act.wait_ge(S("T2_done"), q + 1)
                act.wait_ge(S("Wo_done"), min(q + 2, NT) if isinstance(q, int) else q + 2)
                if isinstance(q, int) and q > NT - 3:
                    act.wait_ge(S("router_done"), q)
                nc.scalar.activation(h2T, ps[2][:, :], ACT.Copy).then_inc(S("h2T_ready"), 1)

            def spread_values(r, m, cs):
                act.wait_ge(S("vp_ready"), r + 1)
                wait(act, S("PV_done"), (r - 1) * B)
                for c in cs:
                    nc.scalar.activation(vx[m].rearrange("p (bg c w) -> p bg c w", c=NC, w=C)[:, :, c], vp.rearrange("p (bg w) -> p bg w", w=C),
                                         ACT.Copy, scale=CA["chunk_of"][:, c:c + 1]).then_inc(S("vx_ready"), 1)

            def own_values(t):
                act.wait_ge(S("PV_done"), t + 1)
                wait(act, S("osum_ready"), t)
                src, dst = (v.rearrange("p (g s i) -> p g s i", g=G, s=HG) for v in (ps[3][:, :], om))
                for h in range(HG):
                    last = nc.scalar.activation(dst[:, :, h], src[:, :, h], ACT.Copy, scale=CA["head_of"][:, h:h + 1])
                last.then_inc(S("om_ready"), 1)

            def act_step(n, m, A=True, Ct=True, more=True):
                t = n * B
                decay(t + 1, 1)
                if A: own_values(t - 1)
                if Ct: evacuate_h2(n - 3)
                if more: spread_values(n + 1, 1 - m, range(0, 2))
                decay(t + 2, 2)
                if more: spread_values(n + 1, 1 - m, range(2, NC))
                own_values(t)
                decay(t + 3, 3)
                own_values(t + 1)
                if more: decay(t + 4, 0)
                own_values(t + 2)
                if A: evacuate_on(n - 1)
                if more: spread_q(n + 1)

            act.wait_ge(S("w_in"), 16 * W_LOADS)
            act.wait_ge(S("q_evac"), NT)
            spread_q(0)
            act.wait_ge(S("te_done"), 1)
            nc.scalar.activation(td[:, :], ps[3][:, 0:U * NC], ACT.Exp).then_inc(S("td_ready"), 1)
            spread_values(0, 0, range(NC))
            decay(0, 0)
            act_step(0, 0, A=False, Ct=False)
            act.wait_ge(S("gz_evac"), U)
            for j in range(4):
                v = gz[:, 2 * j:2 * j + 2, :, 0:P].rearrange("p a b w -> p (a b) w")
                last = nc.scalar.activation(v, v, ACT.Sigmoid)
            last.then_inc(S("gate_ready"), 1)
            act_step(1, 1, Ct=False)
            act_step(2, 0, Ct=False)
            with act.Fori(1, NT // 2 - 1) as i:
                for m in range(2):
                    act_step(i * 2 + 1 + m, 1 - m)
            act_step(NT - 1, 1, more=False)
            own_values(U - 1)
            evacuate_h2(NT - 3)
            evacuate_on(NT - 1)
            evacuate_h2(NT - 2)
            evacuate_h2(NT - 1)

            act.wait_ge(S("lx_ready"), 1)
            nc.scalar.activation(wt, lgx, ACT.Exp).then_inc(S("le_ready"), 1)

            def slot_hots(i, m):
                act.wait_ge(S("gap_ready"), i + 1)
                wait(act, S("inv_done"), i - 1)
                nc.scalar.activation(oneS[m], slot_gap[m], ACT.Square).then_inc(S("gap2_ready"), 1)
                act.wait_ge(S("gap2_ready"), i + 1)
                nc.scalar.activation(oneS[m], oneS[m], ACT.Relu, bias=1.0, scale=-1.0).then_inc(S("oneS_ready"), 1)

            slot_hots(0, 0)
            slot_hots(1, 1)
            with act.Fori(1, U // 4) as j:
                for m in range(2):
                    slot_hots(j * 2 + m, m)

            act.wait_ge(S("eb_ready"), 1)
            act.wait_ge(S("w1_in"), 16 * 3)

            def expert(i):
                return act.value_load(ebi[0:1, i:i + 1].bitcast(I32) if isinstance(i, int) else ebi[0:1, bass.ds(i, 1)].bitcast(I32), min_val=0, max_val=E - 1)

            def take_expert(i, m):
                e = expert(i)
                wait(act, S("y_ready"), i - 3)
                nc.scalar.activation(w1e[m], wtab[:, bass.ds(e * EW, EW)], ACT.Copy).then_inc(S("w1e_ready"), 1)

            def gelu(i, m):
                act.wait_ge(S("h1_ready"), i + 1)
                wait(act, S("mm2_done"), i - 1)
                nc.scalar.activation(ge[m], h1[m], ACT.Gelu).then_inc(S("gelu_ready"), 1)

            take_expert(0, 0)
            take_expert(1, 1)
            gelu(0, 0)
            for i in range(2, 4):
                take_expert(i, i)
                gelu(i - 1, (i - 1) % 2)
            with act.Fori(1, NB // 4) as j:
                for m in range(4):
                    take_expert(j * 4 + m, m)
                    gelu(j * 4 + m - 1, (m - 1) % 2)
            gelu(NB - 1, 1)

            def share(n, j, m):
                act.wait_ge(S(f"y_in{m}"), 32 * (j + 1))
                wait(act, S("x3_ready"), n - 3)
                for b in range(B):
                    last = nc.scalar.activation(ysum[m][:, b * P:(b + 1) * P], cols(Y1, (n * B + b) * P, P), ACT.Copy, scale=cols(tw1, n * B + b, 1))
                last.then_inc(S("c1"), 1)

            for n in range(4):
                share(n, 0, n)
            with act.Fori(1, NT // 4) as j:
                for m in range(4):
                    share(j * 4 + m, j, m)

        @block.tensor
        def _(pe):
            pe.wait_ge(S("c_in"), 32)
            pe.wait_ge(S("csil_ready"), 1)
            for i in range(2):
                last = nc.tensor.matmul(ps[0][:, 4 * i:4 * i + 4], wmods[:, i * D:(i + 1) * D], csil[:, :], start=True, stop=True)
            last.then_inc(S("modt_done"), 1)
            pe.wait_ge(S("w_in"), 16 * W_LOADS)
            nc.tensor.matmul(ps[1][:, 0:P], wg1s[:, :], wg2s[:, :], start=True, stop=True).then_inc(S("wgate_done"), 1)
            pe.wait_ge(S("cbc_ready"), 1)
            for b in range(B):
                last = nc.tensor.matmul(ps[4 + b][:, :], cbc[:, b], wmods[:, 2 * D:6 * D], start=True, stop=True)
            last.then_inc(S("mod_done"), 1)

            def transposes(n, m):
                wait(pe, S("xn_ready"), n * B + B)
                wait(pe, S("hT_ready"), (n - 1) * B)
                for b in range(B):
                    last = nc.tensor.transpose(ps[m][:, b * P:(b + 1) * P], xn[m][:, b * P:(b + 1) * P], ident)
                last.then_inc(S("xT_done"), 1)

            def projections(n, m):
                wait(pe, S("hT_ready"), (n + 1) * B)
                wait(pe, S("q_evac"), n)
                nc.tensor.matmul(ps[2][:, :], wqs[:, :], hT[m], start=True, stop=True).then_inc(S("q_done"), 1)
                wait(pe, S("k_evac"), n)
                nc.tensor.matmul(ps[3][:, :], wks[:, :], hT[m], start=True, stop=True).then_inc(S("k_done"), 1)
                for b in range(B):
                    wait(pe, S("kv_evac"), (n - 1) * B + b + 1)
                    wait(pe, S("gz_evac"), (n - 1) * B + b + 1)
                    nc.tensor.matmul(ps[4 + b][:, 0:TOK], hT[m][:, b * P:(b + 1) * P], wtok[:, :], start=True, stop=True).then_inc(S("tok_done"), 1)

            pe.wait_ge(S("modt_evac"), 1)
            pe.wait_ge(S("wgate_evac"), 1)
            transposes(0, 0)
            transposes(1, 1)
            pe.wait_ge(S("mod_evac"), 1)
            projections(0, 0)
            with pe.Fori(1, NT // 2) as i:
                for m in range(2):
                    n = i * 2 + m
                    transposes(n, m)
                    projections(n - 1, 1 - m)
            projections(NT - 1, 1)

            pe.wait_ge(S("f_ready"), 1)
            pe.wait_ge(S("gz_evac"), U)
            pe.wait_ge(S("k_evac"), NT)
            nc.tensor.matmul(ps[0][:, :], CA["later"], zf[:, :], start=True, stop=True).then_inc(S("g_done"), 1)
            nc.tensor.matmul(ps[1][:, :], CA["upto"], zf[:, :], start=True, stop=True).then_inc(S("f_done"), 1)
            for u in range(U):
                last = nc.tensor.matmul(ps[2][0:H, u * NC:(u + 1) * NC], zf[:, u * H:(u + 1) * H], CA["chunk_of"], start=True, stop=True)
            last.then_inc(S("tc_done"), 1)
            pe.wait_ge(S("tc_evac"), 1)
            nc.tensor.matmul(ps[3][:, 0:U * NC], CA["headsel"][0:H, :], tc[:, :], start=True, stop=True).then_inc(S("te_done"), 1)

            def open_group(dst):
                nc.tensor.matmul(dst, onebf[:, :], onebf[:, 0:1], start=True, stop=True)

            def state_updates(n, m):
                pe.wait_ge(S("kd_ready"), n + 1)
                pe.wait_ge(S("vx_ready"), (n + 1) * B)
                wait(pe, S("o1_ready"), n)
                for b in range(B):
                    for g in range(G):
                        at = b * P + g * C
                        last = nc.tensor.matmul(rowbank[g * C:(g + 1) * C, 0, b * P:(b + 1) * P], kd[m][:, at:at + C],
                                                vx[m][:, b * W + g * P:b * W + (g + 1) * P], start=True, stop=True)
                last.then_inc(S("U_done"), 1)

            def log_decay(t, b):
                pe.wait_ge(S("R_ready"), t + 1)
                wait(pe, S("E_ready"), t - 1)
                nc.tensor.matmul(ps[b % 2][:, :], CA["later"], R[b % 2], start=True, stop=False)
                nc.tensor.matmul(ps[b % 2][:, :], far[:, :], acausal[:, :], start=False, stop=True).then_inc(S("D_done"), 1)

            def scores(t, n, m, b):
                if b == 0:
                    pe.wait_ge(S("Um_ready"), n + 1)
                    pe.wait_ge(S("Qx_ready"), n + 1)
                    pe.wait_ge(S("stage_ready"), n + 1)
                else:
                    pe.wait_ge(S("P_ready"), t)
                open_group(rowbank[0:C, 0, 0:1])
                for c in range(NC):
                    at = b * P + c * C
                    for g in range(G):
                        rows = slice(g * C, (g + 1) * C)
                        q = Qx[rows, :].rearrange("p (s w) -> p s w", s=HG)[:, :, at:at + C]
                        last = nc.tensor.matmul(rowbank[c * C:(c + 1) * C, g, 0:P], kTs[m][rows, at:at + C], q, start=True, stop=True)
                last.then_inc(S("A_done"), 1)

            def weighted_values(t, n, m, b):
                pe.wait_ge(S("P_ready"), t + 1)
                wait(pe, S("om_ready"), t)
                for g in range(G):
                    last = nc.tensor.matmul(ps[3][:, g * P:(g + 1) * P], vx[m][:, b * W + g * P:b * W + (g + 1) * P], PR[b % 2][:, g * P:(g + 1) * P],
                                            start=True, stop=True)
                last.then_inc(S("PV_done"), 1)

            def state_terms(n, m):
                pe.wait_ge(S("P_ready"), (n + 1) * B)
                pe.wait_ge(S("S_step"), n * NC + NC - 1)
                open_group(rowbank[0:C, 0, 0:1])
                for b in range(B):
                    for c in range(NC):
                        for g in range(G):
                            rows = slice(g * C, (g + 1) * C)
                            last = nc.tensor.matmul(rowbank[c * C:(c + 1) * C, g, b * C:(b + 1) * C], qTs[m][rows, b * P + c * C:b * P + (c + 1) * C],
                                                    Sb[m][rows, (c * B + b) * C:(c * B + b + 1) * C], start=True, stop=True)
                last.then_inc(S("inter_done"), 1)

            def turn_on(q):
                pe.wait_ge(S("on_ready"), q + 1)
                wait(pe, S("logits_ready"), q - 1)
                for b in range(B):
                    last = nc.tensor.transpose(ps[2][:, b * P:(b + 1) * P], on[:, b * P:(b + 1) * P], ident)
                last.then_inc(S("T1_done"), 1)

            def output_projection(q):
                pe.wait_ge(S("onT_ready"), q + 1)
                for b in range(B):
                    last = nc.tensor.matmul(ps[2][:, b * P:(b + 1) * P], onT[:, b * P:(b + 1) * P], wog[:, b], start=True, stop=True)
                last.then_inc(S("Wo_done"), 1)

            def turn_h2(q):
                pe.wait_ge(S("h2_ready"), q + 1)
                pe.wait_ge(S("x2_ready"), min(q + 2, NT) if isinstance(q, int) else q + 2)
                if isinstance(q, int) and q > NT - 3:
                    pe.wait_ge(S("logits_ready"), q)
                for b in range(B):
                    last = nc.tensor.transpose(ps[2][:, b * P:(b + 1) * P], h2[:, b * P:(b + 1) * P], ident)
                last.then_inc(S("T2_done"), 1)

            def router(q):
                pe.wait_ge(S("h2T_ready"), q + 1)
                for b in range(B):
                    last = nc.tensor.matmul(ps[2][:, b * E:(b + 1) * E], h2T[:, b * P:(b + 1) * P], wgs[:, :], start=True, stop=True)
                last.then_inc(S("router_done"), 1)

            def pe_step(n, m, A=True, Ct=True, more=True):
                t = n * B
                state_updates(n, m)
                if A: weighted_values(t - 1, n - 1, 1 - m, 3)
                if Ct: turn_h2(n - 3)
                scores(t, n, m, 0)
                log_decay(t + 2, 2)
                scores(t + 1, n, m, 1)
                if Ct: router(n - 3)
                weighted_values(t, n, m, 0)
                log_decay(t + 3, 3)
                scores(t + 2, n, m, 2)
                weighted_values(t + 1, n, m, 1)
                if more: log_decay(t + 4, 0)
                scores(t + 3, n, m, 3)
                weighted_values(t + 2, n, m, 2)
                if A: turn_on(n - 1)
                if more: log_decay(t + 5, 1)
                state_terms(n, m)
                if A: output_projection(n - 1)

            pe.wait_ge(S("eg_ready"), 1)
            pe.wait_ge(S("ef_ready"), 1)
            pe.wait_ge(S("far_ready"), 1)
            log_decay(0, 0)
            log_decay(1, 1)
            pe.wait_ge(S("td_ready"), 1)
            pe.wait_ge(S("wog_ready"), B)
            pe.wait_ge(S("eps_ready"), 3)
            pe_step(0, 0, A=False, Ct=False)
            pe_step(1, 1, Ct=False)
            pe_step(2, 0, Ct=False)
            with pe.Fori(1, NT // 2 - 1) as i:
                for m in range(2):
                    pe_step(i * 2 + 1 + m, 1 - m)
            pe_step(NT - 1, 1, more=False)
            weighted_values(U - 1, NT - 1, 1, 3)
            turn_h2(NT - 3)
            router(NT - 3)
            turn_on(NT - 1)
            output_projection(NT - 1)
            turn_h2(NT - 2)
            router(NT - 2)
            turn_h2(NT - 1)
            router(NT - 1)

            pe.wait_ge(S("M_ready"), 1)
            nc.tensor.matmul(ps[0][:, 0:UE], CA["before"], M, start=True, stop=True).then_inc(S("rank_done"), 1)
            nc.tensor.matmul(ps[1][:, 0:UE], CA["ones"], M, start=True, stop=True).then_inc(S("rank_done"), 1)
            pe.wait_ge(S("logits_ready"), NT)

            def place(i, m, first=False, last=False):
                pe.wait_ge(S("oneS_ready"), i + 1)
                pe.wait_ge(S("oneB_ready"), i + 1)
                for k in range(4):
                    mm = nc.tensor.matmul(ps[2][:, 0:NB], oneS[m][:, k * P:(k + 1) * P], oneB[m][:, k * NB:(k + 1) * NB],
                                          start=first and k == 0, stop=last and k == 3)
                mm.then_inc(S("inv_done"), 1)
            place(0, 0, first=True)
            place(1, 1)
            with pe.Fori(1, U // 4 - 1) as j:
                for m in range(2):
                    place(j * 2 + m, m)
            place(U // 2 - 2, 0)
            place(U // 2 - 1, 1, last=True)

            pe.wait_ge(S("eb_ready"), 1)
            pe.wait_ge(S("w2_in"), 16)
            pe.wait_ge(S("inv_evac"), 2)

            def expert(i):
                return pe.value_load(ebi[0:1, i:i + 1].bitcast(I32) if isinstance(i, int) else ebi[0:1, bass.ds(i, 1)].bitcast(I32), min_val=0, max_val=E - 1)

            def turn_rows(i, j, m4):
                m = m4 % 2
                pe.wait_ge(S(f"gath{m4}"), 16 * (j + 1))
                wait(pe, S("xT_ready"), i - 1)
                nc.tensor.transpose(ps[m][:, 0:P], xg[m4], ident).then_inc(S("Tx_done"), 1)

            def hidden(i, m, m4):
                pe.wait_ge(S("w1e_ready"), i + 1)
                pe.wait_ge(S("xT_ready"), i + 1)
                wait(pe, S("h1_ready"), i - 1)
                for c in range(FC):
                    last = nc.tensor.matmul(ps[2 + m][:, c * P:(c + 1) * P], w1e[m4][:, c * P:(c + 1) * P], xTe[m], start=True, stop=True)
                last.then_inc(S("mm1_done"), 1)

            def result(i, m, e):
                pe.wait_ge(S("gelu_ready"), i + 1)
                wait(pe, S("y_ready"), i - 1)
                for c in range(FC):
                    last = nc.tensor.matmul(ps[4 + m][:, 0:P], ge[m][:, c * P:(c + 1) * P], w2s[:, bass.ds(e * F + c * P, P)], start=(c == 0), stop=(c == FC - 1))
                last.then_inc(S("mm2_done"), 1)

            def pe_block(i, j, m):
                e = expert(i - 2)
                turn_rows(i, j, m)
                hidden(i - 1, (m - 1) % 2, (m - 1) % 4)
                result(i - 2, m % 2, e)

            turn_rows(0, 0, 0)
            turn_rows(1, 0, 1)
            hidden(0, 0, 0)
            pe_block(2, 0, 2)
            pe_block(3, 0, 3)
            with pe.Fori(1, NB // 4) as j:
                for m in range(4):
                    pe_block(j * 4 + m, j, m)
            e = expert(NB - 2)
            hidden(NB - 1, 1, 3)
            result(NB - 2, 0, e)
            result(NB - 1, 1, expert(NB - 1))

        @block.vector
        def _(dve):
            nc.vector.memset(epst[:, 0:1], EPS_LN).then_inc(S("eps_ready"), 1)
            nc.vector.memset(epst[:, 1:2], -0.5).then_inc(S("eps_ready"), 1)
            nc.vector.memset(onebf[:, :], 1.0).then_inc(S("eps_ready"), 1)

            def conditioning():
                dve.wait_ge(S("csil_ready"), 1)
                nc.vector.tensor_copy(cbc[:, :, :], csil[:, :].unsqueeze(2).to_broadcast([P, B, P])).then_inc(S("cbc_ready"), 1)
                dve.wait_ge(S("modt_done"), 1)
                nc.vector.tensor_copy(modT[:, 0], ps[0][:, 0:B])
                nc.vector.tensor_scalar(modT[:, 1], ps[0][:, B:2 * B], 1.0, None, ALU.add).then_inc(S("modt_evac"), 1)
                dve.wait_ge(S("wgate_done"), 1)
                nc.vector.tensor_copy(wtok[:, 2 * P:3 * P], ps[1][:, 0:P]).then_inc(S("wgate_evac"), 1)

            for half, name in enumerate(("x_lo", "x_hi")):
                if half == 1:
                    conditioning()
                dve.wait_ge(S(name), 16 * NT // 2)
                with dve.Fori(half * U // 2 // 4, (half + 1) * U // 2 // 4) as n:
                    for b in range(B):
                        nc.vector.bn_stats(st[:, bass.ds(n * B + b, 1)].rearrange("p a w -> p (a w)"),
                                           xs[:, bass.ds(n, 1), b * P:(b + 1) * P].rearrange("p a w -> p (a w)")).then_inc(S("st_ready"), 1)
            dve.wait_ge(S("st_ready"), U)
            nc.vector.tensor_tensor(ln[:, 0], st[:, :, 1], st[:, :, 4], ALU.add).then_inc(S("lnw1"), 1)
            nc.vector.tensor_tensor(ln[:, 1], st[:, :, 1], st[:, :, 4], ALU.subtract).then_inc(S("lnw1"), 1)
            nc.vector.tensor_tensor(ln[:, 2], st[:, :, 2], st[:, :, 5], ALU.add).then_inc(S("lnw1"), 1)
            dve.wait_ge(S("lnw1"), 3)
            nc.vector.tensor_tensor(ln[:, 3], ln[:, 1], ln[:, 1], ALU.mult).then_inc(S("lnw2"), 1)
            nc.vector.tensor_scalar(mean[:, :], ln[:, 0], 0.5, None, ALU.mult).then_inc(S("lnw2"), 1)
            dve.wait_ge(S("lnw2"), 1)
            nc.vector.scalar_tensor_tensor(out=ln[:, 4], in0=ln[:, 3], scalar=P / 4.0, in1=ln[:, 2], op0=ALU.mult, op1=ALU.add).then_inc(S("var_ready"), 1)
            dve.wait_ge(S("std_ready"), 1)
            nc.vector.reciprocal(rstd[:, :], ln[:, 5]).then_inc(S("rstd_ready"), 1)
            dve.wait_ge(S("lnw2"), 2)
            dve.wait_ge(S("rstd_ready"), 1)
            dve.wait_ge(S("modt_evac"), 1)

            def col(t, n, b):
                return t[:, n * B + b:n * B + b + 1] if isinstance(n, int) else t[:, bass.ds(n * B + b, 1)]

            def normalize(n, m):
                wait(dve, S("xT_done"), n - 1)
                src = step_view(xs, n)
                for b in range(B):
                    nc.vector.tensor_scalar(xn[m][:, b * P:(b + 1) * P], src[:, b * P:(b + 1) * P], col(mean, n, b), col(rstd, n, b),
                                            ALU.subtract, ALU.mult).then_inc(S("xn_ready"), 1)

            def modulate(n, m):
                dve.wait_ge(S("xT_done"), n + 1)
                wait(dve, S("tok_done"), (n - 1) * B)
                for b in range(B):
                    nc.vector.tensor_scalar(hT[m][:, b * P:(b + 1) * P], ps[m][:, b * P:(b + 1) * P], modT[:, 1, b:b + 1], modT[:, 0, b:b + 1],
                                            ALU.mult, ALU.add).then_inc(S("hT_ready"), 1)

            def keep_gate(n):
                for b in range(B):
                    dve.wait_ge(S("kv_evac"), n * B + b + 1)
                    dst = gz[:, bass.ds(n, 1), b].rearrange("p a w -> p (a w)") if not isinstance(n, int) else gz[:, n, b]
                    nc.vector.tensor_copy(dst, ps[4 + b][:, 2 * P:TOK]).then_inc(S("gz_evac"), 1)

            def key_sums(n, m):
                dve.wait_ge(S("ksq_ready"), n + 1)
                w = B * H
                dst = rk[:, n * w:(n + 1) * w] if isinstance(n, int) else rk[:, bass.ds(n * w, w)]
                nc.vector.tensor_reduce(dst, ksq[m].rearrange("p (g d) -> p g d", d=HD), AX, ALU.add).then_inc(S("kss_ready"), 1)

            normalize(0, 0)
            normalize(1, 1)
            modulate(0, 0)
            modulate(1, 1)
            normalize(2, 0)
            keep_gate(0)
            with dve.Fori(1, NT // 2 - 1) as i:
                for m in range(2):
                    n = i * 2 + m
                    modulate(n, m)
                    normalize(n + 1, 1 - m)
                    keep_gate(n - 1)
                    key_sums(n - 2, m)
            modulate(NT - 2, 0)
            normalize(NT - 1, 1)
            keep_gate(NT - 3)
            key_sums(NT - 4, 0)
            modulate(NT - 1, 1)
            keep_gate(NT - 2)
            key_sums(NT - 3, 1)
            keep_gate(NT - 1)
            key_sums(NT - 2, 0)
            key_sums(NT - 1, 1)

            dve.wait_ge(S("gz_evac"), U)
            z = gz[:, :, :, P:P + H].rearrange("p n b h -> p (n b) h")
            za3 = za.rearrange("p (u h) -> p u h", h=H)
            nc.vector.scalar_tensor_tensor(out=za3, in0=z, scalar=-1.0, in1=z, op0=ALU.mult, op1=ALU.max).then_inc(S("za_ready"), 1)
            dve.wait_ge(S("kss_ready"), NT)
            nc.vector.tensor_scalar(rk[:, :], rk[:, :], EPS_NORM * EPS_NORM, None, ALU.max).then_inc(S("kss_cl"), 1)
            dve.wait_ge(S("w_in"), 16 * W_LOADS)
            nc.vector.tensor_scalar(far[:, :].rearrange("p (c w) -> p c w", c=NC), CA["ident"][0:C, 0:C].unsqueeze(1).to_broadcast([C, NC, C]),
                                    LOG_ZERO, None, ALU.mult)
            nc.vector.tensor_scalar(acausal[:, :].rearrange("p (h i) -> p h i", h=H), CA["causal"][0:C].unsqueeze(1).to_broadcast([C, H, C]),
                                    -1.0, 1.0, ALU.mult, ALU.add).then_inc(S("far_ready"), 1)
            dve.wait_ge(S("lz_ready"), 1)
            nc.vector.scalar_tensor_tensor(out=zf[:, :].rearrange("p (u h) -> p u h", h=H), in0=z, scalar=0.0, in1=za3, op0=ALU.min,
                                           op1=ALU.subtract).then_inc(S("f_ready"), 1)
            nc.vector.tensor_scalar(mod[:, 2], mod[:, 2], 1.0, None, ALU.add).then_inc(S("modfix3"), 1)
            for k, j in enumerate((0, 3)):
                nc.vector.scalar_tensor_tensor(out=o1v(0), in0=mod[:, j], scalar=-1.0, in1=mod[:, j], op0=ALU.mult, op1=ALU.max).then_inc(S("modfix"), 1)
                nc.vector.tensor_scalar(o1v(1), mod[:, j], 0.0, 2.0, ALU.is_ge, ALU.mult).then_inc(S("modfix"), 1)
                dve.wait_ge(S("modfix"), 2 * k + 2)
                nc.vector.tensor_scalar(o1v(2), o1v(0), 0.25, None, ALU.max).then_inc(S("modfix2"), 1)
                dve.wait_ge(S("modfix2"), k + 1)
                nc.vector.scalar_tensor_tensor(out=mod[:, j], in0=o1v(1), scalar=-1.0, in1=o1v(2), op0=ALU.add, op1=ALU.mult).then_inc(S("modfix3"), 1)
                dve.wait_ge(S("modfix3"), k + 2)
            for b in range(B):
                nc.vector.scalar_tensor_tensor(out=wog[:, b], in0=wos[:, :], scalar=lnws[:, 0:1], in1=mod[:, 0, b], op0=ALU.mult, op1=ALU.mult).then_inc(S("wog_ready"), 1)
            dve.wait_ge(S("tc_done"), 1)
            nc.vector.tensor_copy(tc[:, :], ps[2][0:H, 0:U * NC]).then_inc(S("tc_evac"), 1)

            def stage(n, m):
                wait(dve, S("A_done"), (n - 1) * B)
                nc.vector.tensor_copy(kTs[m], step_view(kT, n))
                wait(dve, S("inter_done"), n - 1)
                nc.vector.tensor_copy(qTs[m], step_view(qT, n)).then_inc(S("stage_ready"), 1)

            def take_updates(n):
                dve.wait_ge(S("U_done"), n + 1)
                wait(dve, S("S_step"), n * NC)
                nc.vector.tensor_tensor(Um.rearrange("p (c b w) -> p c b w", c=NC, b=B), rowbank[:, 0, :].rearrange("p (b c w) -> p c b w", b=B, c=NC),
                                        CA["blockmask"].unsqueeze(1).unsqueeze(1).to_broadcast([P, NC, B, C]), ALU.mult).then_inc(S("Um_ready"), 1)

            def state_chain(n, m, c):
                if c == 0:
                    dve.wait_ge(S("Um_ready"), n + 1)
                    wait(dve, S("inter_done"), n)
                wait(dve, S("S_step"), n * NC + c)
                before = Sb[m][:, c * B * C:(c + 1) * B * C].rearrange("p (b w) -> p b w", b=B)
                tdc = cols(td, n * B * NC, B * NC).rearrange("p (b c) -> p b c", c=NC)[:, :, c:c + 1].to_broadcast([P, B, C])
                nc.vector.tensor_tensor(stmp.rearrange("p (b w) -> p b w", b=B), before, tdc, ALU.mult).then_inc(S("S_mul"), 1)
                dve.wait_ge(S("S_mul"), n * NC + c + 1)
                dst = Sb[m][:, (c + 1) * B * C:(c + 2) * B * C] if c < NC - 1 else Sb[1 - m][:, 0:B * C]
                nc.vector.tensor_tensor(dst, stmp, Um[:, c * B * C:(c + 1) * B * C], ALU.add).then_inc(S("S_step"), 1)

            def weigh(t, b):
                dve.wait_ge(S("A_done"), t + 1)
                dve.wait_ge(S("E_ready"), t + 1)
                wait(dve, S("PV_done"), t - 1)
                nc.vector.tensor_tensor(PR[b % 2].rearrange("p (g w) -> p g w", g=G), EM[b % 2].rearrange("p (g w) -> p g w", g=G),
                                        rowbank[:, :, 0:P], ALU.mult).then_inc(S("P_ready"), 1)

            def take_state_terms(n):
                dve.wait_ge(S("inter_done"), n + 1)
                wait(dve, S("o2_ready"), n)
                nc.vector.tensor_tensor(o1.rearrange("p (g q d) -> p g q d", g=G, d=HD), rowbank[:, :, 0:B * C].rearrange("p g (q d) -> p g q d", d=HD),
                                        cols(ef, n * B * H, B * H).rearrange("p (g q) -> p g q", g=G).unsqueeze(3).to_broadcast([P, G, B * HG, HD]),
                                        ALU.mult).then_inc(S("o1_ready"), 1)

            def take_values(t, n, b):
                dve.wait_ge(S("om_ready"), t + 1)
                if b == 0: wait(dve, S("ot_ready"), n)
                nc.vector.tensor_reduce(osum[:, b * P:(b + 1) * P].rearrange("p (g i) -> p g i", g=G), om.rearrange("p (g s i) -> p g i s", g=G, s=HG),
                                        AX, ALU.add).then_inc(S("osum_ready"), 1)

            def add_values(q):
                dve.wait_ge(S("osum_ready"), (q + 1) * B)
                wait(dve, S("o2_ready"), q)
                nc.vector.transpose(ot, osum).then_inc(S("ot_ready"), 1)
                dve.wait_ge(S("ot_ready"), q + 1)
                dve.wait_ge(S("o1_ready"), q + 1)
                wait(dve, S("T1_done"), q)
                nc.vector.tensor_tensor(o2.rearrange("p (b g w) -> p b g w", b=B, g=G), o1.rearrange("p (g b w) -> p b g w", b=B, g=G),
                                        ot.rearrange("p (b g w) -> p b g w", b=B, g=G), ALU.add).then_inc(S("o2_ready"), 1)

            def before_statistics(q, tag, src_ready):
                dve.wait_ge(S(src_ready), q + 1)
                wait(dve, S("sum" + tag), 4 * q)

            def statistics(q, k, tag, src):
                for b in range(B):
                    last = nc.vector.bn_stats(stb[k][:, 6 * b:6 * b + 6], src[:, b * P:(b + 1) * P])
                last.then_inc(S("bn" + tag), 1)
                dve.wait_ge(S("bn" + tag), q + 1)
                wait(dve, S("sq" + tag), 2 * q)
                wait(dve, S("var" + tag), q)
                sv = stb[k].rearrange("p (b s) -> p b s", s=6)
                L = lambda j: lnb[k][:, j * B:(j + 1) * B]
                nc.vector.tensor_tensor(L(0), sv[:, :, 1], sv[:, :, 4], ALU.add).then_inc(S("sum" + tag), 1)
                nc.vector.tensor_tensor(L(1), sv[:, :, 1], sv[:, :, 4], ALU.subtract).then_inc(S("sum" + tag), 1)
                nc.vector.tensor_tensor(L(2), sv[:, :, 2], sv[:, :, 5], ALU.add).then_inc(S("sum" + tag), 1)
                dve.wait_ge(S("sum" + tag), 4 * q + 3)
                wait(dve, S(scaled[tag]), q - lag[tag])
                nc.vector.tensor_tensor(L(3), L(1), L(1), ALU.mult).then_inc(S("sq" + tag), 1)
                nc.vector.tensor_scalar(L(7), L(0), 0.5, None, ALU.mult).then_inc(S("sq" + tag), 1)
                dve.wait_ge(S("sq" + tag), 2 * q + 1)
                wait(dve, S("rstd" + tag), q - lag[tag])
                nc.vector.scalar_tensor_tensor(out=L(5), in0=L(3), scalar=P / 4.0, in1=L(2), op0=ALU.mult, op1=ALU.add).then_inc(S("sum" + tag), 1)
                dve.wait_ge(S("sum" + tag), 4 * q + 4)
                nc.vector.tensor_scalar(L(4), L(5), 1.0 / P, EPS_LN, ALU.mult, ALU.add).then_inc(S("var" + tag), 1)

            def scale_rows(q, k, tag, dst, src, done):
                dve.wait_ge(S("rstd" + tag), q + 1)
                dve.wait_ge(S("sq" + tag), 2 * q + 2)
                for b in range(B):
                    last = nc.vector.tensor_scalar(dst[:, b * P:(b + 1) * P], src[:, b * P:(b + 1) * P], lnb[k][:, 7 * B + b:7 * B + b + 1],
                                                   lnb[k][:, 6 * B + b:6 * B + b + 1], ALU.subtract, ALU.mult)
                last.then_inc(S(done), 1)

            def add_attention(q):
                dve.wait_ge(S("Wo_done"), q + 1)
                v = step_view(xs, q)
                nc.vector.tensor_tensor(v, v, ps[2][:, :], ALU.add).then_inc(S("x2_ready"), 1)

            def keep_logits(q):
                dve.wait_ge(S("router_done"), q + 1)
                nc.vector.tensor_tensor(cols(lg, q * B * E, B * E).rearrange("p (b e) -> p b e", b=B), ps[2][:, 0:B * E].rearrange("p (b e) -> p b e", b=B),
                                        bgs[:, :].unsqueeze(1).to_broadcast([P, B, E]), ALU.add).then_inc(S("logits_ready"), 1)

            def stats_A(q):
                before_statistics(q, "A", "o3_ready")
                statistics(q, 0, "A", o3)

            def stats_B(q):
                statistics(q, 1, "B", step_view(xs, q))

            def scale_A(q):
                scale_rows(q, 0, "A", on, o3, "on_ready")

            def scale_B(q):
                wait(dve, S("h2_ready"), q)
                scale_rows(q, 1, "B", xn2, step_view(xs, q), "xn2_ready")

            def dve_step(n, m, A=True, Bt=True, Ct=True, more=True):
                t = n * B
                take_updates(n)
                if Bt: add_attention(n - 2)
                if A: take_values(t - 1, n - 1, 3)
                if Bt: before_statistics(n - 2, "B", "x2_ready")
                weigh(t, 0)
                if A: add_values(n - 1)
                state_chain(n, m, 0)
                weigh(t + 1, 1)
                if Ct: keep_logits(n - 3)
                if Bt: stats_B(n - 2)
                take_values(t, n, 0)
                weigh(t + 2, 2)
                if A: stats_A(n - 1)
                state_chain(n, m, 1)
                take_values(t + 1, n, 1)
                if A: scale_A(n - 1)
                weigh(t + 3, 3)
                state_chain(n, m, 2)
                if Bt: scale_B(n - 2)
                take_values(t + 2, n, 2)
                if more: stage(n + 1, 1 - m)
                take_state_terms(n)
                state_chain(n, m, 3)

            nc.vector.memset(Sb[0][:, 0:B * C], 0.0).then_inc(S("S_zero"), 1)
            dve.wait_ge(S("S_zero"), 1)
            dve.wait_ge(S("k_evac"), NT)
            stage(0, 0)
            dve.wait_ge(S("td_ready"), 1)
            dve_step(0, 0, A=False, Bt=False, Ct=False)
            dve_step(1, 1, Bt=False, Ct=False)
            dve_step(2, 0, Ct=False)
            with dve.Fori(1, NT // 2 - 1) as i:
                for m in range(2):
                    dve_step(i * 2 + 1 + m, 1 - m)
            dve_step(NT - 1, 1, more=False)
            add_attention(NT - 2)
            before_statistics(NT - 2, "B", "x2_ready")
            take_values(U - 1, NT - 1, 3)
            add_values(NT - 1)
            stats_B(NT - 2)
            keep_logits(NT - 3)
            stats_A(NT - 1)
            scale_B(NT - 2)
            scale_A(NT - 1)
            add_attention(NT - 1)
            before_statistics(NT - 1, "B", "x2_ready")
            stats_B(NT - 1)
            keep_logits(NT - 2)
            scale_B(NT - 1)
            keep_logits(NT - 1)

            def e3(t):
                return t.rearrange("p (u e) -> p u e", e=E)

            def eb(t):
                return t.unsqueeze(2).to_broadcast([P, U, E])

            steps = [0]

            def then(ins):
                steps[0] += 1
                ins.then_inc(S("r1"), 1)
                dve.wait_ge(S("r1"), steps[0])

            V = nc.vector
            dve.wait_ge(S("logits_ready"), NT)
            dve.wait_ge(S("h2_ready"), NT)
            dve.wait_ge(S("router_done"), NT)
            dve.wait_ge(S("h2_stored"), 16 * NT)
            then(V.tensor_reduce(mx, e3(lg), AX, ALU.max))
            V.tensor_tensor(e3(lgx), e3(lg), eb(mx), ALU.subtract).then_inc(S("lx_ready"), 1)
            dve.wait_ge(S("le_ready"), 1)
            then(V.tensor_reduce(zs, e3(wt), AX, ALU.add))
            then(V.reciprocal(m1, zs))
            then(V.tensor_tensor(e3(wt), e3(wt), eb(m1), ALU.mult))
            rank8 = CA["rank8"].unsqueeze(1).to_broadcast([P, U, E])

            def choose(src, top, onehot):
                then(V.tensor_reduce(top, e3(src), AX, ALU.max))
                then(V.tensor_tensor(e3(key), e3(src), eb(top), ALU.is_equal))
                then(V.tensor_tensor(e3(key), e3(key), rank8, ALU.mult))
                then(V.tensor_reduce(k1, e3(key), AX, ALU.max))
                then(V.tensor_tensor(e3(onehot), rank8, eb(k1), ALU.is_equal))

            choose(wt, tw1, oh1)
            then(V.scalar_tensor_tensor(out=wt2, in0=oh1, scalar=-2.0, in1=wt, op0=ALU.mult, op1=ALU.add))
            choose(wt2, tw2, oh2)
            V.tensor_tensor(M, oh1, oh2, ALU.add).then_inc(S("M_ready"), 1)
            then(V.tensor_tensor(tws, tw1, tw2, ALU.add))
            then(V.tensor_scalar(tws, tws, EPS_GATE, None, ALU.add))
            then(V.reciprocal(zs, tws))
            then(V.tensor_tensor(tw1, tw1, zs, ALU.mult))
            then(V.tensor_tensor(tw2, tw2, zs, ALU.mult))
            then(V.memset(ones_r, 1.0))
            dve.wait_ge(S("rank_done"), 2)
            then(V.tensor_copy(t1r, ps[1][:, 0:UE]))
            for e in range(E):
                then(V.tensor_tensor_scan(e3(pre)[:, :, e], ones_r[:, 0:U], e3(t1r)[:, :, e], 0.0, ALU.mult, ALU.add))
            then(V.tensor_tensor(e3(cmp32.rearrange("p (e k) -> p (e k)", e=E)) if False else cmp32.rearrange("p (e k) -> p e k", e=E),
                                 e3(pre)[:, U - 1, :].unsqueeze(2).to_broadcast([P, E, 32]),
                                 CA["start_iota"].unsqueeze(1).to_broadcast([P, E, 32]), ALU.is_gt))
            then(V.tensor_reduce(nbk, cmp32.rearrange("p (e k) -> p e k", e=E), AX, ALU.add))
            then(V.tensor_tensor_scan(endb, ones_r[:, 0:E], nbk, 0.0, ALU.mult, ALU.add))
            then(V.tensor_tensor(startb, endb, nbk, ALU.subtract))
            then(V.tensor_scalar(startb, startb, float(P), None, ALU.mult))
            then(V.tensor_tensor(pre, pre, t1r, ALU.subtract))
            then(V.tensor_tensor(pos, pre, ps[0][:, 0:UE], ALU.add))
            then(V.tensor_tensor(e3(pos), e3(pos), startb.unsqueeze(1).to_broadcast([P, U, E]), ALU.add))
            then(V.tensor_tensor(t1r, pos, oh1, ALU.mult))
            then(V.tensor_tensor(t2r, pos, oh2, ALU.mult))
            then(V.tensor_reduce(posf[:, 0:U], e3(t1r), AX, ALU.add))
            then(V.tensor_reduce(posf[:, U:2 * U], e3(t2r), AX, ALU.add))
            i32 = lambda t: t.bitcast(I32)
            then(V.tensor_copy(i32(posi), posf))
            then(V.tensor_scalar(i32(blki), i32(posi), 7, None, ALU.logical_shift_right))
            then(V.tensor_scalar(i32(sli), i32(posi), P - 1, None, ALU.bitwise_and))
            then(V.tensor_copy(blkf, i32(blki)))
            V.tensor_copy(slf, i32(sli)).then_inc(S("slots_ready"), 1)
            ebc3 = ebc.rearrange("p (i e) -> p i e", e=E)
            then(V.tensor_tensor(ebc3, endb.unsqueeze(1).to_broadcast([P, NB, E]), CA["block_iota"].unsqueeze(2).to_broadcast([P, NB, E]), ALU.is_le))
            then(V.tensor_reduce(ebf, ebc3, AX, ALU.add))
            then(V.tensor_scalar(ebf, ebf, float(E - 1), None, ALU.min))
            V.tensor_copy(i32(ebi), ebf).then_inc(S("eb_ready"), 1)

            def one_hots(i, m):
                wait(dve, S("inv_done"), i - 1)
                for k in range(4):
                    last = V.tensor_scalar(oneB[m][:, k * NB:(k + 1) * NB], CA["block_iota"], cols(blkf, 4 * i + k, 1), cols(CA["dest"], 4 * i + k, 1),
                                           ALU.is_equal, ALU.mult)
                last.then_inc(S("oneB_ready"), 1)

            one_hots(0, 0)
            one_hots(1, 1)
            with dve.Fori(1, U // 4) as j:
                for m in range(2):
                    one_hots(j * 2 + m, m)
            dve.wait_ge(S("inv_done"), U // 2)
            then(V.tensor_copy(inv, ps[2][:, 0:NB]))
            then(V.tensor_scalar(invz, inv[:, 0:NB], 0.0, float(PAD), ALU.is_equal, ALU.mult))
            then(V.tensor_scalar(inv[:, 0:NB], inv[:, 0:NB], 1.0, None, ALU.subtract))
            then(V.tensor_tensor(inv[:, 0:NB], inv[:, 0:NB], invz, ALU.add))
            V.tensor_copy(i32(dst_i), inv[:, 0:NB]).then_inc(S("inv_evac"), 1)
            dve.wait_ge(S("inv_evac"), 1)
            V.tensor_scalar(i32(src_i), i32(dst_i), ROWS - 1, None, ALU.bitwise_and).then_inc(S("inv_evac"), 1)
            dve.wait_ge(S("inv_evac"), 2)

            def read_index(i, j, m):
                wait(dve, S(f"gath{m}"), 16 * j)
                V.tensor_copy(i32(idg[m]), cols(i32(src_i), i, 1)).then_inc(S("idg_ready"), 1)

            def write_index(i, j, m4):
                wait(dve, S(f"y_stored{m4}"), 16 * j)
                V.tensor_copy(i32(idy[m4]), cols(i32(dst_i), i, 1))

            def take_rows(i, m):
                dve.wait_ge(S("Tx_done"), i + 1)
                wait(dve, S("mm1_done"), i - 1)
                V.tensor_copy(xTe[m], ps[m][:, 0:P]).then_inc(S("xT_ready"), 1)

            def bias1(i, m, m4):
                dve.wait_ge(S("mm1_done"), i + 1)
                wait(dve, S("gelu_ready"), i - 1)
                V.tensor_tensor(h1[m].rearrange("p (c t) -> p c t", c=FC), ps[2 + m][:, :].rearrange("p (c t) -> p c t", c=FC),
                                w1e[m4][:, F:F + FC].unsqueeze(2).to_broadcast([P, FC, P]), ALU.add).then_inc(S("h1_ready"), 1)

            def bias2(i, m4):
                dve.wait_ge(S("mm2_done"), i + 1)
                V.tensor_tensor(ye[m4], ps[4 + m4 % 2][:, 0:P], w1e[m4][:, F + FC:EW], ALU.add).then_inc(S("y_ready"), 1)

            def dve_block(i, j, m, more=True):
                take_rows(i, m % 2)
                bias1(i - 1, (m - 1) % 2, (m - 1) % 4)
                if more: read_index(i + 3, j + (m + 3) // 4, (m + 3) % 4)
                write_index(i - 2, j - (m < 2), (m - 2) % 4)
                bias2(i - 2, (m - 2) % 4)

            for i in range(4):
                read_index(i, 0, i)
            take_rows(0, 0)
            take_rows(1, 1)
            bias1(0, 0, 0)
            read_index(4, 1, 0)
            for i in range(2, 4):
                dve_block(i, 0, i)
            with dve.Fori(1, NB // 4 - 1) as j:
                for m in range(4):
                    dve_block(j * 4 + m, j, m)
            for m in range(4):
                dve_block(NB - 4 + m, NB // 4 - 1, m, more=m == 0)
            bias1(NB - 1, 1, 3)
            for i in range(NB - 2, NB):
                write_index(i, NB // 4 - 1, i % 4)
                bias2(i, i % 4)

            def sum_rows(n, m):
                dve.wait_ge(S("c1"), n + 1)
                for b in range(B):
                    last = V.scalar_tensor_tensor(out=ysum[m][:, b * P:(b + 1) * P], in0=cols(Y2, (n * B + b) * P, P), scalar=cols(tw2, n * B + b, 1),
                                                  in1=ysum[m][:, b * P:(b + 1) * P], op0=ALU.mult, op1=ALU.add)
                last.then_inc(S("c2"), 1)
                dve.wait_ge(S("c2"), n + 1)
                statistics(n, 2 + m % 2, "C", ysum[m])

            def norm_rows(n, m):
                scale_rows(n, 2 + m % 2, "C", ysum[m], ysum[m], "c3")
                dve.wait_ge(S("c3"), n + 1)
                V.tensor_tensor(ysum[m], ysum[m], GB[0], ALU.mult).then_inc(S("c5"), 1)

            dve.wait_ge(S("gb_ready"), 2)
            sum_rows(0, 0)
            for n in range(1, 4):
                sum_rows(n, n)
                norm_rows(n - 1, n - 1)
            with dve.Fori(1, NT // 4) as j:
                for m in range(4):
                    sum_rows(j * 4 + m, m)
                    norm_rows(j * 4 + m - 1, (m - 1) % 4)
            norm_rows(NT - 1, 3)

        @block.gpsimd
        def _(pool):
            def squares(n, m):
                pool.wait_ge(S("kv_evac"), (n + 1) * B)
                wait(pool, S("kss_ready"), n - 1)
                src = kv[:, n, :, 0:P] if isinstance(n, int) else kv[:, bass.ds(n, 1), :, 0:P].rearrange("p a b w -> p (a b) w")
                nc.gpsimd.tensor_tensor(ksq[m].rearrange("p (b w) -> p b w", b=B), src, src, ALU.mult).then_inc(S("ksq_ready"), 1)
            squares(0, 0)
            squares(1, 1)
            with pool.Fori(1, NT // 2) as i:
                for m in range(2):
                    squares(i * 2 + m, m)

            def decay_rows(t, n, b):
                wait(pool, S("D_done"), t - 1)
                fcol = cols(zf, (n * B + b) * H, H).unsqueeze(2).to_broadcast([P, H, C])
                nc.gpsimd.tensor_tensor(R[b % 2].rearrange("p (h i) -> p h i", h=H), fcol,
                                        CA["causal"].unsqueeze(1).to_broadcast([P, H, C]), ALU.mult).then_inc(S("R_ready"), 1)

            def values(r, m):
                def by_head(t):
                    return cols(t, r * B * H, B * H).rearrange("p (b h) -> p b h", b=B).unsqueeze(3).to_broadcast([P, B, H, HD])
                wait(pool, S("U_done"), r - 1)
                nc.gpsimd.tensor_tensor(kd[m].rearrange("p (b h d) -> p b h d", b=B, h=H), kv_step(r, 0).rearrange("p b (h d) -> p b h d", h=H),
                                        by_head(eg), ALU.mult).then_inc(S("kd_ready"), 1)
                wait(pool, S("vx_ready"), r * B)
                nc.gpsimd.tensor_tensor(vp.rearrange("p (b h d) -> p b h d", b=B, h=H), kv_step(r, P).rearrange("p b (h d) -> p b h d", h=H),
                                        by_head(rk), ALU.mult).then_inc(S("vp_ready"), 1)

            def inverse_std(q, k, tag):
                pool.wait_ge(S("var" + tag), q + 1)
                wait(pool, S(scaled[tag]), q - lag[tag])
                nc.gpsimd.tensor_tensor(lnb[k][:, 6 * B:7 * B], lnb[k][:, 4 * B:5 * B], epst[:, 1:2].to_broadcast([P, B]), ALU.pow).then_inc(S("rstd" + tag), 1)

            def gate(q):
                pool.wait_ge(S("o2_ready"), q + 1)
                nc.gpsimd.tensor_tensor(o3.rearrange("p (b w) -> p b w", b=B), o2.rearrange("p (b w) -> p b w", b=B), gate_step(q),
                                        ALU.mult).then_inc(S("o3_ready"), 1)

            def modulate2(q):
                pool.wait_ge(S("xn2_ready"), q + 1)
                nc.gpsimd.tensor_tensor(h2t, xn2, mod[:, 2].rearrange("p b w -> p (b w)"), ALU.mult).then_inc(S("h2a_ready"), 1)
                pool.wait_ge(S("h2a_ready"), q + 1)
                wait(pool, S("T2_done"), q)
                wait(pool, S("h2_stored"), 16 * q)
                nc.gpsimd.tensor_tensor(h2, h2t, mod[:, 1].rearrange("p b w -> p (b w)"), ALU.add).then_inc(S("h2_ready"), 1)

            def pool_step(n, m, A=True, Bt=True, more=True):
                t = n * B
                decay_rows(t + 2, n, 2)
                if more: values(n + 1, 1 - m)
                decay_rows(t + 3, n, 3)
                if A: gate(n - 1)
                if more: decay_rows(t + 4, n + 1, 0)
                if Bt: inverse_std(n - 2, 1, "B")
                if A: inverse_std(n - 1, 0, "A")
                if more: decay_rows(t + 5, n + 1, 1)
                if Bt: modulate2(n - 2)

            pool.wait_ge(S("f_ready"), 1)
            decay_rows(0, 0, 0)
            decay_rows(1, 0, 1)
            pool.wait_ge(S("rk_ready"), 1)
            pool.wait_ge(S("eg_ready"), 1)
            values(0, 0)
            pool.wait_ge(S("modfix3"), 2)
            pool.wait_ge(S("eps_ready"), 3)
            pool_step(0, 0, A=False, Bt=False)
            pool.wait_ge(S("gate_ready"), 1)
            pool_step(1, 1, Bt=False)
            pool_step(2, 0)
            with pool.Fori(1, NT // 2 - 1) as i:
                for m in range(2):
                    pool_step(i * 2 + 1 + m, 1 - m)
            pool_step(NT - 1, 1, more=False)
            gate(NT - 1)
            inverse_std(NT - 2, 1, "B")
            inverse_std(NT - 1, 0, "A")
            modulate2(NT - 2)
            inverse_std(NT - 1, 1, "B")
            modulate2(NT - 1)

            pool.wait_ge(S("gam_in"), 32)
            pool.wait_ge(S("logits_ready"), NT)
            pool.wait_ge(S("h2_stored"), 16 * NT)
            for j in range(2):
                nc.gpsimd.tensor_tensor(GB[j].rearrange("p (b w) -> p b w", b=B), mod[:, 3], gam[:, j].unsqueeze(1).to_broadcast([P, B, P]),
                                        ALU.mult).then_inc(S("gb_ready"), 1)
            pool.wait_ge(S("gb_ready"), 2)
            with pool.Fori(0, NT) as n:
                nc.gpsimd.tensor_tensor(step_view(xs, n), step_view(xs, n), GB[1], ALU.add).then_inc(S("c4"), 1)

            pool.wait_ge(S("slots_ready"), 1)

            def slot_gaps(i, m):
                wait(pool, S("gap2_ready"), i - 1)
                nc.gpsimd.tensor_tensor(slot_gap[m].rearrange("p (k s) -> p k s", k=4), CA["slot_iota"].unsqueeze(1).to_broadcast([P, 4, P]),
                                        cols(slf, 4 * i, 4).unsqueeze(2).to_broadcast([P, 4, P]), ALU.subtract).then_inc(S("gap_ready"), 1)

            slot_gaps(0, 0)
            slot_gaps(1, 1)
            with pool.Fori(1, U // 4) as j:
                for m in range(2):
                    slot_gaps(j * 2 + m, m)

            bound = pool.alloc_register("bound")
            pool.reg_mov(bound, 2 * ROWS - 1)

            def gather(i, m):
                pool.wait_ge(S("idg_ready"), i + 1)
                wait(pool, S("Tx_done"), i - 3)
                pool.reg_alu(bound, bound, 1, op=ALU.bitwise_or)
                nc.gpsimd.indirect_dma_start(xg[m], None, h2_rows, bass.IndirectOffsetOnAxis(ap=idg[m].bitcast(I32), axis=0),
                                             bounds_check=bound, oob_is_err=False).then_inc(S(f"gath{m}"), 16)

            def scatter(i, m):
                pool.wait_ge(S("y_ready"), i + 1)
                pool.reg_alu(bound, bound, 1, op=ALU.bitwise_or)
                nc.gpsimd.indirect_dma_start(y_rows, bass.IndirectOffsetOnAxis(ap=idy[m].bitcast(I32), axis=0), ye[m], None,
                                             bounds_check=bound, oob_is_err=False).then_inc(S(f"y_stored{m}"), 16)

            def pool_block(i, m, more=True):
                if more: gather(i + 3, (m + 3) % 4)
                scatter(i - 2, (m - 2) % 4)

            for i in range(5):
                gather(i, i % 4)
            for i in range(2, 4):
                pool_block(i, i)
            with pool.Fori(1, NB // 4 - 1) as j:
                for m in range(4):
                    pool_block(j * 4 + m, m)
            for m in range(4):
                pool_block(NB - 4 + m, m, more=m == 0)
            for i in range(NB - 2, NB):
                scatter(i, i % 4)

            def residual(n, m):
                pool.wait_ge(S("c5"), n + 1)
                nc.gpsimd.tensor_tensor(step_view(xs, n), step_view(xs, n), ysum[m], ALU.add).then_inc(S("x3_ready"), 1)

            pool.wait_ge(S("c4"), NT)
            inverse_std(0, 2, "C")
            for n in range(1, 4):
                inverse_std(n, 2 + n % 2, "C")
                residual(n - 1, n - 1)
            with pool.Fori(1, NT // 4) as j:
                for m in range(4):
                    inverse_std(j * 4 + m, 2 + m % 2, "C")
                    residual(j * 4 + m - 1, (m - 1) % 4)
            residual(NT - 1, 3)


def constants(np):
    p = np.arange(P)[:, None]
    q = np.arange(P)[None, :]
    t = {
        "ident": p == q,
        "later": (p // C == q // C) & (p > q),
        "upto": (p // C == q // C) & (p <= q),
        "before": p < q,
        "ones": np.ones((P, P)),
        "headsel": p == q // HD,
        "slot_iota": q + 0 * p,
        "block_iota": np.arange(NB)[None, :] + 0 * p,
        "causal": p % C <= np.arange(C)[None, :],
        "blockmask": (p % C) // HD == np.arange(C)[None, :] // HD,
        "start_iota": P * np.arange(32)[None, :] + 0 * p,
        "dest": P * np.array([[k * U + (u % B) * NT + u // B for k in range(2) for u in range(U)]]) + p + 1,
        "chunk_of": p // C == np.arange(NC)[None, :],
        "head_of": (p % C) // HD == np.arange(HG)[None, :],
        "rank8": E - np.arange(E)[None, :] + 0 * p,
    }
    return np.concatenate([np.asarray(t[n], np.float32) for n, _ in CONST_WIDTHS], axis=1)


def kernel(**inputs):
    import numpy as np
    import concourse.bacc as bacc
    from concourse import mybir as mb
    from concourse.bass_utils import run_bass_kernel_spmd

    a = {k: np.asarray(v) for k, v in inputs.items()}
    arrays = {
        "x": a["L0_attn_x"], "wq_t": a["L0_attn_Wq"].T, "wk_t": a["L0_attn_Wk"].T,
        "wkv_t": np.concatenate([a["L0_attn_Wk"].T, a["L0_attn_Wv"].T], axis=1), "wf_t": a["L0_attn_Wf"].T,
        "wg1": a["L0_attn_Wg1"], "wg2_t": a["L0_attn_Wg2"].T, "lnw": a["L0_attn_ln_w"].reshape(D, 1),
        "wo_t": a["L0_attn_Wo"].T, "wg": a["L0_ffn_Wg"], "bg": a["L0_ffn_bg"], "w1": a["L0_ffn_W1"],
        "b1_t": a["L0_ffn_b1"].reshape(E, FC, P).transpose(2, 0, 1), "w2": a["L0_ffn_W2"], "b2": a["L0_ffn_b2"], "gamma": a["L0_ffn_gamma"],
        "beta": a["L0_ffn_beta"], "c_t": a["L0_c"].T, "wmod": a["L0_wmod"], "consts": constants(np),
    }
    arrays = {f"in_{k}": np.ascontiguousarray(v) for k, v in arrays.items()}
    nc = bacc.Bacc("TRN2", target_bir_lowering=False, num_devices=1)
    args = [nc.dram_tensor(k, v.shape, mb.dt.from_np(v.dtype), kind="ExternalInput").ap() for k, v in arrays.items()]
    args.append(nc.dram_tensor("out_x", (B, N, D), F32, kind="ExternalOutput").ap())
    build(nc, *args)
    r = run_bass_kernel_spmd(nc, [arrays], core_ids=[0])
    return r.results[0]["out_x"]
```

```python
from contextlib import ExitStack

import concourse.bass as bass
from concourse import mybir

F32 = mybir.dt.float32
BF16 = mybir.dt.bfloat16
I32 = mybir.dt.int32
ALU = mybir.AluOpType
ACT = mybir.ActivationFunctionType
AX = mybir.AxisListType.X

P = 128
B, N, D = 4, 1024, 128
H, HD = 16, 8
E, F = 8, 512
NT = N // P
U = NT * B
W = B * P
C = 32
NC = P // C
G = 4
HG = H // G
FC = F // P
TOK = 3 * P + H
NB = 2 * B * N // P + E
LOG_ZERO = -30000.0
EPS_LN, EPS_GATE, EPS_NORM = 1e-5, 1e-8, 1e-12
PAD = 1 << 20
ROWS = B * N
EW = F + FC + D

CONST_WIDTHS = [("ident", P), ("later", P), ("upto", P), ("before", P), ("ones", P), ("headsel", P),
                ("slot_iota", P), ("block_iota", NB), ("causal", C), ("blockmask", C), ("start_iota", 32),
                ("dest", 4 * U), ("chunk_of", NC), ("head_of", HG), ("rank8", E)]
CONST_AT, _at = {}, 0
for _name, _w in CONST_WIDTHS:
    CONST_AT[_name] = (_at, _w)
    _at += _w
CONST_N = _at


def wait(eng, sem, value):
    if not (isinstance(value, int) and value <= 0):
        eng.wait_ge(sem, value)


def build(nc, x, wq_t, wk_t, wkv_t, wf_t, wg1, wg2_t, lnw, wo_t, wg, bg, w1, b1_t, w2, b2, gamma, beta, c_t, wmod,
          consts, out):
    ctx = ExitStack()
    with ctx:
        def sb(name, shape, dt=F32):
            return ctx.enter_context(nc.sbuf_tensor(name, shape, dt))

        def psum(name, shape, dt=F32):
            return ctx.enter_context(nc.psum_tensor(name, shape, dt))

        def sem(name):
            return ctx.enter_context(nc.semaphore(name))

        h2_rows = nc.dram_tensor("h2_rows", (ROWS, D), F32, kind="Internal").ap()
        y_rows = nc.dram_tensor("y_rows", (2 * ROWS, D), F32, kind="Internal").ap()

        xs = sb("xs", [P, NT, W])
        ct = sb("ct", [P, CONST_N])
        qT = sb("qT", [P, NT, W])
        kT = sb("kT", [P, NT, W])
        kv = sb("kv", [P, NT, B, 2 * P])
        gz = sb("gz", [P, NT, B, P + H])
        wqs = sb("wqs", [P, P])
        wks = sb("wks", [P, P])
        wtok = sb("wtok", [P, TOK])
        wos = sb("wos", [P, P])
        wog = sb("wog", [P, B, P])
        lnws = sb("lnws", [P, 1])
        wgs = sb("wgs", [P, E])
        bgs = sb("bgs", [P, E])
        wg1s = sb("wg1s", [HD, D])
        wg2s = sb("wg2s", [HD, D])
        cs = sb("cs", [P, B])
        csil = sb("csil", [P, B])
        modT = sb("modT", [P, 2, B])
        mod = sb("mod", [P, 4, B, P])
        gam = sb("gam", [P, 2, P])
        epst = sb("epst", [P, 2])
        onebf = sb("onebf", [P, C], BF16)
        far = sb("far", [C, P], BF16)
        acausal = sb("acausal", [C, W], BF16)

        st = sb("st", [P, U, 6])
        ln = sb("ln", [P, 8, U])
        mean = sb("mean", [P, U])
        rstd = sb("rstd", [P, U])
        zf = sb("zf", [P, U * H])
        rk = sb("rk", [P, U * H])
        eg = sb("eg", [P, U * H])
        ef = sb("ef", [P, U * H])
        tc = sb("tc", [H, U * NC])
        td = sb("td", [P, U * NC])

        WORK = 38 * W
        work = sb("work", [P, WORK])

        def ws(at, n):
            return work[:, at:at + n]

        xn = [ws(m * W, W) for m in range(2)]
        hT = [ws((2 + m) * W, W) for m in range(2)]
        ksq = [ws((4 + m) * W, W) for m in range(2)]

        wmods = ws(8 * W, 6 * D)
        cbc = ws(10 * W, B * P).rearrange("p (b w) -> p b w", b=B)

        cur = [0]

        def take(n):
            cur[0] += n
            return ws(cur[0] - n, n)

        Qx = take(HG * W)
        kTs, qTs, kd = ([take(W), take(W)] for _ in range(3))
        vx = [take(B * W), take(B * W)]
        vp = take(W)
        R, EM, PR = ([take(W), take(W)] for _ in range(3))
        Um = take(W)
        Sb = [take(W), take(W)]
        stmp = take(B * C)
        om, osum, ot = (take(W) for _ in range(3))
        o1, o2, onT, xn2, h2 = (take(W) for _ in range(5))
        o3, on, h2t, h2T = o2, o2, xn2, onT
        za = o1
        lg = ws(WORK - U * E, U * E)
        stb = [take(B * 6) for _ in range(2)]
        lnb = [take(8 * B) for _ in range(2)]
        assert cur[0] <= WORK - U * E, cur[0]

        UE = U * E
        base = 0

        def at(n):
            nonlocal base
            base += n
            return ws(base - n, n)

        lgx, wt, key, oh1, oh2, wt2, M, rank, pre, pos, t1r, t2r, ones_r = (at(UE) for _ in range(13))
        mx, zs, m1, m2, k1, tw1, tw2, tws, p1, p2 = (at(U) for _ in range(10))
        tot8, nbk, endb, startb, endv = (at(E) for _ in range(5))
        cmp32 = at(E * 32)
        posf = at(2 * U)
        posi, blki, sli = (at(2 * U) for _ in range(3))
        blkf, slf = at(2 * U), at(2 * U)
        ebc = at(NB * E)
        ebf = at(NB)
        ebi = at(NB)
        inv = at(NB)
        invz = at(NB)
        dst_i = at(NB)
        src_i = at(NB)
        oneS = [at(2 * P).bitcast(BF16) for _ in range(2)]
        hotB = [at(2 * NB).bitcast(BF16) for _ in range(2)]
        oneB = [at(4 * NB).bitcast(BF16) for _ in range(2)]
        xg, ye = ([at(P) for _ in range(4)] for _ in range(2))
        xTe = [at(P), at(P)]
        h1, ge = ([at(F), at(F)] for _ in range(2))
        gz_flat = gz[:, :, :, :].rearrange("p n b w -> p (n b w)")
        w1e = [gz_flat[:, k * EW:(k + 1) * EW] for k in range(4)]
        slot_gap = [gz_flat[:, 4 * EW + k * 4 * P:4 * EW + (k + 1) * 4 * P] for k in range(2)]
        gap2 = h1
        ysum = h1 + ge
        idg = [at(1) for _ in range(4)]
        idy = [at(1) for _ in range(4)]
        wtab = at(E * EW)
        stb += [at(B * 6) for _ in range(4)]
        lnb += [at(8 * B) for _ in range(4)]
        GB = [at(W) for _ in range(2)]
        assert base <= WORK - U * E, base
        w2s = kv[:, NT // 2:NT].rearrange("p n b w -> p (n b w)")
        Y1 = kT[:, :, :].rearrange("p n w -> p (n w)")
        Y2 = qT[:, :, :].rearrange("p n w -> p (n w)")

        def temp(j):
            return (xn2, onT, h2)[j].rearrange("p (b w) -> p b w", b=B)

        CA = {k: ct[:, a:a + n] for k, (a, n) in CONST_AT.items()}
        ident = CA["ident"]

        ps4x = psum("ps4x", [P, 4, 512])
        ps = [psum(f"ps{i}", [P, 512]) for i in range(4)] + [ps4x[:, i] for i in range(4)]

        names = """x_lo x_hi w_in w1_in cond_in mod_done mod_evac modt_done modt_evac csil_ready cbc_ready wgate_done wgate_evac
            eps_ready st_ready stat_sums stat_squares var_ready std_ready rstd_ready xn_ready xT_done hT_ready q_done q_evac
            k_done k_evac tok_done kv_evac gz_evac ksq_ready kss_ready gate_ready kss_floored lnk_ready rk_ready abs_z_ready
            exp_z_ready log_z_ready f_ready g_done f_done eg_ready ef_ready tc_done tc_evac te_done td_ready sign_ready
            state_zeroed U_done PV_done D_done A_done inter_done T1_done Wo_done T2_done router_done Um_ready S_mul S_step
            P_ready o1_ready o2_ready on_ready x2_ready xn2_ready logits_ready stage_ready bnA sumA sqA varA rstdA bnB sumB sqB
            varB rstdB own_ready head_sums_ready sums_turned kd_ready vx_ready E_ready Qx_ready onT_ready h2T_ready R_ready
            far_ready vp_ready o3_ready h2a_ready h2_ready h2_stored size_ready mod_ready w2_in y_stored0 y_stored1 y_stored2
            y_stored3 y_in0 y_in1 y_in2 y_in3 gam_in x3_ready out_stored route_step slots_ready logits_shifted exp_ready
            M_ready rank_done gap_ready gap2_ready oneS_ready oneB_ready block_hot inv_done inv_evac eb_ready idg_ready gath0
            gath1 gath2 gath3 w1e_ready Tx_done xT_ready mm1_done h1_ready gelu_ready mm2_done y_ready gb_ready share_ready
            sum_ready factors_ready bnC sumC sqC varC stdC rstdC scaledC beta_added gamma_done wog_ready""".split()
        s = {n: sem(n) for n in names}

        def S(n):
            return s[n]

        block = ctx.enter_context(nc.Block())

        def cols(t, start, n):
            return t[:, start:start + n] if isinstance(start, int) else t[:, bass.ds(start, n)]

        def kv_step(n, lo):
            if isinstance(n, int):
                return kv[:, n, :, lo:lo + P]
            return kv[:, bass.ds(n, 1), :, lo:lo + P].rearrange("p a b w -> p (a b) w")

        def gate_step(n):
            if isinstance(n, int):
                return gz[:, n, :, 0:P]
            return gz[:, bass.ds(n, 1), :, 0:P].rearrange("p a b w -> p (a b) w")

        scaled = {"A": "on_ready", "B": "xn2_ready", "C": "factors_ready"}
        lag = {"A": 0, "B": 0, "C": 3}

        rowbank = ps4x

        x_v = x.rearrange("b (n p) d -> n p b d", p=P)

        def step_view(t, n):
            return t[:, bass.ds(n, 1)].rearrange("p a w -> p (a w)") if not isinstance(n, int) else t[:, n]

        @block.sync
        def _(sp):
            for n in range(NT):
                sp.dma_start(xs[:, n].rearrange("p (b d) -> p b d", b=B), x_v[n]).then_inc(S("x_lo" if n < NT // 2 else "x_hi"), 16)

            h2_v = h2_rows.rearrange("(b n p) d -> n p b d", b=B, p=P)

            def store_h2(q):
                sp.wait_ge(S("h2_ready"), q + 1)
                dst = h2_v[q] if isinstance(q, int) else h2_v[bass.ds(q, 1)].rearrange("a p b d -> (a p) b d")
                sp.dma_start(dst, h2.rearrange("p (b d) -> p b d", b=B)).then_inc(S("h2_stored"), 16)

            with sp.Fori(0, NT) as q:
                store_h2(q)

            sp.wait_ge(S("stage_ready"), NT)
            sp.wait_ge(S("vx_ready"), U)
            sp.dma_start(gam[:, 0], gamma.partition_broadcast(P)).then_inc(S("gam_in"), 16)
            sp.dma_start(gam[:, 1], beta.partition_broadcast(P)).then_inc(S("gam_in"), 16)
            sp.dma_start(w2s.rearrange("p (e c d) -> p e c d", e=E, c=FC), w2.rearrange("e (c p) d -> p e c d", p=P)).then_inc(S("w2_in"), 16)
            sp.wait_ge(S("logits_ready"), NT)
            sp.wait_ge(S("h2_stored"), 16 * NT)
            table = wtab.rearrange("p (e w) -> p e w", e=E)
            sp.dma_start(table[:, :, 0:F], w1.rearrange("e d f -> d e f")).then_inc(S("w1_in"), 16)
            sp.dma_start(table[:, :, F:F + FC], b1_t).then_inc(S("w1_in"), 16)
            sp.dma_start(table[:, :, F + FC:EW], b2.partition_broadcast(P)).then_inc(S("w1_in"), 16)

            for m in range(4):
                sp.wait_ge(S(f"y_stored{m}"), 16 * (NB // 4))
            y_v = y_rows.rearrange("(k b n p) d -> k p n b d", k=2, b=B, p=P)
            for n in range(NT):
                m = n % 4
                wait(sp, S(f"y_in{m}"), 32 * (n // 4))
                for k, dst in enumerate((Y1, Y2)):
                    sp.dma_start(dst[:, n * W:(n + 1) * W].rearrange("p (b d) -> p b d", b=B), y_v[k, :, n]).then_inc(S(f"y_in{m}"), 16)
            out_v = out.rearrange("b (n p) d -> n p b d", p=P)
            with sp.Fori(0, NT) as n:
                sp.wait_ge(S("x3_ready"), n + 1)
                sp.dma_start(out_v[bass.ds(n, 1)].rearrange("a p b d -> (a p) b d"), step_view(xs, n).rearrange("p (b d) -> p b d", b=B)).then_inc(S("out_stored"), 16)
            sp.wait_ge(S("out_stored"), 16 * NT)

        W_LOADS = 11

        @block.scalar
        def _(act):
            act.dma_start(cs[:, :], c_t).then_inc(S("cond_in"), 16)
            act.dma_start(wmods[:, :], wmod).then_inc(S("cond_in"), 16)
            for dst, src in ((ct[:, :], consts), (wqs[:, :], wq_t), (wks[:, :], wk_t), (wtok[:, 0:2 * P], wkv_t),
                             (wtok[:, 3 * P:TOK], wf_t), (wg1s[:, :], wg1), (wg2s[:, :], wg2_t), (wos[:, :], wo_t),
                             (lnws[:, :], lnw), (wgs[:, :], wg), (bgs[:, :], bg.partition_broadcast(P))):
                act.dma_start(dst, src).then_inc(S("w_in"), 16)
            act.wait_ge(S("cond_in"), 32)
            nc.scalar.activation(csil[:, :], cs[:, :], ACT.Silu).then_inc(S("csil_ready"), 1)
            act.wait_ge(S("eps_ready"), 1)
            act.wait_ge(S("var_ready"), 1)
            nc.scalar.activation(ln[:, 5, 0:U // 2], ln[:, 4, 0:U // 2], ACT.Sqrt, bias=epst[:, 0:1], scale=1.0 / P).then_inc(S("std_ready"), 1)
            act.wait_ge(S("mod_done"), 1)
            for b in range(B):
                last = nc.scalar.activation(mod[:, :, b], ps[4 + b][:, :].rearrange("p (j d) -> p j d", j=4), ACT.Copy)
            last.then_inc(S("mod_evac"), 1)

            def a_step(n):
                act.wait_ge(S("q_done"), n + 1)
                nc.scalar.activation(step_view(qT, n), ps[2][:, :], ACT.Silu).then_inc(S("q_evac"), 1)
                act.wait_ge(S("k_done"), n + 1)
                nc.scalar.activation(step_view(kT, n), ps[3][:, :], ACT.Silu).then_inc(S("k_evac"), 1)
                for b in range(B):
                    act.wait_ge(S("tok_done"), n * B + b + 1)
                    dst = kv[:, bass.ds(n, 1), b].rearrange("p a w -> p (a w)") if not isinstance(n, int) else kv[:, n, b]
                    nc.scalar.activation(dst, ps[4 + b][:, 0:2 * P], ACT.Silu).then_inc(S("kv_evac"), 1)
            for n in range(2):
                a_step(n)
            with act.Fori(1, NT // 2) as i:
                for m in range(2):
                    a_step(i * 2 + m)

            act.wait_ge(S("abs_z_ready"), 1)
            nc.scalar.activation(za, za, ACT.Exp, scale=-1.0).then_inc(S("exp_z_ready"), 1)
            act.wait_ge(S("exp_z_ready"), 1)
            nc.scalar.activation(za, za, ACT.Ln, bias=1.0).then_inc(S("log_z_ready"), 1)
            act.wait_ge(S("kss_floored"), 1)
            nc.scalar.activation(rk[:, :], rk[:, :], ACT.Ln).then_inc(S("lnk_ready"), 1)
            act.wait_ge(S("lnk_ready"), 1)
            nc.scalar.activation(rk[:, :], rk[:, :], ACT.Exp, scale=-0.5).then_inc(S("rk_ready"), 1)
            act.wait_ge(S("g_done"), 1)
            nc.scalar.activation(eg[:, :], ps[0][:, :], ACT.Exp).then_inc(S("eg_ready"), 1)
            act.wait_ge(S("f_done"), 1)
            for b in range(B):
                last = nc.scalar.activation(ef[:, :].rearrange("p (n g b s) -> p b n g s", n=NT, g=G, b=B)[:, b],
                                            ps[1][:, :].rearrange("p (n b g s) -> p b n g s", n=NT, g=G, b=B)[:, b], ACT.Exp)
            last.then_inc(S("ef_ready"), 1)
            def decay(t, b):
                act.wait_ge(S("D_done"), t + 1)
                wait(act, S("P_ready"), t - 1)
                nc.scalar.activation(EM[b % 2], ps[b % 2][:, :], ACT.Exp).then_inc(S("E_ready"), 1)

            def spread_q(n):
                wait(act, S("A_done"), n * B)
                for h in range(HG):
                    last = nc.scalar.activation(Qx[:, h * W:(h + 1) * W], step_view(qT, n), ACT.Copy, scale=CA["head_of"][:, h:h + 1])
                last.then_inc(S("Qx_ready"), 1)

            def evacuate_on(q):
                act.wait_ge(S("T1_done"), q + 1)
                wait(act, S("router_done"), q - 1)
                nc.scalar.activation(onT, ps[2][:, :], ACT.Copy).then_inc(S("onT_ready"), 1)

            def evacuate_h2(q):
                act.wait_ge(S("T2_done"), q + 1)
                act.wait_ge(S("Wo_done"), min(q + 2, NT) if isinstance(q, int) else q + 2)
                if isinstance(q, int) and q > NT - 3:
                    act.wait_ge(S("router_done"), q)
                nc.scalar.activation(h2T, ps[2][:, :], ACT.Copy).then_inc(S("h2T_ready"), 1)

            def spread_values(r, m, cs):
                act.wait_ge(S("vp_ready"), r + 1)
                wait(act, S("PV_done"), (r - 1) * B)
                for c in cs:
                    nc.scalar.activation(vx[m].rearrange("p (bg c w) -> p bg c w", c=NC, w=C)[:, :, c], vp.rearrange("p (bg w) -> p bg w", w=C),
                                         ACT.Copy, scale=CA["chunk_of"][:, c:c + 1]).then_inc(S("vx_ready"), 1)

            def own_values(t):
                act.wait_ge(S("PV_done"), t + 1)
                wait(act, S("head_sums_ready"), t)
                src, dst = (v.rearrange("p (g s i) -> p g s i", g=G, s=HG) for v in (ps[3][:, :], om))
                for h in range(HG):
                    last = nc.scalar.activation(dst[:, :, h], src[:, :, h], ACT.Copy, scale=CA["head_of"][:, h:h + 1])
                last.then_inc(S("own_ready"), 1)

            def act_step(n, m, A=True, Ct=True, more=True):
                t = n * B
                decay(t + 1, 1)
                if A: own_values(t - 1)
                if Ct: evacuate_h2(n - 3)
                if more: spread_values(n + 1, 1 - m, range(0, 2))
                decay(t + 2, 2)
                if more: spread_values(n + 1, 1 - m, range(2, NC))
                own_values(t)
                decay(t + 3, 3)
                own_values(t + 1)
                if more: decay(t + 4, 0)
                own_values(t + 2)
                if A: evacuate_on(n - 1)
                if more: spread_q(n + 1)

            act.wait_ge(S("w_in"), 16 * W_LOADS)
            act.wait_ge(S("q_evac"), NT)
            spread_q(0)
            act.wait_ge(S("te_done"), 1)
            nc.scalar.activation(td[:, :], ps[3][:, 0:U * NC], ACT.Exp).then_inc(S("td_ready"), 1)
            spread_values(0, 0, range(NC))
            decay(0, 0)
            act_step(0, 0, A=False, Ct=False)
            act.wait_ge(S("gz_evac"), U)
            for j in range(4):
                v = gz[:, 2 * j:2 * j + 2, :, 0:P].rearrange("p a b w -> p (a b) w")
                last = nc.scalar.activation(v, v, ACT.Sigmoid)
            last.then_inc(S("gate_ready"), 1)
            act_step(1, 1, Ct=False)
            act_step(2, 0, Ct=False)
            with act.Fori(1, NT // 2 - 1) as i:
                for m in range(2):
                    act_step(i * 2 + 1 + m, 1 - m)
            act_step(NT - 1, 1, more=False)
            own_values(U - 1)
            evacuate_h2(NT - 3)
            evacuate_on(NT - 1)
            evacuate_h2(NT - 2)
            evacuate_h2(NT - 1)

            act.wait_ge(S("logits_shifted"), 1)
            nc.scalar.activation(wt, lgx, ACT.Exp).then_inc(S("exp_ready"), 1)

            def square_gaps(i, m):
                act.wait_ge(S("gap_ready"), i + 1)
                wait(act, S("oneS_ready"), i - 1)
                nc.scalar.activation(gap2[m], slot_gap[m], ACT.Square).then_inc(S("gap2_ready"), 1)

            def slot_hots(i, m):
                act.wait_ge(S("gap2_ready"), i + 1)
                wait(act, S("inv_done"), i - 1)
                nc.scalar.activation(oneS[m], gap2[m], ACT.Relu, bias=1.0, scale=-1.0).then_inc(S("oneS_ready"), 1)

            square_gaps(0, 0)
            square_gaps(1, 1)
            slot_hots(0, 0)
            with act.Fori(1, U // 4) as j:
                for m in range(2):
                    square_gaps(j * 2 + m, m)
                    slot_hots(j * 2 + m - 1, 1 - m)
            slot_hots(U // 2 - 1, 1)

            act.wait_ge(S("eb_ready"), 1)
            act.wait_ge(S("w1_in"), 16 * 3)

            def expert(i):
                return act.value_load(ebi[0:1, i:i + 1].bitcast(I32) if isinstance(i, int) else ebi[0:1, bass.ds(i, 1)].bitcast(I32), min_val=0, max_val=E - 1)

            def take_expert(i, m):
                e = expert(i)
                wait(act, S("y_ready"), i - 3)
                nc.scalar.activation(w1e[m], wtab[:, bass.ds(e * EW, EW)], ACT.Copy).then_inc(S("w1e_ready"), 1)

            def gelu(i, m):
                act.wait_ge(S("h1_ready"), i + 1)
                wait(act, S("mm2_done"), i - 1)
                nc.scalar.activation(ge[m], h1[m], ACT.Gelu).then_inc(S("gelu_ready"), 1)

            take_expert(0, 0)
            take_expert(1, 1)
            gelu(0, 0)
            for i in range(2, 4):
                take_expert(i, i)
                gelu(i - 1, (i - 1) % 2)
            with act.Fori(1, NB // 4) as j:
                for m in range(4):
                    take_expert(j * 4 + m, m)
                    gelu(j * 4 + m - 1, (m - 1) % 2)
            gelu(NB - 1, 1)

            def share(n, j, m):
                act.wait_ge(S(f"y_in{m}"), 32 * (j + 1))
                wait(act, S("x3_ready"), n - 3)
                for b in range(B):
                    last = nc.scalar.activation(ysum[m][:, b * P:(b + 1) * P], cols(Y1, (n * B + b) * P, P), ACT.Copy, scale=cols(tw1, n * B + b, 1))
                last.then_inc(S("share_ready"), 1)

            def deviation(n, m):
                act.wait_ge(S("varC"), n + 1)
                ws4 = lnb[2 + m]
                nc.scalar.activation(ws4[:, 5 * B:6 * B], ws4[:, 4 * B:5 * B], ACT.Sqrt).then_inc(S("stdC"), 1)

            def scale_sums(n, m):
                act.wait_ge(S("factors_ready"), n + 1)
                ws4 = lnb[2 + m]
                for b in range(B):
                    last = nc.scalar.activation(ysum[m][:, b * P:(b + 1) * P], ysum[m][:, b * P:(b + 1) * P], ACT.Identity,
                                                scale=ws4[:, 6 * B + b:6 * B + b + 1], bias=ws4[:, 3 * B + b:3 * B + b + 1])
                last.then_inc(S("scaledC"), 1)

            for n in range(4):
                share(n, 0, n)
                if n >= 1: deviation(n - 1, n - 1)
                if n >= 2: scale_sums(n - 2, n - 2)
            with act.Fori(1, NT // 4) as j:
                for m in range(4):
                    share(j * 4 + m, j, m)
                    deviation(j * 4 + m - 1, (m - 1) % 4)
                    scale_sums(j * 4 + m - 2, (m - 2) % 4)
            deviation(NT - 1, 3)
            scale_sums(NT - 2, 2)
            scale_sums(NT - 1, 3)

        @block.tensor
        def _(pe):
            pe.wait_ge(S("cond_in"), 32)
            pe.wait_ge(S("csil_ready"), 1)
            for i in range(2):
                last = nc.tensor.matmul(ps[0][:, 4 * i:4 * i + 4], wmods[:, i * D:(i + 1) * D], csil[:, :], start=True, stop=True)
            last.then_inc(S("modt_done"), 1)
            pe.wait_ge(S("w_in"), 16 * W_LOADS)
            nc.tensor.matmul(ps[1][:, 0:P], wg1s[:, :], wg2s[:, :], start=True, stop=True).then_inc(S("wgate_done"), 1)
            pe.wait_ge(S("cbc_ready"), 1)
            for b in range(B):
                last = nc.tensor.matmul(ps[4 + b][:, :], cbc[:, b], wmods[:, 2 * D:6 * D], start=True, stop=True)
            last.then_inc(S("mod_done"), 1)

            def transposes(n, m):
                wait(pe, S("xn_ready"), n * B + B)
                wait(pe, S("hT_ready"), (n - 1) * B)
                for b in range(B):
                    last = nc.tensor.transpose(ps[m][:, b * P:(b + 1) * P], xn[m][:, b * P:(b + 1) * P], ident)
                last.then_inc(S("xT_done"), 1)

            def projections(n, m):
                wait(pe, S("hT_ready"), (n + 1) * B)
                wait(pe, S("q_evac"), n)
                nc.tensor.matmul(ps[2][:, :], wqs[:, :], hT[m], start=True, stop=True).then_inc(S("q_done"), 1)
                wait(pe, S("k_evac"), n)
                nc.tensor.matmul(ps[3][:, :], wks[:, :], hT[m], start=True, stop=True).then_inc(S("k_done"), 1)
                for b in range(B):
                    wait(pe, S("kv_evac"), (n - 1) * B + b + 1)
                    wait(pe, S("gz_evac"), (n - 1) * B + b + 1)
                    nc.tensor.matmul(ps[4 + b][:, 0:TOK], hT[m][:, b * P:(b + 1) * P], wtok[:, :], start=True, stop=True).then_inc(S("tok_done"), 1)

            pe.wait_ge(S("modt_evac"), 1)
            pe.wait_ge(S("wgate_evac"), 1)
            transposes(0, 0)
            transposes(1, 1)
            pe.wait_ge(S("mod_evac"), 1)
            projections(0, 0)
            with pe.Fori(1, NT // 2) as i:
                for m in range(2):
                    n = i * 2 + m
                    transposes(n, m)
                    projections(n - 1, 1 - m)
            projections(NT - 1, 1)

            pe.wait_ge(S("f_ready"), 1)
            pe.wait_ge(S("gz_evac"), U)
            pe.wait_ge(S("k_evac"), NT)
            nc.tensor.matmul(ps[0][:, :], CA["later"], zf[:, :], start=True, stop=True).then_inc(S("g_done"), 1)
            nc.tensor.matmul(ps[1][:, :], CA["upto"], zf[:, :], start=True, stop=True).then_inc(S("f_done"), 1)
            for u in range(U):
                last = nc.tensor.matmul(ps[2][0:H, u * NC:(u + 1) * NC], zf[:, u * H:(u + 1) * H], CA["chunk_of"], start=True, stop=True)
            last.then_inc(S("tc_done"), 1)
            pe.wait_ge(S("tc_evac"), 1)
            nc.tensor.matmul(ps[3][:, 0:U * NC], CA["headsel"][0:H, :], tc[:, :], start=True, stop=True).then_inc(S("te_done"), 1)

            def open_group(dst):
                nc.tensor.matmul(dst, onebf[:, :], onebf[:, 0:1], start=True, stop=True)

            def state_updates(n, m):
                pe.wait_ge(S("kd_ready"), n + 1)
                pe.wait_ge(S("vx_ready"), (n + 1) * B)
                wait(pe, S("o1_ready"), n)
                for b in range(B):
                    for g in range(G):
                        at = b * P + g * C
                        last = nc.tensor.matmul(rowbank[g * C:(g + 1) * C, 0, b * P:(b + 1) * P], kd[m][:, at:at + C],
                                                vx[m][:, b * W + g * P:b * W + (g + 1) * P], start=True, stop=True)
                last.then_inc(S("U_done"), 1)

            def log_decay(t, b):
                pe.wait_ge(S("R_ready"), t + 1)
                wait(pe, S("E_ready"), t - 1)
                nc.tensor.matmul(ps[b % 2][:, :], CA["later"], R[b % 2], start=True, stop=False)
                nc.tensor.matmul(ps[b % 2][:, :], far[:, :], acausal[:, :], start=False, stop=True).then_inc(S("D_done"), 1)

            def scores(t, n, m, b):
                if b == 0:
                    pe.wait_ge(S("Um_ready"), n + 1)
                    pe.wait_ge(S("Qx_ready"), n + 1)
                    pe.wait_ge(S("stage_ready"), n + 1)
                else:
                    pe.wait_ge(S("P_ready"), t)
                open_group(rowbank[0:C, 0, 0:1])
                for c in range(NC):
                    at = b * P + c * C
                    for g in range(G):
                        rows = slice(g * C, (g + 1) * C)
                        q = Qx[rows, :].rearrange("p (s w) -> p s w", s=HG)[:, :, at:at + C]
                        last = nc.tensor.matmul(rowbank[c * C:(c + 1) * C, g, 0:P], kTs[m][rows, at:at + C], q, start=True, stop=True)
                last.then_inc(S("A_done"), 1)

            def weighted_values(t, n, m, b):
                pe.wait_ge(S("P_ready"), t + 1)
                wait(pe, S("own_ready"), t)
                for g in range(G):
                    last = nc.tensor.matmul(ps[3][:, g * P:(g + 1) * P], vx[m][:, b * W + g * P:b * W + (g + 1) * P], PR[b % 2][:, g * P:(g + 1) * P],
                                            start=True, stop=True)
                last.then_inc(S("PV_done"), 1)

            def state_terms(n, m):
                pe.wait_ge(S("P_ready"), (n + 1) * B)
                pe.wait_ge(S("S_step"), n * NC + NC - 1)
                open_group(rowbank[0:C, 0, 0:1])
                for b in range(B):
                    for c in range(NC):
                        for g in range(G):
                            rows = slice(g * C, (g + 1) * C)
                            last = nc.tensor.matmul(rowbank[c * C:(c + 1) * C, g, b * C:(b + 1) * C], qTs[m][rows, b * P + c * C:b * P + (c + 1) * C],
                                                    Sb[m][rows, (c * B + b) * C:(c * B + b + 1) * C], start=True, stop=True)
                last.then_inc(S("inter_done"), 1)

            def turn_on(q):
                pe.wait_ge(S("on_ready"), q + 1)
                wait(pe, S("logits_ready"), q - 1)
                for b in range(B):
                    last = nc.tensor.transpose(ps[2][:, b * P:(b + 1) * P], on[:, b * P:(b + 1) * P], ident)
                last.then_inc(S("T1_done"), 1)

            def output_projection(q):
                pe.wait_ge(S("onT_ready"), q + 1)
                for b in range(B):
                    last = nc.tensor.matmul(ps[2][:, b * P:(b + 1) * P], onT[:, b * P:(b + 1) * P], wog[:, b], start=True, stop=True)
                last.then_inc(S("Wo_done"), 1)

            def turn_h2(q):
                pe.wait_ge(S("h2_ready"), q + 1)
                pe.wait_ge(S("x2_ready"), min(q + 2, NT) if isinstance(q, int) else q + 2)
                if isinstance(q, int) and q > NT - 3:
                    pe.wait_ge(S("logits_ready"), q)
                for b in range(B):
                    last = nc.tensor.transpose(ps[2][:, b * P:(b + 1) * P], h2[:, b * P:(b + 1) * P], ident)
                last.then_inc(S("T2_done"), 1)

            def router(q):
                pe.wait_ge(S("h2T_ready"), q + 1)
                for b in range(B):
                    last = nc.tensor.matmul(ps[2][:, b * E:(b + 1) * E], h2T[:, b * P:(b + 1) * P], wgs[:, :], start=True, stop=True)
                last.then_inc(S("router_done"), 1)

            def pe_step(n, m, A=True, Ct=True, more=True):
                t = n * B
                state_updates(n, m)
                if isinstance(n, int) and n == 0:
                    for _ in range(8):
                        nc.tensor.matmul(ps[3][:, :], far[:, :], acausal[:, :], start=True, stop=True)
                if A: weighted_values(t - 1, n - 1, 1 - m, 3)
                scores(t, n, m, 0)
                if Ct: turn_h2(n - 3)
                log_decay(t + 2, 2)
                scores(t + 1, n, m, 1)
                if Ct: router(n - 3)
                weighted_values(t, n, m, 0)
                log_decay(t + 3, 3)
                scores(t + 2, n, m, 2)
                weighted_values(t + 1, n, m, 1)
                if more: log_decay(t + 4, 0)
                scores(t + 3, n, m, 3)
                weighted_values(t + 2, n, m, 2)
                if more: log_decay(t + 5, 1)
                if A: turn_on(n - 1)
                state_terms(n, m)
                if A: output_projection(n - 1)

            pe.wait_ge(S("eg_ready"), 1)
            pe.wait_ge(S("ef_ready"), 1)
            pe.wait_ge(S("far_ready"), 1)
            log_decay(0, 0)
            log_decay(1, 1)
            pe.wait_ge(S("td_ready"), 1)
            pe.wait_ge(S("wog_ready"), B)
            pe.wait_ge(S("eps_ready"), 3)
            pe_step(0, 0, A=False, Ct=False)
            pe_step(1, 1, Ct=False)
            pe_step(2, 0, Ct=False)
            with pe.Fori(1, NT // 2 - 1) as i:
                for m in range(2):
                    pe_step(i * 2 + 1 + m, 1 - m)
            pe_step(NT - 1, 1, more=False)
            weighted_values(U - 1, NT - 1, 1, 3)
            turn_h2(NT - 3)
            router(NT - 3)
            turn_on(NT - 1)
            output_projection(NT - 1)
            turn_h2(NT - 2)
            router(NT - 2)
            turn_h2(NT - 1)
            router(NT - 1)

            pe.wait_ge(S("M_ready"), 1)
            nc.tensor.matmul(ps[0][:, 0:UE], CA["before"], M, start=True, stop=True).then_inc(S("rank_done"), 1)
            nc.tensor.matmul(ps[1][:, 0:UE], CA["ones"], M, start=True, stop=True).then_inc(S("rank_done"), 1)
            pe.wait_ge(S("logits_ready"), NT)

            def place(i, m, first=False, last=False):
                pe.wait_ge(S("oneS_ready"), i + 1)
                pe.wait_ge(S("oneB_ready"), i + 1)
                for k in range(4):
                    mm = nc.tensor.matmul(ps[2][:, 0:2 * NB], oneS[m][:, k * P:(k + 1) * P], oneB[m][:, k * 2 * NB:(k + 1) * 2 * NB],
                                          start=first and k == 0, stop=last and k == 3)
                mm.then_inc(S("inv_done"), 1)
            place(0, 0, first=True)
            place(1, 1)
            with pe.Fori(1, U // 4 - 1) as j:
                for m in range(2):
                    place(j * 2 + m, m)
            place(U // 2 - 2, 0)
            place(U // 2 - 1, 1, last=True)

            pe.wait_ge(S("eb_ready"), 1)
            pe.wait_ge(S("w2_in"), 16)
            pe.wait_ge(S("inv_evac"), 2)

            def expert(i):
                return pe.value_load(ebi[0:1, i:i + 1].bitcast(I32) if isinstance(i, int) else ebi[0:1, bass.ds(i, 1)].bitcast(I32), min_val=0, max_val=E - 1)

            def turn_rows(i, j, m4):
                m = m4 % 2
                pe.wait_ge(S(f"gath{m4}"), 16 * (j + 1))
                wait(pe, S("xT_ready"), i - 1)
                nc.tensor.transpose(ps[m][:, 0:P], xg[m4], ident).then_inc(S("Tx_done"), 1)

            def hidden(i, m, m4):
                pe.wait_ge(S("w1e_ready"), i + 1)
                pe.wait_ge(S("xT_ready"), i + 1)
                wait(pe, S("h1_ready"), i - 1)
                for c in range(FC):
                    last = nc.tensor.matmul(ps[2 + m][:, c * P:(c + 1) * P], w1e[m4][:, c * P:(c + 1) * P], xTe[m], start=True, stop=True)
                last.then_inc(S("mm1_done"), 1)

            def result(i, m, e):
                pe.wait_ge(S("gelu_ready"), i + 1)
                wait(pe, S("y_ready"), i - 1)
                for c in range(FC):
                    last = nc.tensor.matmul(ps[4 + m][:, 0:P], ge[m][:, c * P:(c + 1) * P], w2s[:, bass.ds(e * F + c * P, P)], start=(c == 0), stop=(c == FC - 1))
                last.then_inc(S("mm2_done"), 1)

            def pe_block(i, j, m):
                e = expert(i - 2)
                turn_rows(i, j, m)
                hidden(i - 1, (m - 1) % 2, (m - 1) % 4)
                result(i - 2, m % 2, e)

            turn_rows(0, 0, 0)
            turn_rows(1, 0, 1)
            hidden(0, 0, 0)
            pe_block(2, 0, 2)
            pe_block(3, 0, 3)
            with pe.Fori(1, NB // 4) as j:
                for m in range(4):
                    pe_block(j * 4 + m, j, m)
            e = expert(NB - 2)
            hidden(NB - 1, 1, 3)
            result(NB - 2, 0, e)
            result(NB - 1, 1, expert(NB - 1))

        @block.vector
        def _(dve):
            nc.vector.memset(epst[:, 0:1], EPS_LN).then_inc(S("eps_ready"), 1)
            nc.vector.memset(epst[:, 1:2], -0.5).then_inc(S("eps_ready"), 1)
            nc.vector.memset(onebf[:, :], 1.0).then_inc(S("eps_ready"), 1)

            def conditioning():
                dve.wait_ge(S("csil_ready"), 1)
                nc.vector.tensor_copy(cbc[:, :, :], csil[:, :].unsqueeze(2).to_broadcast([P, B, P])).then_inc(S("cbc_ready"), 1)
                dve.wait_ge(S("modt_done"), 1)
                nc.vector.tensor_copy(modT[:, 0], ps[0][:, 0:B])
                nc.vector.tensor_scalar(modT[:, 1], ps[0][:, B:2 * B], 1.0, None, ALU.add).then_inc(S("modt_evac"), 1)
                dve.wait_ge(S("wgate_done"), 1)
                nc.vector.tensor_copy(wtok[:, 2 * P:3 * P], ps[1][:, 0:P]).then_inc(S("wgate_evac"), 1)

            def row_statistics(first, last):
                with dve.Fori(first, last) as n:
                    for b in range(B):
                        nc.vector.bn_stats(st[:, bass.ds(n * B + b, 1)].rearrange("p a w -> p (a w)"),
                                           xs[:, bass.ds(n, 1), b * P:(b + 1) * P].rearrange("p a w -> p (a w)")).then_inc(S("st_ready"), 1)

            def variances(half):
                u = slice(half * U // 2, (half + 1) * U // 2)
                dve.wait_ge(S("st_ready"), (half + 1) * U // 2)
                nc.vector.tensor_tensor(ln[:, 0, u], st[:, u, 1], st[:, u, 4], ALU.add).then_inc(S("stat_sums"), 1)
                nc.vector.tensor_tensor(ln[:, 1, u], st[:, u, 1], st[:, u, 4], ALU.subtract).then_inc(S("stat_sums"), 1)
                nc.vector.tensor_tensor(ln[:, 2, u], st[:, u, 2], st[:, u, 5], ALU.add).then_inc(S("stat_sums"), 1)
                dve.wait_ge(S("stat_sums"), 3 * half + 3)
                nc.vector.tensor_tensor(ln[:, 3, u], ln[:, 1, u], ln[:, 1, u], ALU.mult).then_inc(S("stat_squares"), 1)
                nc.vector.tensor_scalar(mean[:, u], ln[:, 0, u], 0.5, None, ALU.mult).then_inc(S("stat_squares"), 1)
                dve.wait_ge(S("stat_squares"), 2 * half + 2)
                return u, nc.vector.scalar_tensor_tensor(out=ln[:, 4, u], in0=ln[:, 3, u], scalar=P / 4.0, in1=ln[:, 2, u], op0=ALU.mult, op1=ALU.add)

            dve.wait_ge(S("x_lo"), 16 * NT // 2)
            row_statistics(0, NT // 4)
            conditioning()
            row_statistics(NT // 4, NT // 2)
            u, ins = variances(0)
            ins.then_inc(S("var_ready"), 1)
            dve.wait_ge(S("std_ready"), 1)
            nc.vector.reciprocal(rstd[:, u], ln[:, 5, u]).then_inc(S("rstd_ready"), 1)
            dve.wait_ge(S("rstd_ready"), 1)
            dve.wait_ge(S("modt_evac"), 1)

            def col(t, n, b):
                return t[:, n * B + b:n * B + b + 1] if isinstance(n, int) else t[:, bass.ds(n * B + b, 1)]

            def normalize(n, m):
                wait(dve, S("xT_done"), n - 1)
                src = step_view(xs, n)
                for b in range(B):
                    nc.vector.tensor_scalar(xn[m][:, b * P:(b + 1) * P], src[:, b * P:(b + 1) * P], col(mean, n, b), col(rstd, n, b),
                                            ALU.subtract, ALU.mult).then_inc(S("xn_ready"), 1)

            def modulate(n, m):
                dve.wait_ge(S("xT_done"), n + 1)
                wait(dve, S("tok_done"), (n - 1) * B)
                for b in range(B):
                    nc.vector.tensor_scalar(hT[m][:, b * P:(b + 1) * P], ps[m][:, b * P:(b + 1) * P], modT[:, 1, b:b + 1], modT[:, 0, b:b + 1],
                                            ALU.mult, ALU.add).then_inc(S("hT_ready"), 1)

            def keep_gate(n):
                for b in range(B):
                    dve.wait_ge(S("kv_evac"), n * B + b + 1)
                    dst = gz[:, bass.ds(n, 1), b].rearrange("p a w -> p (a w)") if not isinstance(n, int) else gz[:, n, b]
                    nc.vector.tensor_copy(dst, ps[4 + b][:, 2 * P:TOK]).then_inc(S("gz_evac"), 1)

            def key_sums(n, m):
                dve.wait_ge(S("ksq_ready"), n + 1)
                w = B * H
                dst = rk[:, n * w:(n + 1) * w] if isinstance(n, int) else rk[:, bass.ds(n * w, w)]
                nc.vector.tensor_reduce(dst, ksq[m].rearrange("p (g d) -> p g d", d=HD), AX, ALU.add).then_inc(S("kss_ready"), 1)

            normalize(0, 0)
            normalize(1, 1)
            modulate(0, 0)
            modulate(1, 1)
            normalize(2, 0)
            dve.wait_ge(S("x_hi"), 16 * NT // 2)
            row_statistics(NT // 2, 3 * NT // 4)
            keep_gate(0)
            row_statistics(3 * NT // 4, NT)
            u, ins = variances(1)
            ins.then_inc(S("stat_squares"), 1)
            dve.wait_ge(S("stat_squares"), 5)
            nc.vector.tensor_scalar(ln[:, 5, u], ln[:, 4, u], 1.0 / P, EPS_LN, ALU.mult, ALU.add).then_inc(S("var_ready"), 1)
            dve.wait_ge(S("var_ready"), 2)
            modulate(2, 0)
            normalize(3, 1)
            keep_gate(1)
            key_sums(0, 0)
            modulate(3, 1)
            dve.wait_ge(S("rstd_ready"), 2)
            normalize(4, 0)
            keep_gate(2)
            key_sums(1, 1)
            with dve.Fori(2, NT // 2 - 1) as i:
                for m in range(2):
                    n = i * 2 + m
                    modulate(n, m)
                    normalize(n + 1, 1 - m)
                    keep_gate(n - 1)
                    key_sums(n - 2, m)
            modulate(NT - 2, 0)
            normalize(NT - 1, 1)
            keep_gate(NT - 3)
            key_sums(NT - 4, 0)
            modulate(NT - 1, 1)
            keep_gate(NT - 2)
            key_sums(NT - 3, 1)
            keep_gate(NT - 1)
            key_sums(NT - 2, 0)
            key_sums(NT - 1, 1)

            dve.wait_ge(S("gz_evac"), U)
            z = gz[:, :, :, P:P + H].rearrange("p n b h -> p (n b) h")
            za3 = za.rearrange("p (u h) -> p u h", h=H)
            nc.vector.scalar_tensor_tensor(out=za3, in0=z, scalar=-1.0, in1=z, op0=ALU.mult, op1=ALU.max).then_inc(S("abs_z_ready"), 1)
            dve.wait_ge(S("kss_ready"), NT)
            nc.vector.tensor_scalar(rk[:, :], rk[:, :], EPS_NORM * EPS_NORM, None, ALU.max).then_inc(S("kss_floored"), 1)
            dve.wait_ge(S("w_in"), 16 * W_LOADS)
            nc.vector.tensor_scalar(far[:, :].rearrange("p (c w) -> p c w", c=NC), CA["ident"][0:C, 0:C].unsqueeze(1).to_broadcast([C, NC, C]),
                                    LOG_ZERO, None, ALU.mult)
            nc.vector.tensor_scalar(acausal[:, :].rearrange("p (h i) -> p h i", h=H), CA["causal"][0:C].unsqueeze(1).to_broadcast([C, H, C]),
                                    -1.0, 1.0, ALU.mult, ALU.add).then_inc(S("far_ready"), 1)
            dve.wait_ge(S("log_z_ready"), 1)
            nc.vector.scalar_tensor_tensor(out=zf[:, :].rearrange("p (u h) -> p u h", h=H), in0=z, scalar=0.0, in1=za3, op0=ALU.min,
                                           op1=ALU.subtract).then_inc(S("f_ready"), 1)
            nc.vector.tensor_scalar(mod[:, 2], mod[:, 2], 1.0, None, ALU.add).then_inc(S("mod_ready"), 1)
            for k, j in enumerate((0, 3)):
                nc.vector.scalar_tensor_tensor(out=temp(0), in0=mod[:, j], scalar=-1.0, in1=mod[:, j], op0=ALU.mult, op1=ALU.max).then_inc(S("sign_ready"), 1)
                nc.vector.tensor_scalar(temp(1), mod[:, j], 0.0, 2.0, ALU.is_ge, ALU.mult).then_inc(S("sign_ready"), 1)
                dve.wait_ge(S("sign_ready"), 2 * k + 2)
                nc.vector.tensor_scalar(temp(2), temp(0), 0.25, None, ALU.max).then_inc(S("size_ready"), 1)
                dve.wait_ge(S("size_ready"), k + 1)
                nc.vector.scalar_tensor_tensor(out=mod[:, j], in0=temp(1), scalar=-1.0, in1=temp(2), op0=ALU.add, op1=ALU.mult).then_inc(S("mod_ready"), 1)
                dve.wait_ge(S("mod_ready"), k + 2)
            for b in range(B):
                nc.vector.scalar_tensor_tensor(out=wog[:, b], in0=wos[:, :], scalar=lnws[:, 0:1], in1=mod[:, 0, b], op0=ALU.mult, op1=ALU.mult).then_inc(S("wog_ready"), 1)
            dve.wait_ge(S("tc_done"), 1)
            nc.vector.tensor_copy(tc[:, :], ps[2][0:H, 0:U * NC]).then_inc(S("tc_evac"), 1)

            def stage(n, m):
                wait(dve, S("A_done"), (n - 1) * B)
                nc.vector.tensor_copy(kTs[m], step_view(kT, n))
                wait(dve, S("inter_done"), n - 1)
                nc.vector.tensor_copy(qTs[m], step_view(qT, n)).then_inc(S("stage_ready"), 1)

            def take_updates(n):
                dve.wait_ge(S("U_done"), n + 1)
                wait(dve, S("S_step"), n * NC)
                nc.vector.tensor_tensor(Um.rearrange("p (c b w) -> p c b w", c=NC, b=B), rowbank[:, 0, :].rearrange("p (b c w) -> p c b w", b=B, c=NC),
                                        CA["blockmask"].unsqueeze(1).unsqueeze(1).to_broadcast([P, NC, B, C]), ALU.mult).then_inc(S("Um_ready"), 1)

            def state_chain(n, m, c):
                if c == 0:
                    dve.wait_ge(S("Um_ready"), n + 1)
                    wait(dve, S("inter_done"), n)
                wait(dve, S("S_step"), n * NC + c)
                before = Sb[m][:, c * B * C:(c + 1) * B * C].rearrange("p (b w) -> p b w", b=B)
                tdc = cols(td, n * B * NC, B * NC).rearrange("p (b c) -> p b c", c=NC)[:, :, c:c + 1].to_broadcast([P, B, C])
                nc.vector.tensor_tensor(stmp.rearrange("p (b w) -> p b w", b=B), before, tdc, ALU.mult).then_inc(S("S_mul"), 1)
                dve.wait_ge(S("S_mul"), n * NC + c + 1)
                dst = Sb[m][:, (c + 1) * B * C:(c + 2) * B * C] if c < NC - 1 else Sb[1 - m][:, 0:B * C]
                nc.vector.tensor_tensor(dst, stmp, Um[:, c * B * C:(c + 1) * B * C], ALU.add).then_inc(S("S_step"), 1)

            def weigh(t, b):
                dve.wait_ge(S("A_done"), t + 1)
                dve.wait_ge(S("E_ready"), t + 1)
                wait(dve, S("PV_done"), t - 1)
                nc.vector.tensor_tensor(PR[b % 2].rearrange("p (g w) -> p g w", g=G), EM[b % 2].rearrange("p (g w) -> p g w", g=G),
                                        rowbank[:, :, 0:P], ALU.mult).then_inc(S("P_ready"), 1)

            def take_state_terms(n):
                dve.wait_ge(S("inter_done"), n + 1)
                wait(dve, S("o2_ready"), n)
                nc.vector.tensor_tensor(o1.rearrange("p (g q d) -> p g q d", g=G, d=HD), rowbank[:, :, 0:B * C].rearrange("p g (q d) -> p g q d", d=HD),
                                        cols(ef, n * B * H, B * H).rearrange("p (g q) -> p g q", g=G).unsqueeze(3).to_broadcast([P, G, B * HG, HD]),
                                        ALU.mult).then_inc(S("o1_ready"), 1)

            def take_values(t, n, b):
                dve.wait_ge(S("own_ready"), t + 1)
                if b == 0: wait(dve, S("sums_turned"), n)
                nc.vector.tensor_reduce(osum[:, b * P:(b + 1) * P].rearrange("p (g i) -> p g i", g=G), om.rearrange("p (g s i) -> p g i s", g=G, s=HG),
                                        AX, ALU.add).then_inc(S("head_sums_ready"), 1)

            def add_values(q):
                dve.wait_ge(S("head_sums_ready"), (q + 1) * B)
                wait(dve, S("o2_ready"), q)
                nc.vector.transpose(ot, osum).then_inc(S("sums_turned"), 1)
                dve.wait_ge(S("sums_turned"), q + 1)
                dve.wait_ge(S("o1_ready"), q + 1)
                wait(dve, S("T1_done"), q)
                nc.vector.tensor_tensor(o2.rearrange("p (b g w) -> p b g w", b=B, g=G), o1.rearrange("p (g b w) -> p b g w", b=B, g=G),
                                        ot.rearrange("p (b g w) -> p b g w", b=B, g=G), ALU.add).then_inc(S("o2_ready"), 1)

            def before_statistics(q, tag, src_ready):
                dve.wait_ge(S(src_ready), q + 1)
                wait(dve, S("sum" + tag), 4 * q)

            def statistics(q, k, tag, src):
                for b in range(B):
                    last = nc.vector.bn_stats(stb[k][:, 6 * b:6 * b + 6], src[:, b * P:(b + 1) * P])
                last.then_inc(S("bn" + tag), 1)
                dve.wait_ge(S("bn" + tag), q + 1)
                wait(dve, S("sq" + tag), 2 * q)
                wait(dve, S("var" + tag), q)
                sv = stb[k].rearrange("p (b s) -> p b s", s=6)
                L = lambda j: lnb[k][:, j * B:(j + 1) * B]
                nc.vector.tensor_tensor(L(0), sv[:, :, 1], sv[:, :, 4], ALU.add).then_inc(S("sum" + tag), 1)
                nc.vector.tensor_tensor(L(1), sv[:, :, 1], sv[:, :, 4], ALU.subtract).then_inc(S("sum" + tag), 1)
                nc.vector.tensor_tensor(L(2), sv[:, :, 2], sv[:, :, 5], ALU.add).then_inc(S("sum" + tag), 1)
                dve.wait_ge(S("sum" + tag), 4 * q + 3)
                wait(dve, S(scaled[tag]), q - lag[tag])
                nc.vector.tensor_tensor(L(3), L(1), L(1), ALU.mult).then_inc(S("sq" + tag), 1)
                nc.vector.tensor_scalar(L(7), L(0), 0.5, None, ALU.mult).then_inc(S("sq" + tag), 1)
                dve.wait_ge(S("sq" + tag), 2 * q + 1)
                wait(dve, S("rstd" + tag), q - lag[tag])
                nc.vector.scalar_tensor_tensor(out=L(5), in0=L(3), scalar=P / 4.0, in1=L(2), op0=ALU.mult, op1=ALU.add).then_inc(S("sum" + tag), 1)
                dve.wait_ge(S("sum" + tag), 4 * q + 4)
                nc.vector.tensor_scalar(L(4), L(5), 1.0 / P, EPS_LN, ALU.mult, ALU.add).then_inc(S("var" + tag), 1)

            def scale_rows(q, k, tag, dst, src, done):
                dve.wait_ge(S("rstd" + tag), q + 1)
                dve.wait_ge(S("sq" + tag), 2 * q + 2)
                for b in range(B):
                    last = nc.vector.tensor_scalar(dst[:, b * P:(b + 1) * P], src[:, b * P:(b + 1) * P], lnb[k][:, 7 * B + b:7 * B + b + 1],
                                                   lnb[k][:, 6 * B + b:6 * B + b + 1], ALU.subtract, ALU.mult)
                last.then_inc(S(done), 1)

            def add_attention(q):
                dve.wait_ge(S("Wo_done"), q + 1)
                v = step_view(xs, q)
                nc.vector.tensor_tensor(v, v, ps[2][:, :], ALU.add).then_inc(S("x2_ready"), 1)

            def keep_logits(q):
                dve.wait_ge(S("router_done"), q + 1)
                nc.vector.tensor_tensor(cols(lg, q * B * E, B * E).rearrange("p (b e) -> p b e", b=B), ps[2][:, 0:B * E].rearrange("p (b e) -> p b e", b=B),
                                        bgs[:, :].unsqueeze(1).to_broadcast([P, B, E]), ALU.add).then_inc(S("logits_ready"), 1)

            def stats_A(q):
                before_statistics(q, "A", "o3_ready")
                statistics(q, 0, "A", o3)

            def stats_B(q):
                statistics(q, 1, "B", step_view(xs, q))

            def scale_A(q):
                scale_rows(q, 0, "A", on, o3, "on_ready")

            def scale_B(q):
                wait(dve, S("h2_ready"), q)
                scale_rows(q, 1, "B", xn2, step_view(xs, q), "xn2_ready")

            def dve_step(n, m, A=True, Bt=True, Ct=True, more=True):
                t = n * B
                take_updates(n)
                if Bt: add_attention(n - 2)
                if A: take_values(t - 1, n - 1, 3)
                if Bt: before_statistics(n - 2, "B", "x2_ready")
                weigh(t, 0)
                if A: add_values(n - 1)
                state_chain(n, m, 0)
                weigh(t + 1, 1)
                if Ct: keep_logits(n - 3)
                if Bt: stats_B(n - 2)
                take_values(t, n, 0)
                weigh(t + 2, 2)
                if A: stats_A(n - 1)
                state_chain(n, m, 1)
                take_values(t + 1, n, 1)
                if A: scale_A(n - 1)
                weigh(t + 3, 3)
                state_chain(n, m, 2)
                if Bt: scale_B(n - 2)
                take_values(t + 2, n, 2)
                if more: stage(n + 1, 1 - m)
                take_state_terms(n)
                state_chain(n, m, 3)

            nc.vector.memset(Sb[0][:, 0:B * C], 0.0).then_inc(S("state_zeroed"), 1)
            dve.wait_ge(S("state_zeroed"), 1)
            dve.wait_ge(S("k_evac"), NT)
            stage(0, 0)
            dve.wait_ge(S("td_ready"), 1)
            dve_step(0, 0, A=False, Bt=False, Ct=False)
            dve_step(1, 1, Bt=False, Ct=False)
            dve_step(2, 0, Ct=False)
            with dve.Fori(1, NT // 2 - 1) as i:
                for m in range(2):
                    dve_step(i * 2 + 1 + m, 1 - m)
            dve_step(NT - 1, 1, more=False)
            add_attention(NT - 2)
            before_statistics(NT - 2, "B", "x2_ready")
            take_values(U - 1, NT - 1, 3)
            add_values(NT - 1)
            stats_B(NT - 2)
            keep_logits(NT - 3)
            stats_A(NT - 1)
            scale_B(NT - 2)
            scale_A(NT - 1)
            add_attention(NT - 1)
            before_statistics(NT - 1, "B", "x2_ready")
            stats_B(NT - 1)
            keep_logits(NT - 2)
            scale_B(NT - 1)
            keep_logits(NT - 1)

            def e3(t):
                return t.rearrange("p (u e) -> p u e", e=E)

            def eb(t):
                return t.unsqueeze(2).to_broadcast([P, U, E])

            steps = [0]

            def then(ins):
                steps[0] += 1
                ins.then_inc(S("route_step"), 1)
                dve.wait_ge(S("route_step"), steps[0])

            V = nc.vector
            dve.wait_ge(S("logits_ready"), NT)
            dve.wait_ge(S("h2_ready"), NT)
            dve.wait_ge(S("router_done"), NT)
            dve.wait_ge(S("h2_stored"), 16 * NT)
            then(V.tensor_reduce(mx, e3(lg), AX, ALU.max))
            V.tensor_tensor(e3(lgx), e3(lg), eb(mx), ALU.subtract).then_inc(S("logits_shifted"), 1)
            dve.wait_ge(S("exp_ready"), 1)
            then(V.tensor_reduce(zs, e3(wt), AX, ALU.add))
            then(V.reciprocal(m1, zs))
            then(V.tensor_tensor(e3(wt), e3(wt), eb(m1), ALU.mult))
            rank8 = CA["rank8"].unsqueeze(1).to_broadcast([P, U, E])

            def choose(src, top, onehot):
                then(V.tensor_reduce(top, e3(src), AX, ALU.max))
                then(V.tensor_tensor(e3(key), e3(src), eb(top), ALU.is_equal))
                then(V.tensor_tensor(e3(key), e3(key), rank8, ALU.mult))
                then(V.tensor_reduce(k1, e3(key), AX, ALU.max))
                then(V.tensor_tensor(e3(onehot), rank8, eb(k1), ALU.is_equal))

            choose(wt, tw1, oh1)
            then(V.scalar_tensor_tensor(out=wt2, in0=oh1, scalar=-2.0, in1=wt, op0=ALU.mult, op1=ALU.add))
            choose(wt2, tw2, oh2)
            V.tensor_tensor(M, oh1, oh2, ALU.add).then_inc(S("M_ready"), 1)
            then(V.tensor_tensor(tws, tw1, tw2, ALU.add))
            then(V.tensor_scalar(tws, tws, EPS_GATE, None, ALU.add))
            then(V.reciprocal(zs, tws))
            then(V.tensor_tensor(tw1, tw1, zs, ALU.mult))
            then(V.tensor_tensor(tw2, tw2, zs, ALU.mult))
            then(V.memset(ones_r, 1.0))
            dve.wait_ge(S("rank_done"), 2)
            then(V.tensor_copy(t1r, ps[1][:, 0:UE]))
            for e in range(E):
                then(V.tensor_tensor_scan(e3(pre)[:, :, e], ones_r[:, 0:U], e3(t1r)[:, :, e], 0.0, ALU.mult, ALU.add))
            then(V.tensor_tensor(cmp32.rearrange("p (e k) -> p e k", e=E),
                                 e3(pre)[:, U - 1, :].unsqueeze(2).to_broadcast([P, E, 32]),
                                 CA["start_iota"].unsqueeze(1).to_broadcast([P, E, 32]), ALU.is_gt))
            then(V.tensor_reduce(nbk, cmp32.rearrange("p (e k) -> p e k", e=E), AX, ALU.add))
            then(V.tensor_tensor_scan(endb, ones_r[:, 0:E], nbk, 0.0, ALU.mult, ALU.add))
            then(V.tensor_tensor(startb, endb, nbk, ALU.subtract))
            then(V.tensor_scalar(startb, startb, float(P), None, ALU.mult))
            then(V.tensor_tensor(pre, pre, t1r, ALU.subtract))
            then(V.tensor_tensor(pos, pre, ps[0][:, 0:UE], ALU.add))
            then(V.tensor_tensor(e3(pos), e3(pos), startb.unsqueeze(1).to_broadcast([P, U, E]), ALU.add))
            then(V.tensor_tensor(t1r, pos, oh1, ALU.mult))
            then(V.tensor_tensor(t2r, pos, oh2, ALU.mult))
            then(V.tensor_reduce(posf[:, 0:U], e3(t1r), AX, ALU.add))
            then(V.tensor_reduce(posf[:, U:2 * U], e3(t2r), AX, ALU.add))
            i32 = lambda t: t.bitcast(I32)
            then(V.tensor_copy(i32(posi), posf))
            then(V.tensor_scalar(i32(blki), i32(posi), 7, None, ALU.logical_shift_right))
            then(V.tensor_scalar(i32(sli), i32(posi), P - 1, None, ALU.bitwise_and))
            then(V.tensor_copy(blkf, i32(blki)))
            V.tensor_copy(slf, i32(sli)).then_inc(S("slots_ready"), 1)
            ebc3 = ebc.rearrange("p (i e) -> p i e", e=E)
            then(V.tensor_tensor(ebc3, endb.unsqueeze(1).to_broadcast([P, NB, E]), CA["block_iota"].unsqueeze(2).to_broadcast([P, NB, E]), ALU.is_le))
            then(V.tensor_reduce(ebf, ebc3, AX, ALU.add))
            then(V.tensor_scalar(ebf, ebf, float(E - 1), None, ALU.min))
            V.tensor_copy(i32(ebi), ebf).then_inc(S("eb_ready"), 1)

            def one_hots(i, m):
                wait(dve, S("inv_done"), i - 1)
                hot = hotB[m].rearrange("p (k n) -> p k n", k=4)
                V.tensor_tensor(hot, CA["block_iota"].unsqueeze(1).to_broadcast([P, 4, NB]),
                                cols(blkf, 4 * i, 4).unsqueeze(2).to_broadcast([P, 4, NB]), ALU.is_equal).then_inc(S("block_hot"), 1)
                dve.wait_ge(S("block_hot"), i + 1)
                V.tensor_tensor(oneB[m].rearrange("p (k g n) -> p k g n", k=4, g=2), hot.unsqueeze(2).to_broadcast([P, 4, 2, NB]),
                                cols(CA["dest"], 8 * i, 8).rearrange("p (k g) -> p k g", g=2).unsqueeze(3).to_broadcast([P, 4, 2, NB]),
                                ALU.mult).then_inc(S("oneB_ready"), 1)

            one_hots(0, 0)
            one_hots(1, 1)
            with dve.Fori(1, U // 4) as j:
                for m in range(2):
                    one_hots(j * 2 + m, m)
            dve.wait_ge(S("inv_done"), U // 2)
            then(V.tensor_copy(inv, ps[2][:, NB:2 * NB]))
            then(V.scalar_tensor_tensor(out=inv, in0=ps[2][:, 0:NB], scalar=float(P), in1=inv, op0=ALU.mult, op1=ALU.add))
            then(V.tensor_scalar(invz, inv[:, 0:NB], 0.0, float(PAD), ALU.is_equal, ALU.mult))
            then(V.tensor_scalar(inv[:, 0:NB], inv[:, 0:NB], 1.0, None, ALU.subtract))
            then(V.tensor_tensor(inv[:, 0:NB], inv[:, 0:NB], invz, ALU.add))
            V.tensor_copy(i32(dst_i), inv[:, 0:NB]).then_inc(S("inv_evac"), 1)
            dve.wait_ge(S("inv_evac"), 1)
            V.tensor_scalar(i32(src_i), i32(dst_i), ROWS - 1, None, ALU.bitwise_and).then_inc(S("inv_evac"), 1)
            dve.wait_ge(S("inv_evac"), 2)

            def read_index(i, j, m):
                wait(dve, S(f"gath{m}"), 16 * j)
                V.tensor_copy(i32(idg[m]), cols(i32(src_i), i, 1)).then_inc(S("idg_ready"), 1)

            def write_index(i, j, m4):
                wait(dve, S(f"y_stored{m4}"), 16 * j)
                V.tensor_copy(i32(idy[m4]), cols(i32(dst_i), i, 1))

            def take_rows(i, m):
                dve.wait_ge(S("Tx_done"), i + 1)
                wait(dve, S("mm1_done"), i - 1)
                V.tensor_copy(xTe[m], ps[m][:, 0:P]).then_inc(S("xT_ready"), 1)

            def bias1(i, m, m4):
                dve.wait_ge(S("mm1_done"), i + 1)
                wait(dve, S("gelu_ready"), i - 1)
                V.tensor_tensor(h1[m].rearrange("p (c t) -> p c t", c=FC), ps[2 + m][:, :].rearrange("p (c t) -> p c t", c=FC),
                                w1e[m4][:, F:F + FC].unsqueeze(2).to_broadcast([P, FC, P]), ALU.add).then_inc(S("h1_ready"), 1)

            def bias2(i, m4):
                dve.wait_ge(S("mm2_done"), i + 1)
                V.tensor_tensor(ye[m4], ps[4 + m4 % 2][:, 0:P], w1e[m4][:, F + FC:EW], ALU.add).then_inc(S("y_ready"), 1)

            def dve_block(i, j, m, more=True):
                take_rows(i, m % 2)
                bias1(i - 1, (m - 1) % 2, (m - 1) % 4)
                if more: read_index(i + 3, j + (m + 3) // 4, (m + 3) % 4)
                write_index(i - 2, j - (m < 2), (m - 2) % 4)
                bias2(i - 2, (m - 2) % 4)

            for i in range(4):
                read_index(i, 0, i)
            take_rows(0, 0)
            take_rows(1, 1)
            bias1(0, 0, 0)
            read_index(4, 1, 0)
            for i in range(2, 4):
                dve_block(i, 0, i)
            with dve.Fori(1, NB // 4 - 1) as j:
                for m in range(4):
                    dve_block(j * 4 + m, j, m)
            for m in range(4):
                dve_block(NB - 4 + m, NB // 4 - 1, m, more=m == 0)
            bias1(NB - 1, 1, 3)
            for i in range(NB - 2, NB):
                write_index(i, NB // 4 - 1, i % 4)
                bias2(i, i % 4)

            def sum_rows(n, m):
                dve.wait_ge(S("share_ready"), n + 1)
                for b in range(B):
                    last = V.scalar_tensor_tensor(out=ysum[m][:, b * P:(b + 1) * P], in0=cols(Y2, (n * B + b) * P, P), scalar=cols(tw2, n * B + b, 1),
                                                  in1=ysum[m][:, b * P:(b + 1) * P], op0=ALU.mult, op1=ALU.add)
                last.then_inc(S("sum_ready"), 1)
                dve.wait_ge(S("sum_ready"), n + 1)
                wait(dve, S("scaledC"), n - 3)
                statistics(n, 2 + m, "C", ysum[m])

            def norm_factors(n, m):
                dve.wait_ge(S("stdC"), n + 1)
                ws4 = lnb[2 + m]
                V.reciprocal(ws4[:, 6 * B:7 * B], ws4[:, 5 * B:6 * B]).then_inc(S("rstdC"), 1)
                dve.wait_ge(S("rstdC"), n + 1)
                V.scalar_tensor_tensor(out=ws4[:, 3 * B:4 * B], in0=ws4[:, 7 * B:8 * B], scalar=-1.0, in1=ws4[:, 6 * B:7 * B],
                                       op0=ALU.mult, op1=ALU.mult).then_inc(S("factors_ready"), 1)

            sum_rows(0, 0)
            for n in range(1, 4):
                sum_rows(n, n)
                norm_factors(n - 1, n - 1)
            with dve.Fori(1, NT // 4) as j:
                for m in range(4):
                    sum_rows(j * 4 + m, m)
                    norm_factors(j * 4 + m - 1, (m - 1) % 4)
            norm_factors(NT - 1, 3)

        @block.gpsimd
        def _(pool):
            def squares(n, m):
                pool.wait_ge(S("kv_evac"), (n + 1) * B)
                wait(pool, S("kss_ready"), n - 1)
                src = kv[:, n, :, 0:P] if isinstance(n, int) else kv[:, bass.ds(n, 1), :, 0:P].rearrange("p a b w -> p (a b) w")
                nc.gpsimd.tensor_tensor(ksq[m].rearrange("p (b w) -> p b w", b=B), src, src, ALU.mult).then_inc(S("ksq_ready"), 1)
            squares(0, 0)
            pool.wait_ge(S("eps_ready"), 2)
            pool.wait_ge(S("var_ready"), 2)
            nc.gpsimd.tensor_tensor(rstd[:, U // 2:U], ln[:, 5, U // 2:U], epst[:, 1:2].to_broadcast([P, U // 2]), ALU.pow).then_inc(S("rstd_ready"), 1)
            squares(1, 1)
            with pool.Fori(1, NT // 2) as i:
                for m in range(2):
                    squares(i * 2 + m, m)

            def decay_rows(t, n, b):
                wait(pool, S("D_done"), t - 1)
                fcol = cols(zf, (n * B + b) * H, H).unsqueeze(2).to_broadcast([P, H, C])
                nc.gpsimd.tensor_tensor(R[b % 2].rearrange("p (h i) -> p h i", h=H), fcol,
                                        CA["causal"].unsqueeze(1).to_broadcast([P, H, C]), ALU.mult).then_inc(S("R_ready"), 1)

            def values(r, m):
                def by_head(t):
                    return cols(t, r * B * H, B * H).rearrange("p (b h) -> p b h", b=B).unsqueeze(3).to_broadcast([P, B, H, HD])
                wait(pool, S("U_done"), r - 1)
                nc.gpsimd.tensor_tensor(kd[m].rearrange("p (b h d) -> p b h d", b=B, h=H), kv_step(r, 0).rearrange("p b (h d) -> p b h d", h=H),
                                        by_head(eg), ALU.mult).then_inc(S("kd_ready"), 1)
                wait(pool, S("vx_ready"), r * B)
                nc.gpsimd.tensor_tensor(vp.rearrange("p (b h d) -> p b h d", b=B, h=H), kv_step(r, P).rearrange("p b (h d) -> p b h d", h=H),
                                        by_head(rk), ALU.mult).then_inc(S("vp_ready"), 1)

            def inverse_std(q, k, tag):
                pool.wait_ge(S("var" + tag), q + 1)
                wait(pool, S(scaled[tag]), q - lag[tag])
                nc.gpsimd.tensor_tensor(lnb[k][:, 6 * B:7 * B], lnb[k][:, 4 * B:5 * B], epst[:, 1:2].to_broadcast([P, B]), ALU.pow).then_inc(S("rstd" + tag), 1)

            def gate(q):
                pool.wait_ge(S("o2_ready"), q + 1)
                nc.gpsimd.tensor_tensor(o3.rearrange("p (b w) -> p b w", b=B), o2.rearrange("p (b w) -> p b w", b=B), gate_step(q),
                                        ALU.mult).then_inc(S("o3_ready"), 1)

            def modulate2(q):
                pool.wait_ge(S("xn2_ready"), q + 1)
                nc.gpsimd.tensor_tensor(h2t, xn2, mod[:, 2].rearrange("p b w -> p (b w)"), ALU.mult).then_inc(S("h2a_ready"), 1)
                pool.wait_ge(S("h2a_ready"), q + 1)
                wait(pool, S("T2_done"), q)
                wait(pool, S("h2_stored"), 16 * q)
                nc.gpsimd.tensor_tensor(h2, h2t, mod[:, 1].rearrange("p b w -> p (b w)"), ALU.add).then_inc(S("h2_ready"), 1)

            def pool_step(n, m, A=True, Bt=True, more=True):
                t = n * B
                decay_rows(t + 2, n, 2)
                if more: values(n + 1, 1 - m)
                decay_rows(t + 3, n, 3)
                if A: gate(n - 1)
                if more: decay_rows(t + 4, n + 1, 0)
                if Bt: inverse_std(n - 2, 1, "B")
                if A: inverse_std(n - 1, 0, "A")
                if more: decay_rows(t + 5, n + 1, 1)
                if Bt: modulate2(n - 2)

            pool.wait_ge(S("f_ready"), 1)
            decay_rows(0, 0, 0)
            decay_rows(1, 0, 1)
            pool.wait_ge(S("rk_ready"), 1)
            pool.wait_ge(S("eg_ready"), 1)
            values(0, 0)
            pool.wait_ge(S("mod_ready"), 2)
            pool.wait_ge(S("eps_ready"), 3)
            pool_step(0, 0, A=False, Bt=False)
            pool.wait_ge(S("gate_ready"), 1)
            pool_step(1, 1, Bt=False)
            pool_step(2, 0)
            with pool.Fori(1, NT // 2 - 1) as i:
                for m in range(2):
                    pool_step(i * 2 + 1 + m, 1 - m)
            pool_step(NT - 1, 1, more=False)
            gate(NT - 1)
            inverse_std(NT - 2, 1, "B")
            inverse_std(NT - 1, 0, "A")
            modulate2(NT - 2)
            inverse_std(NT - 1, 1, "B")
            modulate2(NT - 1)

            pool.wait_ge(S("gam_in"), 32)
            pool.wait_ge(S("logits_ready"), NT)
            pool.wait_ge(S("h2_stored"), 16 * NT)
            for j in range(2):
                nc.gpsimd.tensor_tensor(GB[j].rearrange("p (b w) -> p b w", b=B), mod[:, 3], gam[:, j].unsqueeze(1).to_broadcast([P, B, P]),
                                        ALU.mult).then_inc(S("gb_ready"), 1)
            pool.wait_ge(S("gb_ready"), 2)
            with pool.Fori(0, NT) as n:
                nc.gpsimd.tensor_tensor(step_view(xs, n), step_view(xs, n), GB[1], ALU.add).then_inc(S("beta_added"), 1)

            pool.wait_ge(S("slots_ready"), 1)

            def slot_gaps(i, m):
                wait(pool, S("gap2_ready"), i - 1)
                nc.gpsimd.tensor_tensor(slot_gap[m].rearrange("p (k s) -> p k s", k=4), CA["slot_iota"].unsqueeze(1).to_broadcast([P, 4, P]),
                                        cols(slf, 4 * i, 4).unsqueeze(2).to_broadcast([P, 4, P]), ALU.subtract).then_inc(S("gap_ready"), 1)

            slot_gaps(0, 0)
            slot_gaps(1, 1)
            with pool.Fori(1, U // 4) as j:
                for m in range(2):
                    slot_gaps(j * 2 + m, m)

            bound = pool.alloc_register("bound")
            pool.reg_mov(bound, 2 * ROWS - 1)

            def gather(i, m):
                pool.wait_ge(S("idg_ready"), i + 1)
                wait(pool, S("Tx_done"), i - 3)
                pool.reg_alu(bound, bound, 1, op=ALU.bitwise_or)
                nc.gpsimd.indirect_dma_start(xg[m], None, h2_rows, bass.IndirectOffsetOnAxis(ap=idg[m].bitcast(I32), axis=0),
                                             bounds_check=bound, oob_is_err=False).then_inc(S(f"gath{m}"), 16)

            def scatter(i, m):
                pool.wait_ge(S("y_ready"), i + 1)
                pool.reg_alu(bound, bound, 1, op=ALU.bitwise_or)
                nc.gpsimd.indirect_dma_start(y_rows, bass.IndirectOffsetOnAxis(ap=idy[m].bitcast(I32), axis=0), ye[m], None,
                                             bounds_check=bound, oob_is_err=False).then_inc(S(f"y_stored{m}"), 16)

            def pool_block(i, m, more=True):
                if more: gather(i + 3, (m + 3) % 4)
                scatter(i - 2, (m - 2) % 4)

            for i in range(5):
                gather(i, i % 4)
            for i in range(2, 4):
                pool_block(i, i)
            with pool.Fori(1, NB // 4 - 1) as j:
                for m in range(4):
                    pool_block(j * 4 + m, m)
            for m in range(4):
                pool_block(NB - 4 + m, m, more=m == 0)
            for i in range(NB - 2, NB):
                scatter(i, i % 4)

            def residual(n, m):
                pool.wait_ge(S("scaledC"), n + 1)
                nc.gpsimd.tensor_tensor(ysum[m], ysum[m], GB[0], ALU.mult).then_inc(S("gamma_done"), 1)
                pool.wait_ge(S("gamma_done"), n + 1)
                nc.gpsimd.tensor_tensor(step_view(xs, n), step_view(xs, n), ysum[m], ALU.add).then_inc(S("x3_ready"), 1)

            pool.wait_ge(S("beta_added"), NT)
            with pool.Fori(0, NT // 4) as j:
                for m in range(4):
                    residual(j * 4 + m, m)


def constants(np):
    p = np.arange(P)[:, None]
    q = np.arange(P)[None, :]
    t = {
        "ident": p == q,
        "later": (p // C == q // C) & (p > q),
        "upto": (p // C == q // C) & (p <= q),
        "before": p < q,
        "ones": np.ones((P, P)),
        "headsel": p == q // HD,
        "slot_iota": q + 0 * p,
        "block_iota": np.arange(NB)[None, :] + 0 * p,
        "causal": p % C <= np.arange(C)[None, :],
        "blockmask": (p % C) // HD == np.arange(C)[None, :] // HD,
        "start_iota": P * np.arange(32)[None, :] + 0 * p,
        "dest": np.array([[v for k in range(2) for u in range(U) for v in (k * U + (u % B) * NT + u // B, 0)]]) + (p + 1) * (np.arange(4 * U)[None, :] % 2),
        "chunk_of": p // C == np.arange(NC)[None, :],
        "head_of": (p % C) // HD == np.arange(HG)[None, :],
        "rank8": E - np.arange(E)[None, :] + 0 * p,
    }
    return np.concatenate([np.asarray(t[n], np.float32) for n, _ in CONST_WIDTHS], axis=1)


def kernel(**inputs):
    import numpy as np
    import concourse.bacc as bacc
    from concourse import mybir as mb
    from concourse.bass_utils import run_bass_kernel_spmd

    a = {k: np.asarray(v) for k, v in inputs.items()}
    arrays = {
        "x": a["L0_attn_x"], "wq_t": a["L0_attn_Wq"].T, "wk_t": a["L0_attn_Wk"].T,
        "wkv_t": np.concatenate([a["L0_attn_Wk"].T, a["L0_attn_Wv"].T], axis=1), "wf_t": a["L0_attn_Wf"].T,
        "wg1": a["L0_attn_Wg1"], "wg2_t": a["L0_attn_Wg2"].T, "lnw": a["L0_attn_ln_w"].reshape(D, 1),
        "wo_t": a["L0_attn_Wo"].T, "wg": a["L0_ffn_Wg"], "bg": a["L0_ffn_bg"], "w1": a["L0_ffn_W1"],
        "b1_t": a["L0_ffn_b1"].reshape(E, FC, P).transpose(2, 0, 1), "w2": a["L0_ffn_W2"], "b2": a["L0_ffn_b2"], "gamma": a["L0_ffn_gamma"],
        "beta": a["L0_ffn_beta"], "c_t": a["L0_c"].T, "wmod": a["L0_wmod"], "consts": constants(np),
    }
    arrays = {f"in_{k}": np.ascontiguousarray(v) for k, v in arrays.items()}
    nc = bacc.Bacc("TRN2", target_bir_lowering=False, num_devices=1)
    args = [nc.dram_tensor(k, v.shape, mb.dt.from_np(v.dtype), kind="ExternalInput").ap() for k, v in arrays.items()]
    args.append(nc.dram_tensor("out_x", (B, N, D), F32, kind="ExternalOutput").ap())
    build(nc, *args)
    r = run_bass_kernel_spmd(nc, [arrays], core_ids=[0])
    return r.results[0]["out_x"]
```
